# Optimizing a Trainium2 kernel written in Bass

```python
import numpy as np
import jax
import jax.numpy as jnp

def _softmax(x, axis=-1):
    return jax.nn.softmax(x, axis=axis)

def _gelu(x):
    return jax.nn.gelu(x, approximate=True)

def _silu(x):
    return jax.nn.silu(x)

def _sigmoid(x):
    return jax.nn.sigmoid(x)

def _layernorm(x, axis=-1, eps=1e-05):
    m = jnp.mean(x, axis=axis, keepdims=True)
    v = jnp.var(x, axis=axis, keepdims=True)
    return (x - m) / jnp.sqrt(v + eps)

def _scatter_add(tgt, idx, src, axis=0):
    return tgt.at[idx].add(src)

def _segment_sum(src, seg, n):
    return jax.ops.segment_sum(src, seg, n)
kernel_name = 'mk_early_fusion_d2_tok_img768_r4_0e1475'

def setup_inputs(seed: int=0):
    np.random.seed(seed)
    _w = jnp.asarray

    def _rec_inputs():
        import jax
        import jax.numpy as jnp
        _rk = jax.random.key(seed)
        x = -0.000348323 + 0.999952 * jax.random.normal(jax.random.fold_in(_rk, 1), (64, 3, 64, 64), jnp.float32)
        txt = 0.00108508 + 1.0006 * jax.random.normal(jax.random.fold_in(_rk, 2), (64, 77, 192), jnp.float32)
        return (x, txt)
    x, txt = _rec_inputs()

    def _L0_tok_setup():
        import jax, jax.numpy as jnp
        import numpy as np
        PATCH = 16
        DIM = 192
        LN_EPS = 1e-05

        def _spt_forward(x, ln_gamma, ln_beta, w, b):
            B, C, H, W = x.shape
            p = PATCH
            x_right = jnp.pad(x, ((0, 0), (0, 0), (0, 0), (1, 0)))[:, :, :, :-1]
            x_left = jnp.pad(x, ((0, 0), (0, 0), (0, 0), (0, 1)))[:, :, :, 1:]
            x_down = jnp.pad(x, ((0, 0), (0, 0), (1, 0), (0, 0)))[:, :, :-1, :]
            x_up = jnp.pad(x, ((0, 0), (0, 0), (0, 1), (0, 0)))[:, :, 1:, :]
            xc = jnp.concatenate((x, x_right, x_left, x_down, x_up), axis=1)
            C5 = 5 * C
            h, wgrid = (H // p, W // p)
            tokens = xc.reshape(B, C5, h, p, wgrid, p)
            tokens = tokens.transpose(0, 2, 4, 3, 5, 1)
            tokens = tokens.reshape(B, h * wgrid, p * p * C5)
            mean = jnp.mean(tokens, axis=-1, keepdims=True)
            var = jnp.var(tokens, axis=-1, keepdims=True)
            normed = (tokens - mean) * jax.lax.rsqrt(var + LN_EPS) * ln_gamma + ln_beta
            return jnp.einsum('bnd,de->bne', normed, w) + b
        key = jax.random.key(seed)
        k1, k2 = jax.random.split(key)
        B, C, H, W = (32, 3, 96, 96)
        patch_dim = PATCH * PATCH * 5 * C
        x = jax.random.normal(k1, (B, C, H, W), dtype=jnp.float32)
        ln_gamma = jnp.ones((patch_dim,), dtype=jnp.float32)
        ln_beta = jnp.zeros((patch_dim,), dtype=jnp.float32)
        w = jax.random.normal(k2, (patch_dim, DIM), dtype=jnp.float32) * patch_dim ** (-0.5)
        b = jnp.zeros((DIM,), dtype=jnp.float32)
        return {'x': x, 'ln_gamma': ln_gamma, 'ln_beta': ln_beta, 'w': w, 'b': b}
    _L0_tok_all = _L0_tok_setup()
    _L0_tok_in = {k: v for k, v in _L0_tok_all.items() if k in ('ln_gamma', 'ln_beta', 'w', 'b')}
    del _L0_tok_all

    def _L0_attn_setup():
        import jax, jax.numpy as jnp
        import numpy as np
        DIM = 192
        HEADS = 12
        HEAD_DIM = DIM // HEADS
        SCALE = HEAD_DIM ** (-0.5)
        H_CONST = 4
        key = jax.random.key(seed)
        ks = jax.random.split(key, 9)
        B, N = (4, 256)
        s = DIM ** (-0.5)
        return {'x': jax.random.normal(ks[0], (B, N, DIM), dtype=jnp.float32), 'qkv_w': jax.random.normal(ks[1], (3 * DIM, DIM), dtype=jnp.float32) * s, 'proj_l_w': jax.random.normal(ks[2], (HEADS, HEADS), dtype=jnp.float32) * HEADS ** (-0.5), 'proj_l_b': jax.random.normal(ks[3], (HEADS,), dtype=jnp.float32) * 0.02, 'proj_w_w': jax.random.normal(ks[4], (HEADS, HEADS), dtype=jnp.float32) * HEADS ** (-0.5), 'proj_w_b': jax.random.normal(ks[5], (HEADS,), dtype=jnp.float32) * 0.02, 'lamb': jax.random.normal(ks[6], (HEADS,), dtype=jnp.float32) * 0.1, 'proj_out_w': jax.random.normal(ks[7], (DIM, DIM), dtype=jnp.float32) * s, 'proj_out_b': jax.random.normal(ks[8], (DIM,), dtype=jnp.float32) * 0.02}
    _L0_attn_all = _L0_attn_setup()
    _L0_attn_in = {k: v for k, v in _L0_attn_all.items() if k in ('qkv_w', 'proj_l_w', 'proj_l_b', 'proj_w_w', 'proj_w_b', 'lamb', 'proj_out_w', 'proj_out_b')}
    del _L0_attn_all

    def _L0_ffn_setup():
        import jax, jax.numpy as jnp
        import numpy as np
        CAPACITY_FACTOR = 1.25
        key = jax.random.key(seed)
        ks = jax.random.split(key, 5)
        B, S, D, F, E = (8, 512, 192, 768, 8)
        return {'x': jax.random.normal(ks[0], (B, S, D), jnp.float32), 'switch_w': jax.random.normal(ks[1], (D, E), jnp.float32) * 0.02, 'switch_b': jnp.zeros((E,), jnp.float32), 'w1': jax.random.normal(ks[2], (E, D, F), jnp.float32) * 0.02, 'b1': jnp.zeros((E, F), jnp.float32), 'w2': jax.random.normal(ks[3], (E, F, D), jnp.float32) * 0.02, 'b2': jnp.zeros((E, D), jnp.float32)}
    _L0_ffn_all = _L0_ffn_setup()
    _L0_ffn_in = {k: v for k, v in _L0_ffn_all.items() if k in ('switch_w', 'switch_b', 'w1', 'b1', 'w2', 'b2')}
    del _L0_ffn_all

    def _L1_attn_setup():
        import jax, jax.numpy as jnp
        import numpy as np
        NUM_HEADS = 12
        NUM_LANDMARKS = 64
        PINV_ITERS = 6

        def moore_penrose_iter_pinv(x, iters=PINV_ITERS):
            abs_x = jnp.abs(x)
            col = abs_x.sum(axis=-1)
            row = abs_x.sum(axis=-2)
            z = jnp.swapaxes(x, -1, -2) / (jnp.max(col) * jnp.max(row))
            I = jnp.eye(x.shape[-1], dtype=x.dtype)
            for _ in range(iters):
                xz = x @ z
                z = 0.25 * z @ (13.0 * I - xz @ (15.0 * I - xz @ (7.0 * I - xz)))
            return z

        def _reference_tuple_inner(x, w_qkv, w_proj, b_proj):
            B, N, C = x.shape
            H = NUM_HEADS
            m = NUM_LANDMARKS
            d = C // H
            scale = d ** (-0.5)
            original_N = N
            rem = N % m
            if rem > 0:
                x = jnp.pad(x, ((0, 0), (m - rem, 0), (0, 0)))
                N = x.shape[1]
            qkv = x @ w_qkv.T
            q, k, v = jnp.split(qkv, 3, axis=-1)
            to_heads = lambda t: t.reshape(B, N, H, d).transpose(0, 2, 1, 3)
            q, k, v = (to_heads(q), to_heads(k), to_heads(v))
            q = q * scale
            l = N // m
            q_landmarks = q.reshape(B, H, m, l, d).mean(axis=3)
            k_landmarks = k.reshape(B, H, m, l, d).mean(axis=3)
            sim1 = jnp.einsum('bhnd,bhmd->bhnm', q, k_landmarks)
            sim2 = jnp.einsum('bhid,bhjd->bhij', q_landmarks, k_landmarks)
            sim3 = jnp.einsum('bhmd,bhnd->bhmn', q_landmarks, k)
            attn1 = jax.nn.softmax(sim1, axis=-1)
            attn2 = jax.nn.softmax(sim2, axis=-1)
            attn3 = jax.nn.softmax(sim3, axis=-1)
            attn2_inv = moore_penrose_iter_pinv(attn2, PINV_ITERS)
            attn = attn1 @ attn2_inv @ attn3
            out = attn1 @ (attn2_inv @ (attn3 @ v))
            out = out.transpose(0, 2, 1, 3).reshape(B, N, C)
            out = out[:, -original_N:]
            out = out @ w_proj.T + b_proj
            return (out, attn)
        key = jax.random.key(seed)
        k1, k2, k3, k4 = jax.random.split(key, 4)
        B, N, C = (2, 512, 192)
        x = jax.random.normal(k1, (B, N, C), dtype=jnp.float32)
        w_qkv = jax.random.normal(k2, (3 * C, C), dtype=jnp.float32) * 0.02
        w_proj = jax.random.normal(k3, (C, C), dtype=jnp.float32) * 0.02
        b_proj = jax.random.normal(k4, (C,), dtype=jnp.float32) * 0.02
        return {'x': x, 'w_qkv': w_qkv, 'w_proj': w_proj, 'b_proj': b_proj}
    _L1_attn_all = _L1_attn_setup()
    _L1_attn_in = {k: v for k, v in _L1_attn_all.items() if k in ('w_qkv', 'w_proj', 'b_proj')}
    del _L1_attn_all

    def _L1_ffn_setup():
        import jax, jax.numpy as jnp
        import numpy as np
        B, S, D, E = (8, 256, 192, 8)
        F = 4 * D
        key = jax.random.key(seed)
        ks = jax.random.split(key, 5)
        scale = 0.02
        x = jax.random.normal(ks[0], (B, S, D), jnp.float32)
        gate_w = jax.random.normal(ks[1], (D, E), jnp.float32) * scale
        gate_b = jnp.zeros((E,), jnp.float32)
        w1 = jax.random.normal(ks[2], (E, D, F), jnp.float32) * scale
        b1 = jnp.zeros((E, F), jnp.float32)
        w2 = jax.random.normal(ks[3], (E, F, D), jnp.float32) * scale
        b2 = jnp.zeros((E, D), jnp.float32)
        return {'x': x, 'gate_w': gate_w, 'gate_b': gate_b, 'w1': w1, 'b1': b1, 'w2': w2, 'b2': b2}
    _L1_ffn_all = _L1_ffn_setup()
    _L1_ffn_in = {k: v for k, v in _L1_ffn_all.items() if k in ('gate_w', 'gate_b', 'w1', 'b1', 'w2', 'b2')}
    del _L1_ffn_all
    return {'x': x, 'txt': txt, 'L0_tok_ln_gamma': _L0_tok_in['ln_gamma'], 'L0_tok_ln_beta': _L0_tok_in['ln_beta'], 'L0_tok_w': _L0_tok_in['w'], 'L0_tok_b': _L0_tok_in['b'], 'L0_attn_qkv_w': _L0_attn_in['qkv_w'], 'L0_attn_proj_l_w': _L0_attn_in['proj_l_w'], 'L0_attn_proj_l_b': _L0_attn_in['proj_l_b'], 'L0_attn_proj_w_w': _L0_attn_in['proj_w_w'], 'L0_attn_proj_w_b': _L0_attn_in['proj_w_b'], 'L0_attn_lamb': _L0_attn_in['lamb'], 'L0_attn_proj_out_w': _L0_attn_in['proj_out_w'], 'L0_attn_proj_out_b': _L0_attn_in['proj_out_b'], 'L0_ffn_switch_w': _L0_ffn_in['switch_w'], 'L0_ffn_switch_b': _L0_ffn_in['switch_b'], 'L0_ffn_w1': _L0_ffn_in['w1'], 'L0_ffn_b1': _L0_ffn_in['b1'], 'L0_ffn_w2': _L0_ffn_in['w2'], 'L0_ffn_b2': _L0_ffn_in['b2'], 'L1_attn_w_qkv': _L1_attn_in['w_qkv'], 'L1_attn_w_proj': _L1_attn_in['w_proj'], 'L1_attn_b_proj': _L1_attn_in['b_proj'], 'L1_ffn_gate_w': _L1_ffn_in['gate_w'], 'L1_ffn_gate_b': _L1_ffn_in['gate_b'], 'L1_ffn_w1': _L1_ffn_in['w1'], 'L1_ffn_b1': _L1_ffn_in['b1'], 'L1_ffn_w2': _L1_ffn_in['w2'], 'L1_ffn_b2': _L1_ffn_in['b2']}

def reference(x, txt, L0_tok_ln_gamma, L0_tok_ln_beta, L0_tok_w, L0_tok_b, L0_attn_qkv_w, L0_attn_proj_l_w, L0_attn_proj_l_b, L0_attn_proj_w_w, L0_attn_proj_w_b, L0_attn_lamb, L0_attn_proj_out_w, L0_attn_proj_out_b, L0_ffn_switch_w, L0_ffn_switch_b, L0_ffn_w1, L0_ffn_b1, L0_ffn_w2, L0_ffn_b2, L1_attn_w_qkv, L1_attn_w_proj, L1_attn_b_proj, L1_ffn_gate_w, L1_ffn_gate_b, L1_ffn_w1, L1_ffn_b1, L1_ffn_w2, L1_ffn_b2):
    import jax
    import jax.numpy as jnp

    def _L0_tok_ref(x, ln_gamma, ln_beta, w, b):
        import jax, jax.numpy as jnp
        import numpy as np
        PATCH = 16
        DIM = 192
        LN_EPS = 1e-05

        def _spt_forward(x, ln_gamma, ln_beta, w, b):
            B, C, H, W = x.shape
            p = PATCH
            x_right = jnp.pad(x, ((0, 0), (0, 0), (0, 0), (1, 0)))[:, :, :, :-1]
            x_left = jnp.pad(x, ((0, 0), (0, 0), (0, 0), (0, 1)))[:, :, :, 1:]
            x_down = jnp.pad(x, ((0, 0), (0, 0), (1, 0), (0, 0)))[:, :, :-1, :]
            x_up = jnp.pad(x, ((0, 0), (0, 0), (0, 1), (0, 0)))[:, :, 1:, :]
            xc = jnp.concatenate((x, x_right, x_left, x_down, x_up), axis=1)
            C5 = 5 * C
            h, wgrid = (H // p, W // p)
            tokens = xc.reshape(B, C5, h, p, wgrid, p)
            tokens = tokens.transpose(0, 2, 4, 3, 5, 1)
            tokens = tokens.reshape(B, h * wgrid, p * p * C5)
            mean = jnp.mean(tokens, axis=-1, keepdims=True)
            var = jnp.var(tokens, axis=-1, keepdims=True)
            normed = (tokens - mean) * jax.lax.rsqrt(var + LN_EPS) * ln_gamma + ln_beta
            return jnp.einsum('bnd,de->bne', normed, w) + b
        return _spt_forward(x, ln_gamma, ln_beta, w, b)

    def _L0_attn_ref(x, qkv_w, proj_l_w, proj_l_b, proj_w_w, proj_w_b, lamb, proj_out_w, proj_out_b):
        import jax, jax.numpy as jnp
        import numpy as np
        DIM = 192
        HEADS = 12
        HEAD_DIM = DIM // HEADS
        SCALE = HEAD_DIM ** (-0.5)
        H_CONST = 4
        B, N, C = x.shape
        qkv = (x @ qkv_w.T).reshape(B, N, 3, HEADS, HEAD_DIM)
        qkv = jnp.transpose(qkv, (2, 0, 3, 1, 4))
        q, k, v = (qkv[0] * SCALE, qkv[1], qkv[2])
        attn = jnp.einsum('bhnd,bhmd->bhnm', q, k)
        attn = jnp.einsum('bhnm,gh->bgnm', attn, proj_l_w) + proj_l_b[:, None, None]
        attn = jax.nn.softmax(attn, axis=-1)
        attn = jnp.einsum('bhnm,gh->bgnm', attn, proj_w_w) + proj_w_b[:, None, None]
        eye = jnp.eye(N, dtype=attn.dtype)[None, None]
        reaction = (H_CONST - 1) * jnp.einsum('bhnk,bhkm->bhnm', attn - eye, attn) + attn
        attn = attn + lamb[None, :, None, None] * reaction
        out = jnp.einsum('bhnm,bhmd->bhnd', attn, v)
        out = jnp.transpose(out, (0, 2, 1, 3)).reshape(B, N, C)
        return out @ proj_out_w.T + proj_out_b

    def _L0_ffn_ref(x, switch_w, switch_b, w1, b1, w2, b2):
        import jax, jax.numpy as jnp
        import numpy as np
        CAPACITY_FACTOR = 1.25
        B, S, D = x.shape
        E = w1.shape[0]
        xf = x.reshape(-1, D)
        N = xf.shape[0]
        capacity = int(CAPACITY_FACTOR * N / E)
        probs = jax.nn.softmax(xf @ switch_w + switch_b, axis=-1)
        prob_max = jnp.max(probs, axis=-1)
        routes = jnp.argmax(probs, axis=-1)
        sort_idx = jnp.lexsort((-prob_max, routes))
        counts = jnp.bincount(routes, length=E)
        starts = jnp.concatenate([jnp.zeros((1,), counts.dtype), jnp.cumsum(counts)[:-1]])
        rank_sorted = jnp.arange(N) - starts[routes[sort_idx]]
        rank = jnp.zeros((N,), jnp.int32).at[sort_idx].set(rank_sorted.astype(jnp.int32))
        keep = rank < capacity
        dest_e = jnp.where(keep, routes, E)
        dest_c = jnp.where(keep, rank, 0)
        buf = jnp.zeros((E + 1, capacity, D), xf.dtype).at[dest_e, dest_c].set(xf)
        h = jax.nn.gelu(jnp.einsum('ecd,edf->ecf', buf[:E], w1) + b1[:, None, :], approximate=False)
        o = jnp.einsum('ecf,efd->ecd', h, w2) + b2[:, None, :]
        y_exp = o[routes, dest_c]
        y = jnp.where(keep[:, None], y_exp, xf)
        out = y * prob_max[:, None]
        return out.reshape(B, S, D)

    def _L1_attn_ref(x, w_qkv, w_proj, b_proj):
        import jax, jax.numpy as jnp
        import numpy as np
        NUM_HEADS = 12
        NUM_LANDMARKS = 64
        PINV_ITERS = 6

        def moore_penrose_iter_pinv(x, iters=PINV_ITERS):
            abs_x = jnp.abs(x)
            col = abs_x.sum(axis=-1)
            row = abs_x.sum(axis=-2)
            z = jnp.swapaxes(x, -1, -2) / (jnp.max(col) * jnp.max(row))
            I = jnp.eye(x.shape[-1], dtype=x.dtype)
            for _ in range(iters):
                xz = x @ z
                z = 0.25 * z @ (13.0 * I - xz @ (15.0 * I - xz @ (7.0 * I - xz)))
            return z

        def _reference_tuple_inner(x, w_qkv, w_proj, b_proj):
            B, N, C = x.shape
            H = NUM_HEADS
            m = NUM_LANDMARKS
            d = C // H
            scale = d ** (-0.5)
            original_N = N
            rem = N % m
            if rem > 0:
                x = jnp.pad(x, ((0, 0), (m - rem, 0), (0, 0)))
                N = x.shape[1]
            qkv = x @ w_qkv.T
            q, k, v = jnp.split(qkv, 3, axis=-1)
            to_heads = lambda t: t.reshape(B, N, H, d).transpose(0, 2, 1, 3)
            q, k, v = (to_heads(q), to_heads(k), to_heads(v))
            q = q * scale
            l = N // m
            q_landmarks = q.reshape(B, H, m, l, d).mean(axis=3)
            k_landmarks = k.reshape(B, H, m, l, d).mean(axis=3)
            sim1 = jnp.einsum('bhnd,bhmd->bhnm', q, k_landmarks)
            sim2 = jnp.einsum('bhid,bhjd->bhij', q_landmarks, k_landmarks)
            sim3 = jnp.einsum('bhmd,bhnd->bhmn', q_landmarks, k)
            attn1 = jax.nn.softmax(sim1, axis=-1)
            attn2 = jax.nn.softmax(sim2, axis=-1)
            attn3 = jax.nn.softmax(sim3, axis=-1)
            attn2_inv = moore_penrose_iter_pinv(attn2, PINV_ITERS)
            attn = attn1 @ attn2_inv @ attn3
            out = attn1 @ (attn2_inv @ (attn3 @ v))
            out = out.transpose(0, 2, 1, 3).reshape(B, N, C)
            out = out[:, -original_N:]
            out = out @ w_proj.T + b_proj
            return (out, attn)
        return _reference_tuple_inner(x, w_qkv, w_proj, b_proj)[0]

    def _L1_ffn_ref(x, gate_w, gate_b, w1, b1, w2, b2):
        import jax, jax.numpy as jnp
        import numpy as np
        B, S, D, E = (8, 256, 192, 8)
        F = 4 * D
        orig_shape = x.shape
        xt = x.reshape(-1, x.shape[-1])
        gates = jax.nn.softmax(xt @ gate_w + gate_b, axis=-1)
        expert_idx = jnp.argmax(gates, axis=-1)
        out = jnp.zeros_like(xt)
        n_experts = w1.shape[0]
        for e in range(n_experts):
            h = jax.nn.gelu(xt @ w1[e] + b1[e], approximate=False)
            y = h @ w2[e] + b2[e]
            out = jnp.where((expert_idx == e)[:, None], y, out)
        return out.reshape(orig_shape)
    h = _L0_tok_ref(x, L0_tok_ln_gamma, L0_tok_ln_beta, L0_tok_w, L0_tok_b)
    h = jnp.concatenate([h, txt], axis=1)
    h = h + _L0_attn_ref(_layernorm(h, axis=-1), L0_attn_qkv_w, L0_attn_proj_l_w, L0_attn_proj_l_b, L0_attn_proj_w_w, L0_attn_proj_w_b, L0_attn_lamb, L0_attn_proj_out_w, L0_attn_proj_out_b)
    h = h + _L0_ffn_ref(_layernorm(h, axis=-1), L0_ffn_switch_w, L0_ffn_switch_b, L0_ffn_w1, L0_ffn_b1, L0_ffn_w2, L0_ffn_b2)
    h = h + _L1_attn_ref(_layernorm(h, axis=-1), L1_attn_w_qkv, L1_attn_w_proj, L1_attn_b_proj)
    h = h + _L1_ffn_ref(_layernorm(h, axis=-1), L1_ffn_gate_w, L1_ffn_gate_b, L1_ffn_w1, L1_ffn_b1, L1_ffn_w2, L1_ffn_b2)
    return h

_drawn_inputs = setup_inputs


def setup_inputs(seed=0):
    import zlib

    import numpy as np

    out = dict(_drawn_inputs(seed))
    spreads = {'L0_tok_ln_gamma': (1.0, 0.2),
     'L0_tok_ln_beta': (0.0, 0.1),
     'L0_tok_b': (0.0, 0.1),
     'L0_ffn_switch_b': (0.0, 0.1),
     'L0_ffn_b1': (0.0, 0.617),
     'L0_ffn_b2': (0.0, 0.356),
     'L1_ffn_gate_b': (0.0, 0.1),
     'L1_ffn_b1': (0.0, 0.289),
     'L1_ffn_b2': (0.0, 0.1)}
    factors = {'L0_attn_proj_l_b': 8.0,
     'L0_ffn_w1': 2.943,
     'L0_ffn_w2': 2.724,
     'L1_attn_w_qkv': 2.979,
     'L1_attn_w_proj': 3.099}
    for name, (base, spread) in spreads.items():
        noise = np.random.default_rng([zlib.crc32(name.encode()), seed]).standard_normal(out[name].shape)
        drawn = base * np.exp(spread * noise) if base else spread * noise
        out[name] = jnp.asarray(drawn.astype(out[name].dtype))
    for name, factor in factors.items():
        out[name] = (out[name] * factor).astype(out[name].dtype)
    return out
```

```python
from contextlib import ExitStack

import concourse.bass as bass
from concourse import mybir

F32 = mybir.dt.float32
I32 = mybir.dt.int32
U32 = mybir.dt.uint32
ALU = mybir.AluOpType
ACT = mybir.ActivationFunctionType
AX = mybir.AxisListType

B, CH, IMG, PATCH = 64, 3, 64, 16
GRID = IMG // PATCH
NP_TOK = GRID * GRID
TXT = 77
N = NP_TOK + TXT
NT = B * N
D = 192
D0, D1 = 128, D - 128
H, HD = 12, 16
SCALE = HD ** -0.5
EPS = 1e-5
VAR_CH = 5 * CH
PD = PATCH * PATCH * VAR_CH
KA = 128
KB = VAR_CH * PATCH - KA
E, F = 8, 768
CAP = int(1.25 * NT / E)
LM = 64
PADS = (-N) % LM
NP = N + PADS
ZL = PADS // 2
LR = LM - ZL + 1
TW = 128
BLOCKS = (NT + E * (TW - 1)) // TW
SLOTS = BLOCKS * TW
HC = 196
GATE, KEEP, TOK = 192, 193, 194
FH = F // 2
FT = F // 128


def clear(nc, sems):
    nums = [s.num for s in sems]
    assert nums == list(range(nums[0], nums[0] + len(nums)))
    nc.all_engine_barrier(sems_to_clear=range(nums[0], nums[-1] + 1))


class Chain:

    def __init__(self, eng, sem):
        self.eng, self.sem, self.n = eng, sem, 0

    def __call__(self, ins):
        self.n += 1
        ins.then_inc(self.sem, 1)
        self.eng.wait_ge(self.sem, self.n)


def norm_stats(dve, link, x, st, mv, rows, done):
    link(dve.bn_stats(st[0:rows, :], x))
    link(dve.bn_aggr(mv[0:rows, 0:2], st[0:rows, :]))
    dve.tensor_scalar(mv[0:rows, 1:2], mv[0:rows, 1:2], EPS, None, ALU.add).then_inc(done, 1)


def norm_rstd(pool, G, mv, rows, done):
    pool.tensor_tensor(mv[0:rows, 2:3], mv[0:rows, 1:2], G.half[0:rows, :], ALU.pow).then_inc(done, 1)


def norm_apply(dve, x, out, mv, rows):
    return dve.tensor_scalar(out, x, mv[0:rows, 0:1], mv[0:rows, 2:3], ALU.subtract, ALU.mult)


def allocator(nc, ctx):
    def sb(name, shape, dt=F32):
        return ctx.enter_context(nc.sbuf_tensor(name, shape, dt))

    def sem(name):
        return ctx.enter_context(nc.semaphore(name))
    return sb, sem


def patch_embedding(nc, G, img, w_dram, lg_dram, lb_dram, b_dram, txt, h0):
    NG, GB = B // 8, 8
    PER = 4
    with ExitStack() as ctx:
        sb, sem = allocator(nc, ctx)
        wa, wb = sb("pe_wa", [KA, PATCH, D]), sb("pe_wb", [KB, PATCH, D])
        ga, gb = sb("pe_ga", [KA, PATCH]), sb("pe_gb", [KB, PATCH])
        ba, bb = sb("pe_ba", [KA, PATCH]), sb("pe_bb", [KB, PATCH])
        wga, wgb = sb("pe_wga", [KA, PATCH, D + 1]), sb("pe_wgb", [KB, PATCH, D + 1])
        suma, sumb = sb("pe_suma", [KA, 2, D + 1]), sb("pe_sumb", [KB, 2, D + 1])
        bias = sb("pe_bias", [1, D])
        gsum, csum = sb("pe_gsum", [128, D + 1]), sb("pe_csum", [128, D])
        xa = [sb(f"pe_xa{i}", [KA, GB * GRID * IMG]) for i in range(PER)]
        xb = [sb(f"pe_xb{i}", [KB, GB * GRID * IMG]) for i in range(PER)]
        sq = sb("pe_sq", [128, GB * GRID * IMG])
        sqa = [sb(f"pe_sqa{i}", [KA, 128]) for i in range(PER)]
        sqb = [sb(f"pe_sqb{i}", [KB, 128]) for i in range(PER)]
        mom = [sb(f"pe_mom{i}", [128, 8]) for i in range(PER)]
        ho = [sb(f"pe_ho{i}", [128, D]) for i in range(PER)]
        loaded, scaled, wsum, ones_ps, acted = (sem(f"pe_{n}") for n in ("loaded", "scaled", "wsum", "ones_ps", "csum"))
        pre = [loaded, scaled, wsum, ones_ps, acted]
        chain = sem("pe_chain")
        pre.append(chain)
        sq_done, sq_summed, acc_ps, var_done, rstd_done, h_done, stored = (
            sem(f"pe_{n}") for n in ("sq_done", "sq_summed", "acc_ps", "var_done", "rstd_done", "h_done", "stored"))
        img_in = [sem(f"pe_img_in{i}") for i in range(PER)]
        body = [sq_done, sq_summed, acc_ps, var_done, rstd_done, h_done, stored] + img_in
        with nc.Block() as block:
            @block.sync
            def _(sp):
                for dst, src in ((wa, w_dram[0:KA]), (wb, w_dram[KA:KA + KB]), (ga, lg_dram[0:KA]),
                                 (gb, lg_dram[KA:KA + KB]), (ba, lb_dram[0:KA]), (bb, lb_dram[KA:KA + KB])):
                    sp.dma_start(dst[:], src).then_inc(loaded, 16)
                sp.dma_start(bias[:], b_dram).then_inc(loaded, 16)

            @block.vector
            def _(dve):
                link = Chain(dve, chain)
                dve.wait_ge(loaded, 16 * 7)
                link(dve.memset(wga[:, :, D:D + 1], 1.0))
                link(dve.memset(wgb[:, :, D:D + 1], 1.0))
                for w, g, o, k, be, s in ((wa, ga, wga, KA, ba, suma), (wb, gb, wgb, KB, bb, sumb)):
                    link(dve.tensor_tensor(o[:, :, 0:D], w[:], g[:].unsqueeze(2).broadcast_to([k, PATCH, D]), ALU.mult))
                    link(dve.tensor_reduce(s[:, 0, :], o[:].rearrange("p f e -> p e f"), AX.X, ALU.add))
                    link(dve.tensor_tensor(w[:], w[:], be[:].unsqueeze(2).broadcast_to([k, PATCH, D]), ALU.mult))
                    link(dve.tensor_reduce(s[:, 1, 0:D], w[:].rearrange("p f e -> p e f"), AX.X, ALU.add))
                dve.tensor_copy(mom[0][:, 7:8], G.ones[:, 0:1]).then_inc(scaled, 1)
                dve.wait_ge(ones_ps, 1)
                dve.tensor_copy(gsum[:], G.ps[0][:, 0:D + 1])
                dve.tensor_copy(csum[:], G.ps[1][:, 0:D]).then_inc(acted, 1)
                dve.wait_ge(acted, 1)

            @block.tensor
            def _(pe):
                pe.wait_ge(scaled, 1)
                pe.matmul(G.ps[0][:, 0:D + 1], G.ones[0:KA, :], suma[:, 0, :], start=True, stop=False)
                pe.matmul(G.ps[0][:, 0:D + 1], G.ones[0:KB, :], sumb[:, 0, :], start=False, stop=True)
                pe.matmul(G.ps[1][:, 0:D], G.ones[0:KA, :], suma[:, 1, 0:D], start=True, stop=False)
                pe.matmul(G.ps[1][:, 0:D], G.ones[0:KB, :], sumb[:, 1, 0:D], start=False, stop=False)
                pe.matmul(G.ps[1][:, 0:D], G.ones[0:1, :], bias[:], start=False, stop=True).then_inc(ones_ps, 1)
        clear(nc, pre)
        with nc.Fori(0, NG // PER) as it:
            with nc.Block() as block:
                @block.sync
                def _(sp):
                    for s in range(PER):
                        at = bass.ds((it * PER + s) * (GB * GRID * IMG), GB * GRID * IMG)
                        sp.dma_start(xa[s][:], img[0:KA, at]).then_inc(img_in[s], 16)
                        sp.dma_start(xb[s][:], img[KA:KA + KB, at]).then_inc(img_in[s], 16)
                    for s in range(PER):
                        sp.wait_ge(h_done, s + 1)
                        sp.dma_start(h0[bass.ds((it * PER + s) * 128, 128), :], ho[s][:]).then_inc(stored, 16)
                    sp.wait_ge(stored, 16 * PER)

                @block.scalar
                def _(act):
                    for s in range(PER):
                        act.wait_ge(img_in[s], 32)
                        for t, (x, k) in enumerate(((xa[s], KA), (xb[s], KB))):
                            if s or t:
                                act.wait_ge(sq_summed, 2 * s + t)
                            act.activation(sq[0:k, :], x[:], ACT.Square).then_inc(sq_done, 1)

                @block.vector
                def _(dve):
                    link = Chain(dve, chain)
                    for s in range(PER):
                        for t, (o, k) in enumerate(((sqa[s], KA), (sqb[s], KB))):
                            dve.wait_ge(sq_done, 2 * s + t + 1)
                            dve.tensor_reduce(o[:], sq[0:k, :].rearrange("p (t f) -> p t f", f=PATCH), AX.X,
                                              ALU.add).then_inc(sq_summed, 1)
                        m, acc = mom[s], G.ps[s]
                        dve.wait_ge(acc_ps, s + 1)
                        link(dve.tensor_scalar(m[:, 0:1], acc[:, D:D + 1], 1.0 / PD, None, ALU.mult))
                        link(dve.tensor_tensor(m[:, 1:2], m[:, 0:1], m[:, 0:1], ALU.mult))
                        link(dve.tensor_scalar(m[:, 2:3], G.ps[4 + s][:, 0:1], 1.0 / PD, m[:, 1:2], ALU.mult, ALU.subtract))
                        link(dve.tensor_scalar(m[:, 2:3], m[:, 2:3], EPS, None, ALU.add))
                        dve.tensor_scalar(m[:, 4:5], m[:, 0:1], -1.0, None, ALU.mult).then_inc(var_done, 1)
                        dve.wait_ge(var_done, s + 1)
                        link(dve.scalar_tensor_tensor(ho[s][:], gsum[:, 0:D], m[:, 4:5], acc[:, 0:D], ALU.mult, ALU.add))
                        dve.wait_ge(rstd_done, s + 1)
                        dve.scalar_tensor_tensor(ho[s][:], ho[s][:], m[:, 3:4], csum[:], ALU.mult,
                                                 ALU.add).then_inc(h_done, 1)

                @block.gpsimd
                def _(pool):
                    for s in range(PER):
                        pool.wait_ge(var_done, s + 1)
                        pool.tensor_tensor(mom[s][:, 3:4], mom[s][:, 2:3], G.half[:], ALU.pow).then_inc(rstd_done, 1)

                @block.tensor
                def _(pe):
                    for s in range(PER):
                        pe.wait_ge(img_in[s], 32)
                        va = xa[s][:].rearrange("p (t f) -> p f t", f=PATCH)
                        vb = xb[s][:].rearrange("p (t f) -> p f t", f=PATCH)
                        for f in range(PATCH):
                            pe.matmul(G.ps[s][:, 0:D + 1], va[:, f, :], wga[:, f, :], start=(f == 0), stop=False)
                            pe.matmul(G.ps[s][:, 0:D + 1], vb[:, f, :], wgb[:, f, :], start=False,
                                      stop=(f == PATCH - 1))
                        pe.wait_ge(sq_summed, 2 * s + 2)
                        pe.matmul(G.ps[4 + s][:, 0:1], sqa[s][:], G.ones[0:KA, 0:1], start=True, stop=False)
                        pe.matmul(G.ps[4 + s][:, 0:1], sqb[s][:], G.ones[0:KB, 0:1], start=False,
                                  stop=True).then_inc(acc_ps, 1)
            clear(nc, [chain] + body)


def load_tokens(nc, G, h0, txt, weights):
    with ExitStack() as ctx:
        sb, sem = allocator(nc, ctx)
        rows_in = sem("rows_in")
        with nc.Block() as block:
            @block.sync
            def _(sp):
                h = G.h[:]
                sp.dma_start(h[0:NP_TOK, :, 0:D], h0.rearrange("(b n) d -> n b d", n=NP_TOK)).then_inc(rows_in, 16)
                sp.dma_start(h[NP_TOK:N, :, 0:D], txt.rearrange("b n d -> n b d")).then_inc(rows_in, 16)
                sp.wait_ge(rows_in, 32)
        clear(nc, [rows_in])


def talking_attention(nc, G, A):
    with ExitStack() as ctx:
        sb, sem = allocator(nc, ctx)
        names = ("var", "rstd", "xn", "xT_ps", "xT", "qkv_ps", "qk", "v", "qs0", "qs1", "s_ps", "negmax", "exp", "p", "pT_ps",
                 "pT", "vs", "u_ps", "us", "r_ps", "o", "oT_ps", "oT", "y_ps", "yn", "yT_ps", "yT", "lg_ps",
                 "dve_chain", "weights_in", "ready")
        S = {n: sem("l0_" + n) for n in names}
        wqkv0, wqkv1 = sb("l0_wqkv0", [D0, 3 * D]), sb("l0_wqkv1", [D1, 3 * D])
        wl0, wl1 = sb("l0_wl0", [D0, H]), sb("l0_wl1", [D1, H])
        lbias = sb("l0_lbias", [D1 + 1, H])
        ww = sb("l0_ww", [N, (H + 1) * D])
        lam = sb("l0_lam", [N, D])
        c1, c2 = sb("l0_c1", [N, D]), sb("l0_c2", [N, D])
        wo0, wo1 = sb("l0_wo0", [D0, D]), sb("l0_wo1", [D1 + 1, D])
        sw0, sw1 = sb("l0_sw0", [D0, E]), sb("l0_sw1", [D1 + 1, E])
        T = []
        for s in range(2):
            t = {}
            for n, shape in (("st", [N, 6]), ("mv", [N, 3]), ("xn", [N, D]), ("xT0", [D0, N]), ("xT1", [D1, N]),
                             ("q0", [D0, N]), ("q1", [D1, N]), ("k0", [D0, N]), ("k1", [D1 + 1, N]), ("v", [N, D]),
                             ("qs0", [D0, H, N]), ("qs1", [D1 + 1, H, N]), ("nm", [N, H]), ("rs", [N, H]),
                             ("p", [N, H, N]), ("pT", [N, H, N]), ("vs", [N, H + 1, D]), ("u", [N, D]),
                             ("o", [N, D]), ("oT0", [D0, N]), ("oT1", [D1 + 1, N])):
                t[n] = sb(f"l0_{n}_{s}", shape)
            T.append(t)
        with nc.Block() as block:
            @block.sync
            def _(sp):
                lots = ((wqkv0[:], A["wqkv"][0:D0]), (wqkv1[:], A["wqkv"][D0:D]), (wl0[:], A["wl"][0:D0]),
                        (wl1[:], A["wl"][D0:D]), (lbias[D1:D1 + 1, :], A["lb"]),
                        (ww[:], A["ww"].broadcast_to([N, (H + 1) * D])), (lam[:], A["lamb"].broadcast_to([N, D])),
                        (wo0[:], A["wo"][0:D0]), (wo1[:], A["wo"][D0:D + 1]),
                        (sw0[:], A["sw"][0:D0]), (sw1[:], A["sw"][D0:D + 1]))
                for dst, src in lots:
                    sp.dma_start(dst, src).then_inc(S["weights_in"], 16)
                sp.wait_ge(S["weights_in"], 16 * len(lots))

            @block.vector
            def _(dve):
                dve.wait_ge(S["weights_in"], 16 * 11)
                dve.tensor_scalar(c1[:], lam[:], -2.0, 1.0, ALU.mult, ALU.add)
                dve.tensor_scalar(c2[:], lam[:], 3.0, None, ALU.mult)
                for s in range(2):
                    dve.memset(T[s]["k1"][D1:D1 + 1, :], 1.0)
                    dve.memset(T[s]["oT1"][D1:D1 + 1, :], 1.0)
                    dve.tensor_copy(T[s]["qs1"][D1:D1 + 1, :, :],
                                    lbias[D1:D1 + 1, :].unsqueeze(2).broadcast_to([1, H, N])).then_inc(S["ready"], 1)
                dve.wait_ge(S["ready"], 2)
        clear(nc, list(S.values()))
        with nc.Fori(0, B // 2) as it:
            hrow = [G.h[:, bass.ds(it * 2 + s, 1), 0:D].rearrange("p a d -> p (a d)") for s in range(2)]
            bank = [[G.ps[4 * s + j] for j in range(4)] for s in range(2)]
            with nc.Block() as block:
                @block.vector
                def _(dve):
                    link = Chain(dve, S["dve_chain"])
                    for s in range(2):
                        t = T[s]
                        norm_stats(dve, link, hrow[s], t["st"], t["mv"], N, S["var"])
                    for s in range(2):
                        t = T[s]
                        dve.wait_ge(S["rstd"], s + 1)
                        norm_apply(dve, hrow[s], t["xn"][:], t["mv"], N).then_inc(S["xn"], 1)
                    for s in range(2):
                        t, bk = T[s], bank[s]
                        dve.wait_ge(S["qkv_ps"], s + 1)
                        dve.tensor_copy(t["v"][:], bk[2][0:N, 0:D]).then_inc(S["v"], 1)
                        dve.wait_ge(S["qk"], s + 1)
                        dve.tensor_tensor(t["qs0"][:], t["q0"][:].unsqueeze(1).broadcast_to([D0, H, N]),
                                          wl0[:].unsqueeze(2).broadcast_to([D0, H, N]), ALU.mult).then_inc(S["qs0"], 1)
                    for s in range(2):
                        t, bk = T[s], bank[s]
                        for j in range(3):
                            dve.wait_ge(S["s_ps"], 3 * s + j + 1)
                            dve.tensor_reduce(t["nm"][:, 4 * j:4 * j + 4],
                                              bk[1 + j][0:N, 0:4 * N].rearrange("p (g m) -> p g m", m=N), AX.X,
                                              ALU.max, negate=True).then_inc(S["negmax"], 1)
                    for s in range(2):
                        t = T[s]
                        dve.wait_ge(S["exp"], 3 * (s + 1))
                        link(dve.reciprocal(t["rs"][:], t["rs"][:]))
                        dve.tensor_tensor(t["p"][:], t["p"][:], t["rs"][:].unsqueeze(2).broadcast_to([N, H, N]),
                                          ALU.mult).then_inc(S["p"], 1)
                    for s in range(2):
                        t, bk = T[s], bank[s]
                        dve.wait_ge(S["u_ps"], s + 1)
                        link(dve.tensor_copy(t["u"][:], bk[3][0:N, 0:D]))
                        dve.tensor_tensor(t["vs"][:], t["u"][:].unsqueeze(1).broadcast_to([N, H + 1, D]),
                                          ww[:].rearrange("p (h d) -> p h d", d=D), ALU.mult).then_inc(S["us"], 1)
                        dve.wait_ge(S["us"], s + 1)
                        link(dve.tensor_tensor(t["u"][:], t["u"][:], c1[:], ALU.mult))
                    for s in range(2):
                        t, bk = T[s], bank[s]
                        dve.wait_ge(S["r_ps"], s + 1)
                        link(dve.tensor_tensor(t["o"][:], bk[0][0:N, 0:D], c2[:], ALU.mult))
                        dve.tensor_tensor(t["o"][:], t["o"][:], t["u"][:], ALU.add).then_inc(S["o"], 1)
                    for s in range(2):
                        t, bk = T[s], bank[s]
                        dve.wait_ge(S["y_ps"], s + 1)
                        link(dve.tensor_tensor(hrow[s], hrow[s], bk[2][0:N, 0:D], ALU.add))
                        norm_stats(dve, link, hrow[s], t["st"], t["mv"], N, S["var"])
                    for s in range(2):
                        t = T[s]
                        dve.wait_ge(S["rstd"], 2 + s + 1)
                        norm_apply(dve, hrow[s], t["xn"][:], t["mv"], N).then_inc(S["yn"], 1)
                    for s in range(2):
                        dve.wait_ge(S["lg_ps"], s + 1)
                        link(dve.tensor_copy(G.lg[:, :, bass.ds(it * 2 + s, 1)], bank[s][3][0:N, 0:E].unsqueeze(2)))

                @block.gpsimd
                def _(pool):
                    for s in range(2):
                        pool.wait_ge(S["var"], s + 1)
                        norm_rstd(pool, G, T[s]["mv"], N, S["rstd"])
                    for s in range(2):
                        t = T[s]
                        pool.wait_ge(S["qk"], s + 1)
                        pool.tensor_tensor(t["qs1"][0:D1, :, :], t["q1"][:].unsqueeze(1).broadcast_to([D1, H, N]),
                                           wl1[:].unsqueeze(2).broadcast_to([D1, H, N]), ALU.mult).then_inc(S["qs1"], 1)
                    for s in range(2):
                        t = T[s]
                        pool.wait_ge(S["v"], s + 1)
                        pool.tensor_tensor(t["vs"][:], t["v"][:].unsqueeze(1).broadcast_to([N, H + 1, D]),
                                           ww[:].rearrange("p (h d) -> p h d", d=D), ALU.mult).then_inc(S["vs"], 1)
                    for s in range(2):
                        pool.wait_ge(S["var"], 2 + s + 1)
                        norm_rstd(pool, G, T[s]["mv"], N, S["rstd"])

                @block.scalar
                def _(act):
                    for s in range(2):
                        t, bk = T[s], bank[s]
                        act.wait_ge(S["xT_ps"], s + 1)
                        act.copy(t["xT0"][:], bk[0][:, 0:N])
                        act.copy(t["xT1"][:], bk[0][0:D1, 128:128 + N]).then_inc(S["xT"], 1)
                    for s in range(2):
                        t, bk = T[s], bank[s]
                        act.wait_ge(S["qkv_ps"], s + 1)
                        act.mul(t["q0"][:], bk[1][:, 0:N], SCALE)
                        act.mul(t["q1"][:], bk[1][0:D1, N:2 * N], SCALE)
                        act.copy(t["k0"][:], bk[1][:, 2 * N:3 * N])
                        act.copy(t["k1"][0:D1, :], bk[1][0:D1, 3 * N:4 * N]).then_inc(S["qk"], 1)
                    for s in range(2):
                        t, bk = T[s], bank[s]
                        for j in range(3):
                            act.wait_ge(S["negmax"], 3 * s + j + 1)
                            for g in range(4 * j, 4 * j + 4):
                                last = act.activation(t["p"][:, g, :], bk[1 + j][0:N, (g % 4) * N:(g % 4 + 1) * N],
                                                      ACT.Exp, bias=t["nm"][:, g:g + 1], accum_out=t["rs"][:, g:g + 1])
                            last.then_inc(S["exp"], 1)
                    for s in range(2):
                        t, bk = T[s], bank[s]
                        for j in range(3):
                            act.wait_ge(S["pT_ps"], 3 * s + j + 1)
                            act.copy(t["pT"][:, 4 * j:4 * j + 4, :].rearrange("p g m -> p (g m)"),
                                     bk[j][0:N, 0:4 * N]).then_inc(S["pT"], 1)
                    for name, o0, o1, b in (("oT", "oT0", "oT1", 1), ("yT", "oT0", "oT1", 0)):
                        for s in range(2):
                            t, bk = T[s], bank[s]
                            act.wait_ge(S[name + "_ps"], s + 1)
                            act.copy(t[o0][:], bk[b][:, 0:N])
                            act.copy(t[o1][0:D1, :], bk[b][0:D1, 128:128 + N]).then_inc(S[name], 1)

                @block.tensor
                def _(pe):
                    def turn(src, bk):
                        pe.transpose(bk[:, 0:N], src[:, 0:D0], G.ident[0:N, 0:N])
                        return pe.transpose(bk[0:D1, 128:128 + N], src[:, D0:D], G.ident[0:N, 0:N])

                    for s in range(2):
                        pe.wait_ge(S["xn"], s + 1)
                        turn(T[s]["xn"], bank[s][0]).then_inc(S["xT_ps"], 1)
                    for s in range(2):
                        t, bk = T[s], bank[s]
                        pe.wait_ge(S["xT"], s + 1)
                        for j in range(2):
                            for m, (a, n) in enumerate(((0, D0), (D0, D1))):
                                o = bk[1][0:n, (2 * j + m) * N:(2 * j + m + 1) * N]
                                pe.matmul(o, wqkv0[:, j * D + a:j * D + a + n], t["xT0"][:], start=True, stop=False)
                                pe.matmul(o, wqkv1[:, j * D + a:j * D + a + n], t["xT1"][:], start=False, stop=True)
                        pe.matmul(bk[2][0:N, 0:D], t["xT0"][:], wqkv0[:, 2 * D:3 * D], start=True, stop=False)
                        pe.matmul(bk[2][0:N, 0:D], t["xT1"][:], wqkv1[:, 2 * D:3 * D], start=False,
                                  stop=True).then_inc(S["qkv_ps"], 1)
                    for s in range(2):
                        t, bk = T[s], bank[s]
                        pe.wait_ge(S["qs0"], s + 1)
                        pe.wait_ge(S["qs1"], s + 1)
                        for g in range(H):
                            o = bk[1 + g // 4][0:N, (g % 4) * N:(g % 4 + 1) * N]
                            pe.matmul(o, t["qs0"][:, g, :], t["k0"][:], start=True, stop=False)
                            mm = pe.matmul(o, t["qs1"][:, g, :], t["k1"][:], start=False, stop=True)
                            if g % 4 == 3:
                                mm.then_inc(S["s_ps"], 1)
                    for s in range(2):
                        t, bk = T[s], bank[s]
                        pe.wait_ge(S["p"], s + 1)
                        for g in range(H):
                            mm = pe.transpose(bk[g // 4][0:N, (g % 4) * N:(g % 4 + 1) * N], t["p"][:, g, :],
                                              G.ident[0:N, 0:N])
                            if g % 4 == 3:
                                mm.then_inc(S["pT_ps"], 1)

                    def mixed(t, o):
                        for h in range(H):
                            pe.matmul(o, t["pT"][:, h, :], t["vs"][:, h, :], start=(h == 0), stop=False)
                        return pe.matmul(o, G.ones[0:N, 0:N], t["vs"][:, H, :], start=False, stop=True)

                    for s in range(2):
                        pe.wait_ge(S["pT"], 3 * (s + 1))
                        pe.wait_ge(S["vs"], s + 1)
                        mixed(T[s], bank[s][3][0:N, 0:D]).then_inc(S["u_ps"], 1)
                    for s in range(2):
                        pe.wait_ge(S["us"], s + 1)
                        mixed(T[s], bank[s][0][0:N, 0:D]).then_inc(S["r_ps"], 1)
                    for s in range(2):
                        pe.wait_ge(S["o"], s + 1)
                        turn(T[s]["o"], bank[s][1]).then_inc(S["oT_ps"], 1)
                    for s in range(2):
                        t, bk = T[s], bank[s]
                        pe.wait_ge(S["oT"], s + 1)
                        pe.matmul(bk[2][0:N, 0:D], t["oT0"][:], wo0[:], start=True, stop=False)
                        pe.matmul(bk[2][0:N, 0:D], t["oT1"][:], wo1[:], start=False, stop=True).then_inc(S["y_ps"], 1)
                    for s in range(2):
                        pe.wait_ge(S["yn"], s + 1)
                        turn(T[s]["xn"], bank[s][0]).then_inc(S["yT_ps"], 1)
                    for s in range(2):
                        t, bk = T[s], bank[s]
                        pe.wait_ge(S["yT"], s + 1)
                        pe.matmul(bk[3][0:N, 0:E], t["oT0"][:], sw0[:], start=True, stop=False)
                        pe.matmul(bk[3][0:N, 0:E], t["oT1"][:], sw1[:], start=False, stop=True).then_inc(S["lg_ps"], 1)
            clear(nc, list(S.values()))


def route(nc, G, xs, layer):
    Q = E * B
    with ExitStack() as ctx:
        sb, sem = allocator(nc, ctx)
        names = ("dve_chain", "dve_to_act", "act_to_dve", "dve_to_pe", "pe_to_dve", "iota", "dest")
        S = {n: sem(f"r{layer}_" + n) for n in names}
        z, ex, oh, key, t0, t1, rk, ekeep = (sb(f"r{layer}_{n}", [N, E, B]) for n in
                                             ("z", "ex", "oh", "key", "t0", "t1", "rk", "keep"))
        mx, t2, gate, dest = (sb(f"r{layer}_{n}", [N, B]) for n in ("mx", "t2", "gate", "dest"))
        dest_i = sb(f"r{layer}_desti", [N, B], I32)
        tok_i = sb(f"r{layer}_toki", [N, B], I32)
        pref_i = sb(f"r{layer}_prefi", [N, E], I32)
        pref = sb(f"r{layer}_pref", [N, E])
        lo, cand, cnt, few, step = (sb(f"r{layer}_{n}", [N, E]) for n in ("lo", "cand", "cnt", "few", "step"))
        blk, cum, base, start = (sb(f"r{layer}_{n}", [N, E]) for n in ("blk", "cum", "base", "start"))
        full_i, full = sb(f"r{layer}_fulli", [N, E, BLOCKS], I32), sb(f"r{layer}_full", [N, E, BLOCKS])
        bj_i = sb(f"r{layer}_bji", [1, BLOCKS, E], I32)
        bj, bje = sb(f"r{layer}_bj", [1, BLOCKS, E]), sb(f"r{layer}_bje", [1, BLOCKS])
        over_b = lambda a: a[:].unsqueeze(2).broadcast_to([N, E, B])
        over_e = lambda a: a[:].unsqueeze(1).broadcast_to([N, E, B])
        by_b = lambda a: a[:].rearrange("p e b -> p b e")
        flat = lambda a: a[:].rearrange("p e b -> p (e b)")
        counts = {"act": 0, "pe": 0}

        def ranked(dve, link, mask, out):
            counts["pe"] += 1
            dve.nop().then_inc(S["dve_to_pe"], 1)
            dve.wait_ge(S["pe_to_dve"], counts["pe"])
            link(dve.tensor_copy(flat(t1), G.ps[1][0:N, 0:Q]))
            link(dve.tensor_tensor_scan(flat(out), flat(z_ones), flat(t1), 0.0, ALU.mult, ALU.add))
            link(dve.tensor_tensor(out[:], out[:], t1[:], ALU.subtract))
            link(dve.tensor_copy(start[:], out[:, :, 0]))
            link(dve.tensor_tensor(cnt[:], out[:, :, B - 1], t1[:, :, B - 1], ALU.add))
            link(dve.tensor_tensor(cnt[:], cnt[:], start[:], ALU.subtract))
            link(dve.tensor_tensor(out[:], out[:], over_b(start), ALU.subtract))
            link(dve.tensor_tensor(flat(out), flat(out), G.ps[0][0:N, 0:Q], ALU.add))

        z_ones = ex if False else sb(f"r{layer}_ones", [N, E, B])
        with nc.Block() as block:
            @block.gpsimd
            def _(pool):
                pool.iota(tok_i[:], [[N, B]], base=0, channel_multiplier=1)
                pool.iota(pref_i[:], [[-1, E]], base=E, channel_multiplier=0)
                pool.iota(full_i[:], [[0, E], [TW, BLOCKS]], base=0, channel_multiplier=0)
                pool.iota(bj_i[:], [[1, BLOCKS], [0, E]], base=0, channel_multiplier=0).then_inc(S["iota"], 1)

            @block.scalar
            def _(act):
                act.wait_ge(S["dve_to_act"], 1)
                act.activation(flat(ex), flat(z), ACT.Exp).then_inc(S["act_to_dve"], 1)

            @block.vector
            def _(dve):
                link = Chain(dve, S["dve_chain"])
                dve.memset(z_ones[:], 1.0)
                link(dve.tensor_reduce(mx[:], by_b(G.lg), AX.X, ALU.max))
                dve.tensor_tensor(z[:], G.lg[:], over_e(mx), ALU.subtract).then_inc(S["dve_to_act"], 1)
                dve.wait_ge(S["iota"], 1)
                link(dve.tensor_copy(G.h[:, :, TOK], tok_i[:]))
                link(dve.tensor_copy(pref[:], pref_i[:]))
                link(dve.tensor_copy(bj[:], bj_i[:]))
                link(dve.tensor_copy(full[:], full_i[:]))
                dve.wait_ge(S["act_to_dve"], 1)
                link(dve.tensor_reduce(t2[:], by_b(ex), AX.X, ALU.add))
                link(dve.reciprocal(gate[:], t2[:]))
                link(dve.tensor_copy(G.h[:, :, GATE], gate[:]))
                link(dve.tensor_scalar(t0[:], ex[:], 1.0, None, ALU.is_ge))
                link(dve.tensor_tensor(t0[:], t0[:], over_b(pref), ALU.mult))
                link(dve.tensor_reduce(t2[:], by_b(t0), AX.X, ALU.max))
                link(dve.tensor_tensor(oh[:], t0[:], over_e(t2), ALU.is_equal))
                link(dve.tensor_tensor(key[:], oh[:], over_e(gate), ALU.mult))
                link(dve.memset(lo[:], 0.0))
                link(dve.memset(step[:], 1.0))
                if layer:
                    link(dve.memset(G.h[:, :, KEEP:KEEP + 1], 1.0))
        clear(nc, list(S.values()))
        if layer == 0:
            with nc.Fori(0, 28) as it:
                with nc.Block() as block:
                    @block.tensor
                    def _(pe):
                        pe.wait_ge(S["dve_to_pe"], 1)
                        pe.matmul(G.ps[2][0:N, 0:E], G.ones[0:N, 0:N], few[:], start=True,
                                  stop=True).then_inc(S["pe_to_dve"], 1)

                    @block.vector
                    def _(dve):
                        link = Chain(dve, S["dve_chain"])
                        link(dve.tensor_tensor(cand[:], lo[:], step[:], ALU.add))
                        link(dve.tensor_tensor(t0[:], key[:], over_b(cand), ALU.is_ge))
                        dve.tensor_reduce(few[:], t0[:], AX.X, ALU.add).then_inc(S["dve_to_pe"], 1)
                        dve.wait_ge(S["pe_to_dve"], 1)
                        link(dve.tensor_scalar(cnt[:], G.ps[2][0:N, 0:E], float(CAP), None, ALU.is_ge))
                        link(dve.tensor_tensor(cnt[:], cnt[:], step[:], ALU.mult))
                        link(dve.tensor_tensor(lo[:], lo[:], cnt[:], ALU.add))
                        link(dve.tensor_scalar(step[:], step[:], 0.5, None, ALU.mult))
                clear(nc, list(S.values()))
        masks = [oh] if layer else [ekeep, oh]
        with nc.Block() as block:
            @block.tensor
            def _(pe):
                n = 0
                if layer == 0:
                    n += 1
                    pe.wait_ge(S["dve_to_pe"], n)
                    pe.matmul(G.ps[2][0:N, 0:E], G.ones[0:N, 0:N], few[:], start=True, stop=True)\
                        .then_inc(S["pe_to_dve"], 1)
                for m in masks:
                    n += 1
                    pe.wait_ge(S["dve_to_pe"], n)
                    pe.matmul(G.ps[0][0:N, 0:Q], G.before[0:N, 0:N], flat(m), start=True, stop=True)
                    pe.matmul(G.ps[1][0:N, 0:Q], G.ones[0:N, 0:N], flat(m), start=True, stop=True)\
                        .then_inc(S["pe_to_dve"], 1)

            @block.vector
            def _(dve):
                link = Chain(dve, S["dve_chain"])
                if layer == 0:
                    link(dve.tensor_tensor(t0[:], key[:], over_b(lo), ALU.is_gt))
                    dve.tensor_reduce(few[:], t0[:], AX.X, ALU.add).then_inc(S["dve_to_pe"], 1)
                    counts["pe"] += 1
                    dve.wait_ge(S["pe_to_dve"], counts["pe"])
                    link(dve.tensor_scalar(few[:], G.ps[2][0:N, 0:E], -1.0, float(CAP), ALU.mult, ALU.add))
                    link(dve.tensor_tensor(ekeep[:], key[:], over_b(lo), ALU.is_equal))
                    link(dve.tensor_tensor(ekeep[:], ekeep[:], oh[:], ALU.mult))
                    ranked(dve, link, ekeep, rk)
                    link(dve.tensor_tensor(rk[:], rk[:], over_b(few), ALU.is_lt))
                    link(dve.tensor_tensor(ekeep[:], ekeep[:], rk[:], ALU.mult))
                    link(dve.tensor_tensor(ekeep[:], ekeep[:], t0[:], ALU.add))
                    link(dve.tensor_reduce(G.h[:, :, KEEP], by_b(ekeep), AX.X, ALU.add))
                ranked(dve, link, oh, rk)
                link(dve.tensor_tensor(full[:], cnt[:].unsqueeze(2).broadcast_to([N, E, BLOCKS]),
                                       full[:], ALU.is_gt))
                link(dve.tensor_reduce(blk[:], full[:], AX.X, ALU.add))
                link(dve.tensor_scalar(blk[:], blk[:], float(TW), None, ALU.mult))
                link(dve.tensor_tensor_scan(cum[:], z_ones[:, :, 0], blk[:], 0.0, ALU.mult, ALU.add))
                link(dve.tensor_tensor(base[:], cum[:], blk[:], ALU.subtract))
                link(dve.tensor_tensor(rk[:], rk[:], over_b(base), ALU.add))
                link(dve.tensor_tensor(rk[:], rk[:], oh[:], ALU.mult))
                link(dve.tensor_reduce(dest[:], by_b(rk), AX.X, ALU.add))
                dve.tensor_copy(dest_i[:], dest[:]).then_inc(S["dest"], 1)
                link(dve.tensor_scalar(cum[:], cum[:], 1.0 / TW, None, ALU.mult))
                link(dve.tensor_tensor(bj[:], bj[:], cum[0:1, :].unsqueeze(1).broadcast_to([1, BLOCKS, E]), ALU.is_ge))
                link(dve.tensor_reduce(bje[:], bj[:], AX.X, ALU.add))
                link(dve.tensor_scalar(bje[:], bje[:], float(E - 1), None, ALU.min))
                link(dve.tensor_copy(G.expert[0:1, :], bje[:]))

            @block.gpsimd
            def _(pool):
                pool.wait_ge(S["dest"], 1)
                for b in range(B):
                    pool.indirect_dma_start(xs, bass.IndirectOffsetOnAxis(dest_i[:, b:b + 1].bitcast(U32), 0),
                                            G.h[:, b, :], None).then_inc(G.rows_sent[layer], 16)
                pool.wait_ge(G.rows_sent[layer], 16 * B)
        clear(nc, list(S.values()))


def experts(nc, G, xs, dst, W, layer):
    PER = 6
    n_it = BLOCKS // PER
    assert BLOCKS % PER == 0
    with ExitStack() as ctx:
        sb, sem = allocator(nc, ctx)
        names = ("weights_in", "ones_set", "xs_in", "xn", "xT_ps", "xT", "h_ps", "gelu", "hT_ps", "hT", "y_ps", "out",
                 "var", "rstd", "dve_chain")
        S = {n: sem(f"f{layer}_" + n) for n in names}
        w1a, w1b = sb(f"f{layer}_w1a", [D0, E * F]), sb(f"f{layer}_w1b", [D1 + 1, E * F])
        w2 = sb(f"f{layer}_w2s", [128, E * FT * D])
        b2 = sb(f"f{layer}_b2s", [1, E * D])
        x = [sb(f"f{layer}_x{i}", [TW, HC]) for i in range(PER)]
        o = [sb(f"f{layer}_o{i}", [TW, D]) for i in range(PER)]
        tok = [sb(f"f{layer}_tok{i}", [TW, 1], I32) for i in range(PER)]
        xn = [sb(f"f{layer}_xn{i}", [TW, D]) for i in range(PER)]
        st = [sb(f"f{layer}_st{i}", [TW, 6]) for i in range(PER)]
        mv = [sb(f"f{layer}_mv{i}", [TW, 3]) for i in range(PER)]
        xT0 = [sb(f"f{layer}_xT0{i}", [D0, TW]) for i in range(2)]
        xT1 = [sb(f"f{layer}_xT1{i}", [D1 + 1, TW]) for i in range(2)]
        hs = [sb(f"f{layer}_hs{i}", [TW, F]) for i in range(2)]
        hT = [sb(f"f{layer}_hT{i}", [128, FT, TW]) for i in range(2)]
        with nc.Block() as block:
            @block.sync
            def _(sp):
                for e in range(E):
                    sp.dma_start(w1a[:, e * F:(e + 1) * F], W["w1"][e, 0:D0, :]).then_inc(S["weights_in"], 16)
                    sp.dma_start(w1b[:, e * F:(e + 1) * F], W["w1"][e, D0:D + 1, :]).then_inc(S["weights_in"], 16)
                    sp.dma_start(w2[:, e * FT * D:(e + 1) * FT * D].rearrange("p (c d) -> p c d", d=D),
                                 W["w2"][e].rearrange("(c p) d -> p c d", p=128)).then_inc(S["weights_in"], 16)
                sp.dma_start(b2[:], W["b2"]).then_inc(S["weights_in"], 16)
                sp.wait_ge(S["weights_in"], 16 * (3 * E + 1))

            @block.vector
            def _(dve):
                for i in range(2):
                    dve.memset(xT1[i][D1:D1 + 1, :], 1.0).then_inc(S["ones_set"], 1)
                dve.wait_ge(S["ones_set"], 2)
        clear(nc, list(S.values()))
        with nc.Fori(0, n_it) as it:
            with nc.Block() as block:
                @block.sync
                def _(sp):
                    for i in range(PER):
                        sp.dma_start(x[i][:], xs[bass.ds((it * PER + i) * TW, TW), :]).then_inc(S["xs_in"], 16)

                @block.vector
                def _(dve):
                    link = Chain(dve, S["dve_chain"])

                    def norm(i):
                        dve.wait_ge(S["rstd"], i + 1)
                        norm_apply(dve, x[i][:, 0:D], xn[i][:], mv[i], TW).then_inc(S["xn"], 1)

                    def h_turned(i):
                        u = i % 2
                        dve.wait_ge(S["hT_ps"], i + 1)
                        if i >= 2:
                            dve.wait_ge(S["y_ps"], i - 1)
                        dve.tensor_copy(hT[u][:, 0:4, :].rearrange("p c t -> p (c t)"), G.ps[6][:, :])
                        dve.tensor_copy(hT[u][:, 4:6, :].rearrange("p c t -> p (c t)"),
                                        G.ps[7][:, 0:2 * TW]).then_inc(S["hT"], 1)

                    def finish(i):
                        dve.wait_ge(S["y_ps"], i + 1)
                        y = G.ps[1][:, 0:D]
                        if layer:
                            dve.tensor_tensor(o[i][:], y, x[i][:, 0:D], ALU.add).then_inc(S["out"], 1)
                        else:
                            link(dve.tensor_tensor(o[i][:], y, xn[i][:], ALU.subtract))
                            link(dve.scalar_tensor_tensor(o[i][:], o[i][:], x[i][:, KEEP:KEEP + 1], xn[i][:],
                                                          ALU.mult, ALU.add))
                            dve.scalar_tensor_tensor(o[i][:], o[i][:], x[i][:, GATE:GATE + 1], x[i][:, 0:D],
                                                     ALU.mult, ALU.add).then_inc(S["out"], 1)

                    dve.wait_ge(S["xs_in"], 16 * PER)
                    for i in range(PER):
                        norm_stats(dve, link, x[i][:, 0:D], st[i], mv[i], TW, S["var"])
                        link(dve.tensor_copy(tok[i][:], x[i][:, TOK:TOK + 1]))
                    norm(0)
                    norm(1)
                    for i in range(PER):
                        if i + 2 < PER:
                            norm(i + 2)
                        h_turned(i)
                        finish(i)

                @block.scalar
                def _(act):
                    def x_turned(i):
                        u = i % 2
                        act.wait_ge(S["xT_ps"], i + 1)
                        if i >= 2:
                            act.wait_ge(S["h_ps"], 2 * (i - 1))
                        act.copy(xT0[u][:], G.ps[0][:, 0:TW])
                        act.copy(xT1[u][0:D1, :], G.ps[0][0:D1, TW:2 * TW]).then_inc(S["xT"], 1)

                    x_turned(0)
                    for i in range(PER):
                        if i + 1 < PER:
                            x_turned(i + 1)
                        u = i % 2
                        if i >= 2:
                            act.wait_ge(S["hT_ps"], i - 1)
                        for c in range(2):
                            act.wait_ge(S["h_ps"], 2 * i + c + 1)
                            act.activation(hs[u][:, c * FH:(c + 1) * FH], G.ps[2 + 2 * u + c][:, 0:FH],
                                           ACT.Gelu).then_inc(S["gelu"], 1)

                @block.tensor
                def _(pe):
                    ex = [None] * PER

                    def turn(i):
                        pe.wait_ge(S["xn"], i + 1)
                        if i:
                            pe.wait_ge(S["xT"], i)
                        pe.transpose(G.ps[0][:, 0:TW], xn[i][:, 0:D0], G.ident[:, :])
                        pe.transpose(G.ps[0][0:D1, TW:2 * TW], xn[i][:, D0:D], G.ident[:, :]).then_inc(S["xT_ps"], 1)

                    def first(i):
                        u = i % 2
                        ex[i] = pe.value_load(G.expert[0:1, bass.ds(it * PER + i, 1)], min_val=0, max_val=E - 1)
                        pe.wait_ge(S["xT"], i + 1)
                        if i >= 2:
                            pe.wait_ge(S["gelu"], 2 * (i - 1))
                        for c in range(2):
                            at = bass.ds(ex[i] * F + c * FH, FH)
                            pe.matmul(G.ps[2 + 2 * u + c][:, 0:FH], xT0[u][:], w1a[:, at], start=True, stop=False)
                            pe.matmul(G.ps[2 + 2 * u + c][:, 0:FH], xT1[u][:], w1b[:, at], start=False,
                                      stop=True).then_inc(S["h_ps"], 1)

                    def second(i):
                        u = i % 2
                        pe.wait_ge(S["gelu"], 2 * (i + 1))
                        if i:
                            pe.wait_ge(S["hT"], i)
                        for c in range(FT):
                            mm = pe.transpose(G.ps[6 + c // 4][:, (c % 4) * TW:(c % 4 + 1) * TW],
                                              hs[u][:, c * 128:(c + 1) * 128], G.ident[:, :])
                        mm.then_inc(S["hT_ps"], 1)
                        if i:
                            pe.wait_ge(S["out"], i)
                        pe.wait_ge(S["hT"], i + 1)
                        for c in range(FT):
                            pe.matmul(G.ps[1][:, 0:D], hT[u][:, c, :], w2[:, bass.ds(ex[i] * (FT * D) + c * D, D)],
                                      start=(c == 0), stop=False)
                        pe.matmul(G.ps[1][:, 0:D], G.ones[0:1, 0:TW], b2[:, bass.ds(ex[i] * D, D)], start=False,
                                  stop=True).then_inc(S["y_ps"], 1)

                    turn(0)
                    first(0)
                    for i in range(PER):
                        if i + 1 < PER:
                            turn(i + 1)
                            first(i + 1)
                        second(i)

                @block.gpsimd
                def _(pool):
                    for i in range(PER):
                        pool.wait_ge(S["var"], i + 1)
                        norm_rstd(pool, G, mv[i], TW, S["rstd"])
                    for i in range(PER):
                        pool.wait_ge(S["out"], i + 1)
                        pool.indirect_dma_start(dst, bass.IndirectOffsetOnAxis(tok[i][:].bitcast(U32), 0), o[i][:],
                                                None, bounds_check=NT - 1, oob_is_err=False).then_inc(G.rows_out[layer], 16)
                    pool.wait_ge(G.rows_out[layer], (it + 1) * (16 * PER))
            clear(nc, list(S.values()))


def reload_tokens(nc, G, src):
    with ExitStack() as ctx:
        sb, sem = allocator(nc, ctx)
        rows_in = sem("rows_back")
        with nc.Block() as block:
            @block.sync
            def _(sp):
                sp.dma_start(G.h[:, :, 0:D], src.rearrange("(b n) d -> n b d", n=N)).then_inc(rows_in, 16)
                sp.wait_ge(rows_in, 16)
        clear(nc, [rows_in])


def landmark_attention(nc, G, A):
    PAIRS = H // 2
    SPAN = LM + LR
    STEPS = 6
    ROOT = float(ZL) ** 0.5
    with ExitStack() as ctx:
        sb, sem = allocator(nc, ctx)
        names = ("var", "rstd", "xn", "xT_ps", "xT", "xl", "qk_ps", "mq", "kl", "s2_ps", "nm", "exp", "x", "col_ps",
                 "dve_chain", "setup", "weights_in",
                 "v", "mk", "s1_ps", "s3_ps", "s1_shift", "s1_exp", "s3_nm", "s3_exp", "p1", "p1T_ps", "p3T_ps",
                 "p1T", "p3T", "r_ps", "xr", "x_copy", "w0_ps", "wv", "w2_ps", "u", "z_ps", "t", "wv_ps", "a_ps", "b",
                 "zr", "o_ps", "o", "oT_ps", "oT", "y_ps", "yn", "yT_ps", "yT", "lg_ps", "red")
        S = {n: sem("l1_" + n) for n in names}
        wqkv0, wqkv1 = sb("l1_wqkv0", [D0, 3 * D]), sb("l1_wqkv1", [D1, 3 * D])
        wo0, wo1 = sb("l1_wo0", [D0, D]), sb("l1_wo1", [D1 + 1, D])
        sw0, sw1 = sb("l1_sw0", [D0, E]), sb("l1_sw1", [D1 + 1, E])
        head, rootw, colw, eye = sb("l1_head", [128, 8]), sb("l1_rootw", [128, 1]), sb("l1_colw", [128, 2]), \
            sb("l1_eye", [128, LR])
        qmask, kmask = sb("l1_qmask", [128, 8]), sb("l1_kmask", [128, 8])
        eye13, eye15 = sb("l1_eye13", [128, PAIRS, LR]), sb("l1_eye15", [128, PAIRS, LR])
        X = sb("l1_x", [128, B, PAIRS * LR])
        rowmax, colmax, most, cinv = sb("l1_rowmax", [128, PAIRS]), sb("l1_colmax", [2, PAIRS, LR]), \
            sb("l1_most", [128, 4]), sb("l1_cinv", [128, 1])
        T = []
        for s in range(2):
            t = {}
            for n, shape in (("st", [N, 6]), ("mv", [N, 3]), ("xn", [N, D]), ("xT0", [D0, N]), ("xT1", [D1, N]),
                             ("xl0", [D0, LR]), ("xl1", [D1, LR]), ("mq0", [128, 8, LM]), ("mq1", [64, 4, LM]),
                             ("kl0", [D0, LR]), ("kl1", [D1, LR]), ("nm", [128, PAIRS]), ("rs", [128, PAIRS]),
                             ("rt", [128, PAIRS]), ("q0", [D0, N]), ("q1", [D1, N]), ("k0", [D0, N]), ("k1", [D1, N]),
                             ("v", [N, D]), ("mk0", [128, 8, LR]), ("mk1", [64, 4, LR]), ("p1", [N, H, LM]),
                             ("nm1", [N, H]), ("rz1", [N, H]), ("p3", [128, PAIRS, N]), ("nm3", [128, PAIRS]),
                             ("rs3", [128, PAIRS]), ("e3", [128, PAIRS]), ("p1T", [128, PAIRS, N]),
                             ("p3T", [N, PAIRS, 128]), ("xr", [128, PAIRS, LM]), ("wv", [128, PAIRS, LM]),
                             ("u", [128, PAIRS, LR]), ("t", [128, PAIRS, LM]), ("b", [128, PAIRS, HD]),
                             ("zr", [128, PAIRS, 2 * HD]), ("o", [N, D]), ("oT0", [D0, N]), ("oT1", [D1 + 1, N])):
                t[n] = sb(f"l1_{n}_{s}", shape)
            T.append(t)
        with nc.Block() as block:
            @block.sync
            def _(sp):
                lots = ((wqkv0[:], A["wqkv"][0:D0]), (wqkv1[:], A["wqkv"][D0:D]), (wo0[:], A["wo"][0:D0]),
                        (wo1[:], A["wo"][D0:D + 1]), (sw0[:], A["sw"][0:D0]), (sw1[:], A["sw"][D0:D + 1]),
                        (head[:], A["head"]), (rootw[:], A["rootw"]), (colw[:], A["colw"]), (eye[:], A["eye"]))
                for dst, src in lots:
                    sp.dma_start(dst, src).then_inc(S["weights_in"], 16)

            @block.vector
            def _(dve):
                for s in range(2):
                    t = T[s]
                    for n in ("xl0", "xl1", "mq0", "mq1", "p1", "t", "zr"):
                        dve.memset(t[n][:], 0.0)
                    dve.memset(t["oT1"][D1:D1 + 1, :], 1.0)
                dve.memset(rowmax[:], 0.0)
                dve.memset(colmax[:], 0.0)
                dve.memset(most[:], 0.0)
                dve.wait_ge(S["weights_in"], 16 * 10)
                dve.tensor_scalar(qmask[:], head[:], SCALE / 2, None, ALU.mult)
                dve.tensor_scalar(kmask[:], head[:], 0.5, None, ALU.mult)
                over = eye[:].unsqueeze(1).broadcast_to([128, PAIRS, LR])
                dve.tensor_scalar(eye13[:], over, 13.0, None, ALU.mult)
                dve.tensor_scalar(eye15[:], over, 15.0, None, ALU.mult).then_inc(S["setup"], 1)
                dve.wait_ge(S["setup"], 1)
        clear(nc, list(S.values()))

        def hrow(it, s):
            return G.h[:, bass.ds(it * 2 + s, 1), 0:D].rearrange("p a d -> p (a d)")

        def turn(pe, src, bk):
            pe.transpose(bk[:, 0:N], src[:, 0:D0], G.ident[0:N, 0:N])
            return pe.transpose(bk[0:D1, 128:128 + N], src[:, D0:D], G.ident[0:N, 0:N])

        def turned(act, bk, o0, o1):
            act.copy(o0[:], bk[:, 0:N])
            return act.copy(o1[0:D1, :], bk[0:D1, 128:128 + N])

        def normed(dve, link, it):
            for s in range(2):
                norm_stats(dve, link, hrow(it, s), T[s]["st"], T[s]["mv"], N, S["var"])
            for s in range(2):
                dve.wait_ge(S["rstd"], s + 1)
                norm_apply(dve, hrow(it, s), T[s]["xn"][:], T[s]["mv"], N).then_inc(S["xn"], 1)

        def landmarks(dve):
            for s in range(2):
                t = T[s]
                dve.wait_ge(S["xT"], s + 1)
                for x, o in ((t["xT0"], t["xl0"]), (t["xT1"], t["xl1"])):
                    dve.tensor_copy(o[:, 0:1], x[:, 0:1])
                    two = x[:, 1:N].rearrange("p (j i) -> p i j", i=2)
                    last = dve.tensor_tensor(o[:, 1:LR - 1], two[:, 0, :], two[:, 1, :], ALU.add)
                last.then_inc(S["xl"], 1)

        def masked(dve, src, mask, out, rows, heads):
            return dve.tensor_tensor(out[:, :, 0:LR], src.unsqueeze(1).broadcast_to([rows, heads, LR]),
                                     mask[0:rows, 0:heads].unsqueeze(2).broadcast_to([rows, heads, LR]), ALU.mult)

        def landmark_rows(pe, t, bk, at, part):
            for m, (a, n) in enumerate(((0, D0), (D0, D1))):
                o = bk[0:n, at + m * LR:at + (m + 1) * LR]
                pe.matmul(o, wqkv0[:, part * D + a:part * D + a + n], t["xl0"][:], start=True, stop=False)
                last = pe.matmul(o, wqkv1[:, part * D + a:part * D + a + n], t["xl1"][:], start=False, stop=True)
            return last

        def pair_query(t, p):
            m = t["mq0"][:, 2 * p:2 * p + 2, :] if p < 4 else t["mq1"][:, 2 * p - 8:2 * p - 6, :]
            return m.rearrange("p a j -> p (a j)")

        with nc.Fori(0, B // 2) as it:
            with nc.Block() as block:
                @block.gpsimd
                def _(pool):
                    for s in range(2):
                        pool.wait_ge(S["var"], s + 1)
                        norm_rstd(pool, G, T[s]["mv"], N, S["rstd"])

                @block.vector
                def _(dve):
                    link = Chain(dve, S["dve_chain"])
                    normed(dve, link, it)
                    landmarks(dve)
                    for s in range(2):
                        t, bk = T[s], G.ps[4 * s + 1]
                        dve.wait_ge(S["qk_ps"], s + 1)
                        masked(dve, bk[:, 0:LR], qmask, t["mq0"], 128, 8)
                        masked(dve, bk[0:64, LR:2 * LR], qmask, t["mq1"], 64, 4)
                        dve.tensor_scalar(t["kl0"][:], bk[:, 2 * LR:3 * LR], 0.5, None, ALU.mult)
                        dve.tensor_scalar(t["kl1"][:], bk[0:64, 3 * LR:4 * LR], 0.5, None, ALU.mult)\
                           .then_inc(S["mq"], 1)
                    for s in range(2):
                        t, bk = T[s], G.ps[4 * s + 2]
                        dve.wait_ge(S["s2_ps"], s + 1)
                        dve.tensor_reduce(t["nm"][:], bk[:, 0:PAIRS * LR].rearrange("p (a j) -> p a j", j=LR), AX.X,
                                          ALU.max, negate=True).then_inc(S["nm"], 1)
                    for s in range(2):
                        t = T[s]
                        xe = t["u"]
                        dve.wait_ge(S["exp"], s + 1)
                        link(dve.scalar_tensor_tensor(t["rs"][:], xe[:, :, LR - 1], float(ZL - 1), t["rs"][:],
                                                      ALU.mult, ALU.add))
                        link(dve.reciprocal(t["rt"][:], t["rs"][:]))
                        link(dve.tensor_tensor(t["rs"][:], t["rs"][:], t["rt"][:], ALU.mult))
                        link(dve.tensor_tensor(rowmax[:], rowmax[:], t["rs"][:], ALU.max))
                        link(dve.tensor_scalar(t["rt"][:], t["rt"][:], rootw[:], None, ALU.mult))
                        link(dve.tensor_scalar(xe[:, :, LR - 1], xe[:, :, LR - 1], ROOT, None, ALU.mult))
                        row = X[:, bass.ds(it * 2 + s, 1), :].rearrange("p a (q j) -> p (a q) j", j=LR)
                        dve.tensor_tensor(row, xe[:], t["rt"][:].unsqueeze(2).broadcast_to([128, PAIRS, LR]),
                                          ALU.mult).then_inc(S["x"], 1)
                    for s in range(2):
                        dve.wait_ge(S["col_ps"], s + 1)
                        link(dve.tensor_tensor(colmax[:], colmax[:],
                                               G.ps[4 * s + 3][0:2, 0:PAIRS * LR].rearrange("p (a j) -> p a j", j=LR),
                                               ALU.max))

                @block.scalar
                def _(act):
                    for s in range(2):
                        act.wait_ge(S["xT_ps"], s + 1)
                        turned(act, G.ps[4 * s], T[s]["xT0"], T[s]["xT1"]).then_inc(S["xT"], 1)
                    for s in range(2):
                        t, bk = T[s], G.ps[4 * s + 2]
                        act.wait_ge(S["nm"], s + 1)
                        for p in range(PAIRS):
                            last = act.activation(t["u"][:, p, :], bk[:, p * LR:(p + 1) * LR], ACT.Exp,
                                                  bias=t["nm"][:, p:p + 1], accum_out=t["rs"][:, p:p + 1])
                        last.then_inc(S["exp"], 1)

                @block.tensor
                def _(pe):
                    for s in range(2):
                        pe.wait_ge(S["xn"], s + 1)
                        turn(pe, T[s]["xn"], G.ps[4 * s]).then_inc(S["xT_ps"], 1)
                    for s in range(2):
                        pe.wait_ge(S["xl"], s + 1)
                        landmark_rows(pe, T[s], G.ps[4 * s + 1], 0, 0)
                        landmark_rows(pe, T[s], G.ps[4 * s + 1], 2 * LR, 1).then_inc(S["qk_ps"], 1)
                    for s in range(2):
                        t, bk = T[s], G.ps[4 * s + 2]
                        pe.wait_ge(S["mq"], s + 1)
                        for p in range(PAIRS):
                            mm = pe.matmul(bk[:, p * LR:(p + 1) * LR], pair_query(t, p),
                                           (t["kl0"] if p < 4 else t["kl1"])[:], start=True, stop=True)
                        mm.then_inc(S["s2_ps"], 1)
                    for s in range(2):
                        pe.wait_ge(S["x"], s + 1)
                        row = X[:, bass.ds(it * 2 + s, 1), :].rearrange("p a q -> p (a q)")
                        pe.matmul(G.ps[4 * s + 3][0:2, 0:PAIRS * LR], colw[:], row, start=True,
                                  stop=True).then_inc(S["col_ps"], 1)
            clear(nc, list(S.values()))
        with nc.Block() as block:
            @block.vector
            def _(dve):
                link = Chain(dve, S["dve_chain"])
                link(dve.tensor_scalar(colmax[:, :, LR - 1], colmax[:, :, LR - 1], 1.0 / ROOT, None, ALU.mult))
                link(dve.tensor_reduce(most[0:2, 1:2], colmax[:].rearrange("p a j -> p (a j)"), AX.X, ALU.max))
                link(dve.tensor_reduce(most[:, 0:1], rowmax[:], AX.X, ALU.max))
                link(dve.tensor_reduce(cinv[:], colw[:], AX.X, ALU.add))
                link(dve.tensor_scalar(cinv[:], cinv[:], 0.0, None, ALU.is_gt))
                dve.tensor_tensor(most[:, 0:1], most[:, 0:1], cinv[:], ALU.mult).then_inc(S["setup"], 1)
                dve.wait_ge(S["red"], 1)
                link(dve.tensor_tensor(cinv[:], most[:, 2:3], most[:, 3:4], ALU.mult))
                link(dve.reciprocal(cinv[:], cinv[:]))

            @block.gpsimd
            def _(pool):
                pool.wait_ge(S["setup"], 1)
                pool.partition_all_reduce(most[:, 2:4], most[:, 0:2], 128, bass.bass_isa.ReduceOp.max)\
                    .then_inc(S["red"], 1)
        clear(nc, list(S.values()))

        halves = [(0, slice(0, LR), slice(0, LM)), (1, slice(LM, SPAN), slice(LM, 2 * LM))]

        def each_head(pe, lhs, rhs, out, width):
            for p in range(PAIRS):
                for _, k, m in halves:
                    last = pe.matmul(out[m, p * width:(p + 1) * width], lhs[k, p, :], rhs(k, p), start=True, stop=True)
            return last

        def tiles(bk, width):
            return bk[:, 0:PAIRS * width].rearrange("p (a j) -> p a j", j=width)

        with nc.Fori(0, B // 2) as it:
            with nc.Block() as block:
                @block.gpsimd
                def _(pool):
                    for k in range(2):
                        for s in range(2):
                            pool.wait_ge(S["var"], 2 * k + s + 1)
                            norm_rstd(pool, G, T[s]["mv"], N, S["rstd"])

                @block.vector
                def _(dve):
                    link = Chain(dve, S["dve_chain"])
                    normed(dve, link, it)
                    landmarks(dve)
                    for s in range(2):
                        t, bk = T[s], G.ps[4 * s + 2]
                        dve.wait_ge(S["qk_ps"], s + 1)
                        masked(dve, bk[:, D:D + LR], qmask, t["mq0"], 128, 8)
                        masked(dve, bk[0:64, D + LR:D + 2 * LR], qmask, t["mq1"], 64, 4)
                        masked(dve, bk[:, D + 2 * LR:D + 3 * LR], kmask, t["mk0"], 128, 8)
                        masked(dve, bk[0:64, D + 3 * LR:D + 4 * LR], kmask, t["mk1"], 64, 4).then_inc(S["mk"], 1)
                    for s in range(2):
                        t = T[s]
                        dve.wait_ge(S["s1_ps"], s + 1)
                        b0, b3 = tiles(G.ps[4 * s], LR), tiles(G.ps[4 * s + 3], LR)
                        b0 = G.ps[4 * s][0:N, 0:8 * LR].rearrange("p (a j) -> p a j", j=LR)
                        b3 = G.ps[4 * s + 3][0:N, 0:4 * LR].rearrange("p (a j) -> p a j", j=LR)
                        dve.tensor_reduce(t["nm1"][:, 0:8], b0, AX.X, ALU.max, negate=True)
                        link(dve.tensor_reduce(t["nm1"][:, 8:H], b3, AX.X, ALU.max, negate=True))
                        over = lambda a, b: t["nm1"][:, a:b].unsqueeze(2).broadcast_to([N, b - a, LR])
                        dve.tensor_tensor(t["p1"][:, 0:8, 0:LR], b0, over(0, 8), ALU.add)
                        dve.tensor_tensor(t["p1"][:, 8:H, 0:LR], b3, over(8, H), ALU.add).then_inc(S["s1_shift"], 1)
                    for s in range(2):
                        t = T[s]
                        dve.wait_ge(S["s3_ps"], s + 1)
                        for j in range(2):
                            link(dve.tensor_reduce(
                                t["nm3"][:, 3 * j:3 * j + 3],
                                G.ps[4 * s + 1 + j][:, 0:3 * N].rearrange("p (a n) -> p a n", n=N), AX.X, ALU.max,
                                negate=True))
                        dve.tensor_scalar(t["nm3"][:], t["nm3"][:], 0.0, None, ALU.min).then_inc(S["s3_nm"], 1)
                    for s in range(2):
                        t = T[s]
                        dve.wait_ge(S["s1_exp"], s + 1)
                        last = t["p1"][:, :, LR - 1]
                        link(dve.tensor_reduce(t["rz1"][:], t["p1"][:, :, 0:LR], AX.X, ALU.add))
                        link(dve.scalar_tensor_tensor(t["rz1"][:], last, float(ZL - 1), t["rz1"][:], ALU.mult, ALU.add))
                        link(dve.reciprocal(t["rz1"][:], t["rz1"][:]))
                        dve.tensor_scalar(last, last, ROOT, None, ALU.mult).then_inc(S["p1"], 1)
                    for s in range(2):
                        t = T[s]
                        dve.wait_ge(S["s3_exp"], s + 1)
                        link(dve.scalar_tensor_tensor(t["rs3"][:], t["e3"][:], float(PADS), t["rs3"][:], ALU.mult,
                                                      ALU.add))
                        link(dve.reciprocal(t["rs3"][:], t["rs3"][:]))
                        link(dve.tensor_scalar(t["rs3"][:], t["rs3"][:], rootw[:], None, ALU.mult))
                        dve.wait_ge(S["r_ps"], s + 1)
                        r = tiles(G.ps[4 * s], 2 * HD)
                        for i in range(2):
                            h = slice(LM * i, LM * i + LM)
                            last = dve.tensor_tensor(t["xr"][h, :, LR:LM], r[h, :, HD * i:HD * i + HD],
                                                     t["rs3"][h, :].unsqueeze(2).broadcast_to([LM, PAIRS, HD]), ALU.mult)
                        last.then_inc(S["xr"], 1)
                    for s in range(2):
                        dve.wait_ge(S["w0_ps"], s + 1)
                        dve.tensor_scalar(T[s]["wv"][:], tiles(G.ps[4 * s + 1], LM), cinv[:], None,
                                          ALU.mult).then_inc(S["wv"], 1)
                    for k in range(STEPS - 1):
                        for s in range(2):
                            t = T[s]
                            dve.wait_ge(S["wv"], 2 * k + s + 1)
                            link(dve.scalar_tensor_tensor(t["u"][:], t["wv"][:, :, 0:LR], -7.0, eye15[:], ALU.mult,
                                                          ALU.add))
                            dve.wait_ge(S["w2_ps"], 2 * k + s + 1)
                            dve.tensor_tensor(t["u"][:], t["u"][:], tiles(G.ps[4 * s + 2], LR),
                                              ALU.add).then_inc(S["u"], 1)
                        for s in range(2):
                            dve.wait_ge(S["z_ps"], 2 * k + s + 1)
                            dve.tensor_tensor(T[s]["t"][:, :, 0:LR], eye13[:], tiles(G.ps[4 * s + 3], LR),
                                              ALU.subtract).then_inc(S["t"], 1)
                        for s in range(2):
                            dve.wait_ge(S["wv_ps"], 2 * k + s + 1)
                            dve.tensor_scalar(T[s]["wv"][:], tiles(G.ps[4 * s + 1], LM), 0.25, None,
                                              ALU.mult).then_inc(S["wv"], 1)
                    for k, c in enumerate((7.0, 15.0)):
                        for s in range(2):
                            t = T[s]
                            if k == 0:
                                dve.wait_ge(S["wv"], 2 * (STEPS - 1) + s + 1)
                            dve.wait_ge(S["a_ps"], 2 * k + s + 1)
                            dve.scalar_tensor_tensor(t["b"][:], t["wv"][:, :, LR:LM], c, tiles(G.ps[4 * s + 2 + k], HD),
                                                     ALU.mult, ALU.subtract).then_inc(S["b"], 1)
                    for s in range(2):
                        t = T[s]
                        dve.wait_ge(S["a_ps"], 4 + s + 1)
                        link(dve.scalar_tensor_tensor(t["b"][:], t["wv"][:, :, LR:LM], 13.0, tiles(G.ps[4 * s + 1], HD),
                                                      ALU.mult, ALU.subtract))
                        for i, rows, _ in halves:
                            last = dve.tensor_scalar(t["zr"][rows, :, HD * i:HD * i + HD], t["b"][rows, :, :], 0.25,
                                                     None, ALU.mult)
                        last.then_inc(S["zr"], 1)
                    for s in range(2):
                        t = T[s]
                        dve.wait_ge(S["o_ps"], s + 1)
                        dve.tensor_tensor(t["o"][:].rearrange("p (h d) -> p h d", d=HD),
                                          G.ps[4 * s][0:N, 0:D].rearrange("p (h d) -> p h d", d=HD),
                                          t["rz1"][:].unsqueeze(2).broadcast_to([N, H, HD]), ALU.mult)\
                           .then_inc(S["o"], 1)
                    for s in range(2):
                        t = T[s]
                        dve.wait_ge(S["y_ps"], s + 1)
                        link(dve.tensor_tensor(hrow(it, s), hrow(it, s), G.ps[4 * s + 2][0:N, 0:D], ALU.add))
                        norm_stats(dve, link, hrow(it, s), t["st"], t["mv"], N, S["var"])
                    for s in range(2):
                        t = T[s]
                        dve.wait_ge(S["rstd"], 2 + s + 1)
                        norm_apply(dve, hrow(it, s), t["xn"][:], t["mv"], N).then_inc(S["yn"], 1)
                    for s in range(2):
                        dve.wait_ge(S["lg_ps"], s + 1)
                        dve.tensor_copy(G.lg[:, :, bass.ds(it * 2 + s, 1)], G.ps[4 * s][0:N, 0:E].unsqueeze(2))

                @block.scalar
                def _(act):
                    for s in range(2):
                        act.wait_ge(S["xT_ps"], s + 1)
                        turned(act, G.ps[4 * s], T[s]["xT0"], T[s]["xT1"]).then_inc(S["xT"], 1)
                    for s in range(2):
                        t, bk = T[s], G.ps[4 * s + 1]
                        act.wait_ge(S["qk_ps"], s + 1)
                        act.mul(t["q0"][:], bk[:, 0:N], SCALE)
                        act.mul(t["q1"][:], bk[0:D1, N:2 * N], SCALE)
                        act.copy(t["k0"][:], bk[:, 2 * N:3 * N])
                        act.copy(t["k1"][:], bk[0:D1, 3 * N:4 * N])
                        act.wait_ge(S["mk"], s + 1)
                        act.copy(t["v"][:], G.ps[4 * s + 2][0:N, 0:D]).then_inc(S["v"], 1)
                    for s in range(2):
                        t = T[s]
                        act.copy(t["xr"][:, :, 0:LR], X[:, bass.ds(it * 2 + s, 1), :]
                                 .rearrange("p a (q j) -> p (a q) j", j=LR)).then_inc(S["x_copy"], 1)
                    for s in range(2):
                        t = T[s]
                        act.wait_ge(S["s1_shift"], s + 1)
                        act.activation(t["p1"][:, :, 0:LR], t["p1"][:, :, 0:LR], ACT.Exp).then_inc(S["s1_exp"], 1)
                    for s in range(2):
                        t = T[s]
                        act.wait_ge(S["s3_nm"], s + 1)
                        for p in range(PAIRS):
                            act.activation(t["p3"][:, p, :], G.ps[4 * s + 1 + p // 3][:, (p % 3) * N:(p % 3 + 1) * N],
                                           ACT.Exp, bias=t["nm3"][:, p:p + 1], accum_out=t["rs3"][:, p:p + 1])
                        act.activation(t["e3"][:], t["nm3"][:], ACT.Exp).then_inc(S["s3_exp"], 1)
                    for s in range(2):
                        t = T[s]
                        act.wait_ge(S["p1T_ps"], s + 1)
                        act.copy(t["p1T"][:, 0:4, :], tiles4(G.ps[4 * s], 4, N))
                        act.copy(t["p1T"][:, 4:6, :], tiles4(G.ps[4 * s + 3], 2, N)).then_inc(S["p1T"], 1)
                    for s in range(2):
                        t = T[s]
                        act.wait_ge(S["p3T_ps"], s + 1)
                        act.copy(t["p3T"][:, 0:4, :], tiles4(G.ps[4 * s + 1], 4, 128)[0:N])
                        act.copy(t["p3T"][:, 4:6, :], tiles4(G.ps[4 * s + 2], 2, 128)[0:N]).then_inc(S["p3T"], 1)
                    for name, b in (("oT", 1), ("yT", 3)):
                        for s in range(2):
                            act.wait_ge(S[name + "_ps"], s + 1)
                            turned(act, G.ps[4 * s + b], T[s]["oT0"], T[s]["oT1"]).then_inc(S[name], 1)

                @block.tensor
                def _(pe):
                    for s in range(2):
                        pe.wait_ge(S["xn"], s + 1)
                        turn(pe, T[s]["xn"], G.ps[4 * s]).then_inc(S["xT_ps"], 1)
                    for s in range(2):
                        t, b1, b2 = T[s], G.ps[4 * s + 1], G.ps[4 * s + 2]
                        pe.wait_ge(S["xl"], s + 1)
                        for j in range(2):
                            for m, (a, n) in enumerate(((0, D0), (D0, D1))):
                                o = b1[0:n, (2 * j + m) * N:(2 * j + m + 1) * N]
                                pe.matmul(o, wqkv0[:, j * D + a:j * D + a + n], t["xT0"][:], start=True, stop=False)
                                pe.matmul(o, wqkv1[:, j * D + a:j * D + a + n], t["xT1"][:], start=False, stop=True)
                        pe.matmul(b2[0:N, 0:D], t["xT0"][:], wqkv0[:, 2 * D:3 * D], start=True, stop=False)
                        pe.matmul(b2[0:N, 0:D], t["xT1"][:], wqkv1[:, 2 * D:3 * D], start=False, stop=True)
                        landmark_rows(pe, t, b2, D, 0)
                        landmark_rows(pe, t, b2, D + 2 * LR, 1).then_inc(S["qk_ps"], 1)
                    for s in range(2):
                        t = T[s]
                        flat = lambda a: a[:].rearrange("p a j -> p (a j)")
                        pe.wait_ge(S["mk"], s + 1)
                        pe.wait_ge(S["v"], s + 1)
                        pe.matmul(G.ps[4 * s][0:N, 0:8 * LR], t["q0"][:], flat(t["mk0"]), start=True, stop=True)
                        pe.matmul(G.ps[4 * s + 3][0:N, 0:4 * LR], t["q1"][:], flat(t["mk1"]), start=True,
                                  stop=True).then_inc(S["s1_ps"], 1)
                        for p in range(PAIRS):
                            mm = pe.matmul(G.ps[4 * s + 1 + p // 3][:, (p % 3) * N:(p % 3 + 1) * N], pair_query(t, p),
                                           (t["k0"] if p < 4 else t["k1"])[:], start=True, stop=True)
                        mm.then_inc(S["s3_ps"], 1)
                    for s in range(2):
                        t = T[s]
                        pe.wait_ge(S["p1"], s + 1)
                        for p in range(PAIRS):
                            mm = pe.transpose(G.ps[4 * s + (0 if p < 4 else 3)][:, (p % 4) * N:(p % 4 + 1) * N],
                                              t["p1"][:, 2 * p:2 * p + 2, :].rearrange("p a j -> p (a j)"),
                                              G.ident[0:N, 0:N])
                        mm.then_inc(S["p1T_ps"], 1)
                    for s in range(2):
                        t = T[s]
                        pe.wait_ge(S["s3_exp"], s + 1)
                        for p in range(PAIRS):
                            mm = pe.transpose(G.ps[4 * s + 1 + p // 4][0:N, (p % 4) * 128:(p % 4 + 1) * 128],
                                              t["p3"][:, p, :], G.ident[:, :])
                        mm.then_inc(S["p3T_ps"], 1)
                    for s in range(2):
                        t = T[s]
                        pe.wait_ge(S["p1T"], s + 1)
                        pe.wait_ge(S["p3T"], s + 1)
                        for p in range(PAIRS):
                            mm = pe.matmul(G.ps[4 * s][:, p * 2 * HD:(p + 1) * 2 * HD], t["p3T"][:, p, :],
                                           t["v"][:, p * 2 * HD:(p + 1) * 2 * HD], start=True, stop=True)
                        mm.then_inc(S["r_ps"], 1)
                    for s in range(2):
                        t = T[s]
                        pe.wait_ge(S["x_copy"], s + 1)
                        pe.wait_ge(S["xr"], s + 1)
                        each_head(pe, t["xr"], lambda k, p: t["xr"][k, p, :], G.ps[4 * s + 1], LM)\
                            .then_inc(S["w0_ps"], 1)
                    for k_ in range(STEPS - 1):
                        for s in range(2):
                            t = T[s]
                            pe.wait_ge(S["wv"], 2 * k_ + s + 1)
                            each_head(pe, t["wv"], lambda k, p: t["wv"][k, p, 0:LR], G.ps[4 * s + 2], LR)\
                                .then_inc(S["w2_ps"], 1)
                        for s in range(2):
                            t = T[s]
                            pe.wait_ge(S["u"], 2 * k_ + s + 1)
                            each_head(pe, t["wv"], lambda k, p: t["u"][k, p, :], G.ps[4 * s + 3], LR)\
                                .then_inc(S["z_ps"], 1)
                        for s in range(2):
                            t = T[s]
                            pe.wait_ge(S["t"], 2 * k_ + s + 1)
                            each_head(pe, t["t"], lambda k, p: t["wv"][k, p, :], G.ps[4 * s + 1], LM)\
                                .then_inc(S["wv_ps"], 1)
                    for k_ in range(3):
                        for s in range(2):
                            t = T[s]
                            if k_ == 0:
                                pe.wait_ge(S["wv"], 2 * (STEPS - 1) + s + 1)
                                rhs = lambda k, p: t["wv"][k, p, LR:LM]
                            else:
                                pe.wait_ge(S["b"], 2 * (k_ - 1) + s + 1)
                                rhs = lambda k, p: t["b"][k, p, :]
                            each_head(pe, t["wv"], rhs, G.ps[4 * s + (2, 3, 1)[k_]], HD).then_inc(S["a_ps"], 1)
                    for s in range(2):
                        t = T[s]
                        pe.wait_ge(S["zr"], s + 1)
                        for p in range(PAIRS):
                            mm = pe.matmul(G.ps[4 * s][0:N, p * 2 * HD:(p + 1) * 2 * HD], t["p1T"][:, p, :],
                                           t["zr"][:, p, :], start=True, stop=True)
                        mm.then_inc(S["o_ps"], 1)
                    for s in range(2):
                        pe.wait_ge(S["o"], s + 1)
                        turn(pe, T[s]["o"], G.ps[4 * s + 1]).then_inc(S["oT_ps"], 1)
                    for s in range(2):
                        t, bk = T[s], G.ps[4 * s + 2]
                        pe.wait_ge(S["oT"], s + 1)
                        pe.matmul(bk[0:N, 0:D], t["oT0"][:], wo0[:], start=True, stop=False)
                        pe.matmul(bk[0:N, 0:D], t["oT1"][:], wo1[:], start=False, stop=True).then_inc(S["y_ps"], 1)
                    for s in range(2):
                        pe.wait_ge(S["yn"], s + 1)
                        turn(pe, T[s]["xn"], G.ps[4 * s + 3]).then_inc(S["yT_ps"], 1)
                    for s in range(2):
                        t, bk = T[s], G.ps[4 * s]
                        pe.wait_ge(S["yT"], s + 1)
                        pe.matmul(bk[0:N, 0:E], t["oT0"][:], sw0[:], start=True, stop=False)
                        pe.matmul(bk[0:N, 0:E], t["oT1"][:], sw1[:], start=False, stop=True).then_inc(S["lg_ps"], 1)
            clear(nc, list(S.values()))


def tiles4(bk, n, width):
    return bk[:, 0:n * width].rearrange("p (a j) -> p a j", j=width)


class Shared:
    pass


def build(nc, img, pw, plg, plb, pb, txt, a0, f0, a1, f1, out):
    h0 = nc.dram_tensor("h0", [B * NP_TOK, D], F32).ap()
    xs = [nc.dram_tensor(f"xs{i}", [SLOTS, HC], F32).ap() for i in range(2)]
    h2 = nc.dram_tensor("h2", [NT, D], F32).ap()
    with ExitStack() as ctx:
        sb, sem = allocator(nc, ctx)
        G = Shared()
        G.ps = [ctx.enter_context(nc.psum_tensor(f"bank{i}", [128, 512], F32)) for i in range(8)]
        G.ident, G.ones, G.before = sb("ident", [128, 128]), sb("ones", [128, 128]), sb("before", [128, 128])
        G.half = sb("minus_half", [128, 1])
        G.rows_sent = [sem(f"rows_sent{i}") for i in range(2)]
        G.rows_out = [sem(f"rows_out{i}") for i in range(2)]
        G.h = sb("h", [N, B, HC])
        G.lg = sb("logits", [N, E, B])
        G.expert = sb("expert", [1, BLOCKS], I32)
        set_a, set_b, set_c, zeroed = sem("set_a"), sem("set_b"), sem("set_c"), sem("zeroed")
        with ExitStack() as part1:
            empty = part1.enter_context(nc.sbuf_tensor("empty", [TW, BLOCKS, HC], F32))
            past_i = part1.enter_context(nc.sbuf_tensor("past", [TW, BLOCKS], I32))
            with nc.Block() as block:
                @block.vector
                def _(dve):
                    dve.memset(G.ones[:], 1.0).then_inc(set_a, 1)
                    dve.memset(G.half[:], -0.5)
                    dve.memset(G.h[:, :, D:HC], 0.0)
                    dve.memset(empty[:], 0.0).then_inc(set_a, 1)
                    dve.wait_ge(set_a, 2)
                    dve.wait_ge(set_b, 3)
                    dve.tensor_copy(empty[:, :, TOK], past_i[:]).then_inc(set_c, 1)

                @block.gpsimd
                def _(pool):
                    pool.iota(past_i[:], [[0, BLOCKS]], base=NT + 8, channel_multiplier=1).then_inc(set_b, 1)
                    pool.wait_ge(set_a, 1)
                    pool.affine_select(out=G.ident[:], in_=G.ones[:], compare_op=ALU.is_equal, fill=0.0, base=0,
                                       pattern=[[-1, 128]], channel_multiplier=1).then_inc(set_b, 1)
                    pool.affine_select(out=G.before[:], in_=G.ones[:], compare_op=ALU.is_gt, fill=0.0, base=0,
                                       pattern=[[1, 128]], channel_multiplier=-1).then_inc(set_b, 1)

                @block.sync
                def _(sp):
                    sp.wait_ge(set_c, 1)
                    for x in xs:
                        sp.dma_start(x.rearrange("(j p) c -> p j c", p=TW), empty[:]).then_inc(zeroed, 16)
                    sp.wait_ge(zeroed, 32)
            clear(nc, [set_a, set_b, set_c, zeroed])
        patch_embedding(nc, G, img, pw, plg, plb, pb, txt, h0)
        load_tokens(nc, G, h0, txt, None)
        talking_attention(nc, G, a0)
        route(nc, G, xs[0], 0)
        experts(nc, G, xs[0], h2, f0, 0)
        reload_tokens(nc, G, h2)
        landmark_attention(nc, G, a1)
        route(nc, G, xs[1], 1)
        experts(nc, G, xs[1], out, f1, 1)


def kernel(**inputs):
    import numpy as np
    import concourse.bacc as _bacc
    from concourse.bass_utils import run_bass_kernel_spmd as _run

    I = {k: np.ascontiguousarray(v) for k, v in inputs.items()}
    xp = np.pad(I["x"], ((0, 0), (0, 0), (1, 1), (1, 1)))
    c = slice(1, -1)
    shifts = [xp[:, :, c, c], xp[:, :, c, :-2], xp[:, :, c, 2:], xp[:, :, :-2, c], xp[:, :, 2:, c]]
    xc = np.concatenate(shifts, axis=1).reshape(B, VAR_CH, GRID, PATCH, IMG)
    img = np.ascontiguousarray(xc.transpose(1, 3, 0, 2, 4)).reshape(VAR_CH * PATCH, B * GRID * IMG)
    feat = lambda a: np.ascontiguousarray(a.reshape(PATCH, PATCH, VAR_CH, -1).transpose(2, 0, 1, 3))
    rootw = np.tile(np.where(np.arange(LM) == LR - 1, ZL ** 0.5, 1.0), 2).astype(np.float32)
    real = np.tile(np.arange(LM) < LR, 2)
    a = {
        "img": img,
        "pw": feat(I["L0_tok_w"]).reshape(VAR_CH * PATCH, PATCH, D),
        "plg": feat(I["L0_tok_ln_gamma"]).reshape(VAR_CH * PATCH, PATCH),
        "plb": feat(I["L0_tok_ln_beta"]).reshape(VAR_CH * PATCH, PATCH),
        "pb": I["L0_tok_b"][None],
        "txt": I["txt"],
        "a0_wqkv": I["L0_attn_qkv_w"].T,
        "a0_wl": np.repeat(I["L0_attn_proj_l_w"].T, HD, axis=0),
        "a0_lb": I["L0_attn_proj_l_b"][None],
        "a0_ww": np.concatenate([np.repeat(I["L0_attn_proj_w_w"].T, HD, axis=1),
                                 np.repeat(I["L0_attn_proj_w_b"], HD)[None]]).reshape(1, -1),
        "a0_lamb": np.repeat(I["L0_attn_lamb"], HD)[None],
        "a0_wo": np.concatenate([I["L0_attn_proj_out_w"].T, I["L0_attn_proj_out_b"][None]]),
        "a0_sw": np.concatenate([I["L0_ffn_switch_w"], I["L0_ffn_switch_b"][None]]),
        "f0_w1": np.concatenate([I["L0_ffn_w1"], I["L0_ffn_b1"][:, None]], axis=1),
        "f0_w2": I["L0_ffn_w2"],
        "f0_b2": I["L0_ffn_b2"].reshape(1, -1),
        "a1_wqkv": I["L1_attn_w_qkv"].T,
        "a1_wo": np.concatenate([I["L1_attn_w_proj"].T, I["L1_attn_b_proj"][None]]),
        "a1_head": np.kron(np.eye(8), np.ones((HD, 1))).astype(np.float32),
        "a1_rootw": rootw.reshape(-1, 1),
        "a1_colw": (np.kron(np.eye(2), np.ones((LM, 1))) * (rootw * real).reshape(-1, 1)).astype(np.float32),
        "a1_eye": np.tile(np.eye(LM, LR, dtype=np.float32), (2, 1)),
        "a1_sw": np.concatenate([I["L1_ffn_gate_w"], I["L1_ffn_gate_b"][None]]),
        "f1_w1": np.concatenate([I["L1_ffn_w1"], I["L1_ffn_b1"][:, None]], axis=1),
        "f1_w2": I["L1_ffn_w2"],
        "f1_b2": I["L1_ffn_b2"].reshape(1, -1),
    }
    nc = _bacc.Bacc("TRN2", target_bir_lowering=False, num_devices=1)
    arrays, t = {}, {}
    for k, v in a.items():
        v = np.ascontiguousarray(v)
        arrays[k] = v
        t[k] = nc.dram_tensor(k, v.shape, mybir.dt.from_np(v.dtype), kind="ExternalInput").ap()
    out = nc.dram_tensor("out", (NT, D), F32, kind="ExternalOutput").ap()
    sub = lambda p: {k[3:]: v for k, v in t.items() if k.startswith(p + "_")}
    build(nc, t["img"], t["pw"], t["plg"], t["plb"], t["pb"], t["txt"], sub("a0"), sub("f0"), sub("a1"), sub("f1"),
          out)
    r = _run(nc, [arrays], core_ids=[0])
    return r.results[0]["out"].reshape(B, N, D)
```

```python
from contextlib import ExitStack

import concourse.bass as bass
from concourse import mybir

F32 = mybir.dt.float32
I32 = mybir.dt.int32
U32 = mybir.dt.uint32
ALU = mybir.AluOpType
ACT = mybir.ActivationFunctionType
AX = mybir.AxisListType

B, CH, IMG, PATCH = 64, 3, 64, 16
GRID = IMG // PATCH
NP_TOK = GRID * GRID
TXT = 77
N = NP_TOK + TXT
NT = B * N
D = 192
D0, D1 = 128, D - 128
H, HD = 12, 16
SCALE = HD ** -0.5
EPS = 1e-5
VAR_CH = 5 * CH
PD = PATCH * PATCH * VAR_CH
KA = 128
KB = VAR_CH * PATCH - KA
E, F = 8, 768
CAP = int(1.25 * NT / E)
LM = 64
PADS = (-N) % LM
NP = N + PADS
ZL = PADS // 2
LR = LM - ZL + 1
TW = 128
BLOCKS = (NT + E * (TW - 1)) // TW
SLOTS = BLOCKS * TW
HC = 196
GATE, KEEP, TOK = 192, 193, 194
SL = 4
MC = 8
FH = F // 2
FT = F // 128


def clear(nc, sems):
    nums = sorted(s.num for s in sems)
    cuts = [0] + [i for i in range(1, len(nums)) if nums[i] != nums[i - 1] + 1] + [len(nums)]
    runs = [range(nums[a], nums[b - 1] + 1) for a, b in zip(cuts, cuts[1:])]
    for run in runs[1:]:
        nc.gpsimd.sem_clear(run)
    nc.all_engine_barrier(sems_to_clear=runs[0])


class Chain:

    def __init__(self, eng, sem):
        self.eng, self.sem, self.n = eng, sem, 0

    def __call__(self, ins):
        self.n += 1
        ins.then_inc(self.sem, 1)
        self.eng.wait_ge(self.sem, self.n)


def norm_stats(dve, link, x, st, mv, rows, done):
    link(dve.bn_stats(st[0:rows, :], x))
    link(dve.bn_aggr(mv[0:rows, 0:2], st[0:rows, :]))
    dve.tensor_scalar(mv[0:rows, 1:2], mv[0:rows, 1:2], EPS, None, ALU.add).then_inc(done, 1)


def norm_rstd(pool, G, mv, rows, done):
    pool.tensor_tensor(mv[0:rows, 2:3], mv[0:rows, 1:2], G.half[0:rows, :], ALU.pow).then_inc(done, 1)


def norm_apply(dve, x, out, mv, rows):
    return dve.tensor_scalar(out, x, mv[0:rows, 0:1], mv[0:rows, 2:3], ALU.subtract, ALU.mult)


def turn(pe, G, src, bk):
    pe.transpose(bk[:, 0:N], src[:, 0:D0], G.ident[0:N, 0:N])
    return pe.transpose(bk[0:D1, 128:128 + N], src[:, D0:D], G.ident[0:N, 0:N])


def turned(act, bk, o0, o1):
    act.copy(o0[:], bk[:, 0:N])
    return act.copy(o1[0:D1, :], bk[0:D1, 128:128 + N])


def queries_keys_values(pe, w0, w1, t, qk, v):
    for m, (a, n) in enumerate(((0, D0), (D0, D1))):
        for j in range(2):
            o = qk[0:n, (2 * m + j) * N:(2 * m + j + 1) * N]
            pe.matmul(o, w0[:, j * D + a:j * D + a + n], t["xT0"][:], start=True, stop=False)
            pe.matmul(o, w1[:, j * D + a:j * D + a + n], t["xT1"][:], start=False, stop=True)
    pe.matmul(v[0:N, 0:D], t["xT0"][:], w0[:, 2 * D:3 * D], start=True, stop=False)
    return pe.matmul(v[0:N, 0:D], t["xT1"][:], w1[:, 2 * D:3 * D], start=False, stop=True)


def allocator(nc, ctx):
    def sb(name, shape, dt=F32):
        return ctx.enter_context(nc.sbuf_tensor(name, shape, dt))

    def sem(name):
        return ctx.enter_context(nc.semaphore(name))
    return sb, sem


def patch_embedding(nc, G, img, w_dram, lg_dram, lb_dram, b_dram, txt, h0):
    NG, GB = B // 8, 8
    PER = 4
    with ExitStack() as ctx:
        sb, sem = allocator(nc, ctx)
        wa, wb = sb("pe_wa", [KA, PATCH, D]), sb("pe_wb", [KB, PATCH, D])
        ga, gb = sb("pe_ga", [KA, PATCH]), sb("pe_gb", [KB, PATCH])
        ba, bb = sb("pe_ba", [KA, PATCH]), sb("pe_bb", [KB, PATCH])
        wga, wgb = sb("pe_wga", [KA, PATCH, D + 1]), sb("pe_wgb", [KB, PATCH, D + 1])
        suma, sumb = sb("pe_suma", [KA, 2, D + 1]), sb("pe_sumb", [KB, 2, D + 1])
        bias = sb("pe_bias", [1, D])
        gsum, csum = sb("pe_gsum", [128, D + 1]), sb("pe_csum", [128, D])
        xa = [sb(f"pe_xa{i}", [KA, GB * GRID * IMG]) for i in range(PER)]
        xb = [sb(f"pe_xb{i}", [KB, GB * GRID * IMG]) for i in range(PER)]
        sq = sb("pe_sq", [128, GB * GRID * IMG])
        sqa = [sb(f"pe_sqa{i}", [KA, 128]) for i in range(PER)]
        sqb = [sb(f"pe_sqb{i}", [KB, 128]) for i in range(PER)]
        mom = [sb(f"pe_mom{i}", [128, 8]) for i in range(PER)]
        ho = [sb(f"pe_ho{i}", [128, D]) for i in range(PER)]
        loaded, scaled, wsum, ones_ps, acted = (sem(f"pe_{n}") for n in ("loaded", "scaled", "wsum", "ones_ps", "csum"))
        pre = [loaded, scaled, wsum, ones_ps, acted]
        chain = sem("pe_chain")
        pre.append(chain)
        sq_done, sq_summed, acc_ps, var_done, rstd_done, h_done, stored = (
            sem(f"pe_{n}") for n in ("sq_done", "sq_summed", "acc_ps", "var_done", "rstd_done", "h_done", "stored"))
        img_in = [sem(f"pe_img_in{i}") for i in range(PER)]
        body = [sq_done, sq_summed, acc_ps, var_done, rstd_done, h_done, stored] + img_in
        with nc.Block() as block:
            @block.sync
            def _(sp):
                for dst, src in ((wa, w_dram[0:KA]), (wb, w_dram[KA:KA + KB]), (ga, lg_dram[0:KA]),
                                 (gb, lg_dram[KA:KA + KB]), (ba, lb_dram[0:KA]), (bb, lb_dram[KA:KA + KB])):
                    sp.dma_start(dst[:], src).then_inc(loaded, 16)
                sp.dma_start(bias[:], b_dram).then_inc(loaded, 16)

            @block.vector
            def _(dve):
                link = Chain(dve, chain)
                dve.wait_ge(loaded, 16 * 7)
                link(dve.memset(wga[:, :, D:D + 1], 1.0))
                link(dve.memset(wgb[:, :, D:D + 1], 1.0))
                for w, g, o, k, be, s in ((wa, ga, wga, KA, ba, suma), (wb, gb, wgb, KB, bb, sumb)):
                    link(dve.tensor_tensor(o[:, :, 0:D], w[:], g[:].unsqueeze(2).broadcast_to([k, PATCH, D]), ALU.mult))
                    link(dve.tensor_reduce(s[:, 0, :], o[:].rearrange("p f e -> p e f"), AX.X, ALU.add))
                    link(dve.tensor_tensor(w[:], w[:], be[:].unsqueeze(2).broadcast_to([k, PATCH, D]), ALU.mult))
                    link(dve.tensor_reduce(s[:, 1, 0:D], w[:].rearrange("p f e -> p e f"), AX.X, ALU.add))
                dve.tensor_copy(mom[0][:, 7:8], G.ones[:, 0:1]).then_inc(scaled, 1)
                dve.wait_ge(ones_ps, 1)
                dve.tensor_copy(gsum[:], G.ps[0][:, 0:D + 1])
                dve.tensor_copy(csum[:], G.ps[1][:, 0:D]).then_inc(acted, 1)
                dve.wait_ge(acted, 1)

            @block.tensor
            def _(pe):
                pe.wait_ge(scaled, 1)
                pe.matmul(G.ps[0][:, 0:D + 1], G.ones[0:KA, :], suma[:, 0, :], start=True, stop=False)
                pe.matmul(G.ps[0][:, 0:D + 1], G.ones[0:KB, :], sumb[:, 0, :], start=False, stop=True)
                pe.matmul(G.ps[1][:, 0:D], G.ones[0:KA, :], suma[:, 1, 0:D], start=True, stop=False)
                pe.matmul(G.ps[1][:, 0:D], G.ones[0:KB, :], sumb[:, 1, 0:D], start=False, stop=False)
                pe.matmul(G.ps[1][:, 0:D], G.ones[0:1, :], bias[:], start=False, stop=True).then_inc(ones_ps, 1)
        clear(nc, pre)
        with nc.Fori(0, NG // PER) as it:
            with nc.Block() as block:
                @block.sync
                def _(sp):
                    for s in range(PER):
                        at = bass.ds((it * PER + s) * (GB * GRID * IMG), GB * GRID * IMG)
                        sp.dma_start(xa[s][:], img[0:KA, at]).then_inc(img_in[s], 16)
                        sp.dma_start(xb[s][:], img[KA:KA + KB, at]).then_inc(img_in[s], 16)
                    for s in range(PER):
                        sp.wait_ge(h_done, s + 1)
                        sp.dma_start(h0[bass.ds((it * PER + s) * 128, 128), :], ho[s][:]).then_inc(stored, 16)
                    sp.wait_ge(stored, 16 * PER)

                @block.scalar
                def _(act):
                    for s in range(PER):
                        act.wait_ge(img_in[s], 32)
                        for t, (x, k) in enumerate(((xa[s], KA), (xb[s], KB))):
                            if s or t:
                                act.wait_ge(sq_summed, 2 * s + t)
                            act.activation(sq[0:k, :], x[:], ACT.Square).then_inc(sq_done, 1)

                @block.vector
                def _(dve):
                    link = Chain(dve, chain)
                    for s in range(PER):
                        for t, (o, k) in enumerate(((sqa[s], KA), (sqb[s], KB))):
                            dve.wait_ge(sq_done, 2 * s + t + 1)
                            dve.tensor_reduce(o[:], sq[0:k, :].rearrange("p (t f) -> p t f", f=PATCH), AX.X,
                                              ALU.add).then_inc(sq_summed, 1)
                        m, acc = mom[s], G.ps[s]
                        dve.wait_ge(acc_ps, s + 1)
                        link(dve.tensor_scalar(m[:, 0:1], acc[:, D:D + 1], 1.0 / PD, None, ALU.mult))
                        link(dve.tensor_tensor(m[:, 1:2], m[:, 0:1], m[:, 0:1], ALU.mult))
                        link(dve.tensor_scalar(m[:, 2:3], G.ps[4 + s][:, 0:1], 1.0 / PD, m[:, 1:2], ALU.mult, ALU.subtract))
                        link(dve.tensor_scalar(m[:, 2:3], m[:, 2:3], EPS, None, ALU.add))
                        dve.tensor_scalar(m[:, 4:5], m[:, 0:1], -1.0, None, ALU.mult).then_inc(var_done, 1)
                        dve.wait_ge(var_done, s + 1)
                        link(dve.scalar_tensor_tensor(ho[s][:], gsum[:, 0:D], m[:, 4:5], acc[:, 0:D], ALU.mult, ALU.add))
                        dve.wait_ge(rstd_done, s + 1)
                        dve.scalar_tensor_tensor(ho[s][:], ho[s][:], m[:, 3:4], csum[:], ALU.mult,
                                                 ALU.add).then_inc(h_done, 1)

                @block.gpsimd
                def _(pool):
                    for s in range(PER):
                        pool.wait_ge(var_done, s + 1)
                        pool.tensor_tensor(mom[s][:, 3:4], mom[s][:, 2:3], G.half[:], ALU.pow).then_inc(rstd_done, 1)

                @block.tensor
                def _(pe):
                    for s in range(PER):
                        pe.wait_ge(img_in[s], 32)
                        va = xa[s][:].rearrange("p (t f) -> p f t", f=PATCH)
                        vb = xb[s][:].rearrange("p (t f) -> p f t", f=PATCH)
                        for f in range(PATCH):
                            pe.matmul(G.ps[s][:, 0:D + 1], va[:, f, :], wga[:, f, :], start=(f == 0), stop=False)
                            pe.matmul(G.ps[s][:, 0:D + 1], vb[:, f, :], wgb[:, f, :], start=False,
                                      stop=(f == PATCH - 1))
                        pe.wait_ge(sq_summed, 2 * s + 2)
                        pe.matmul(G.ps[4 + s][:, 0:1], sqa[s][:], G.ones[0:KA, 0:1], start=True, stop=False)
                        pe.matmul(G.ps[4 + s][:, 0:1], sqb[s][:], G.ones[0:KB, 0:1], start=False,
                                  stop=True).then_inc(acc_ps, 1)
            clear(nc, [chain] + body)


def load_tokens(nc, G, h0, txt, weights):
    with ExitStack() as ctx:
        sb, sem = allocator(nc, ctx)
        rows_in = sem("rows_in")
        with nc.Block() as block:
            @block.sync
            def _(sp):
                h = G.h[:]
                sp.dma_start(h[0:NP_TOK, :, 0:D], h0.rearrange("(b n) d -> n b d", n=NP_TOK)).then_inc(rows_in, 16)
                sp.dma_start(h[NP_TOK:N, :, 0:D], txt.rearrange("b n d -> n b d")).then_inc(rows_in, 16)
                sp.wait_ge(rows_in, 32)
        clear(nc, [rows_in])


def talking_attention(nc, G, A):
    NC = -(-N // MC)
    NM = NC * MC
    R = H * MC
    GROUPS = ((0, 5), (5, 10), (10, 12))
    assert NC == H
    with ExitStack() as ctx:
        sb, sem = allocator(nc, ctx)
        names = ("var", "rstd", "xn", "xT_ps", "xT", "qkv_ps", "qk", "v", "qs0", "qs1", "s_ps", "negmax", "exp", "p",
                 "c_ps", "c", "m_ps", "m", "aT_ps", "aT", "u_ps", "u", "r_ps", "o", "oT_ps", "oT", "y_ps", "yn",
                 "yT_ps", "yT", "lg_ps", "dve_chain", "weights_in", "ready")
        S = {n: sem("l0_" + n) for n in names}
        wqkv0, wqkv1 = sb("l0_wqkv0", [D0, 3 * D]), sb("l0_wqkv1", [D1, 3 * D])
        wl0, wl1 = sb("l0_wl0", [D0, H]), sb("l0_wl1", [D1, H])
        lbias = sb("l0_lbias", [D1 + 1, H])
        mix = sb("l0_mixs", [R + 1, R])
        lam = sb("l0_lam", [N, D])
        c1, c2 = sb("l0_c1", [N, D]), sb("l0_c2", [N, D])
        wo0, wo1 = sb("l0_wo0", [D0, D]), sb("l0_wo1", [D1 + 1, D])
        sw0, sw1 = sb("l0_sw0", [D0, E]), sb("l0_sw1", [D1 + 1, E])
        T = []
        for s in range(SL):
            t = {}
            for n, shape in (("st", [N, 6]), ("mv", [N, 3]), ("xn", [N, D]), ("xT0", [D0, N]), ("xT1", [D1, N]),
                             ("qk0", [D0, 2, N]), ("qk1", [D1 + 1, 2, N]), ("v", [N, D]),
                             ("qs0", [D0, H, N]), ("qs1", [D1 + 1, H, N]), ("nm", [N, H]), ("rs", [N, H]),
                             ("p", [N, H, NM]), ("c", [R + 1, NC, N]), ("m", [N, H, NM]), ("aT", [NM, H, N]),
                             ("u", [N, D]), ("o", [N, D]), ("oT0", [D0, N]), ("oT1", [D1 + 1, N])):
                t[n] = sb(f"l0_{n}_{s}", shape)
            T.append(t)
        with nc.Block() as block:
            @block.sync
            def _(sp):
                lots = ((wqkv0[:], A["wqkv"][0:D0]), (wqkv1[:], A["wqkv"][D0:D]), (wl0[:], A["wl"][0:D0]),
                        (wl1[:], A["wl"][D0:D]), (lbias[D1:D1 + 1, :], A["lb"]), (mix[:], A["mix"]),
                        (lam[:], A["lamb"].broadcast_to([N, D])),
                        (wo0[:], A["wo"][0:D0]), (wo1[:], A["wo"][D0:D + 1]),
                        (sw0[:], A["sw"][0:D0]), (sw1[:], A["sw"][D0:D + 1]))
                for dst, src in lots:
                    sp.dma_start(dst, src).then_inc(S["weights_in"], 16)

            @block.vector
            def _(dve):
                for s in range(SL):
                    t = T[s]
                    dve.memset(t["qk1"][D1:D1 + 1, :, :], 1.0)
                    dve.memset(t["oT1"][D1:D1 + 1, :], 1.0)
                    dve.memset(t["c"][R:R + 1, :, :], 1.0)
                    dve.memset(t["p"][:, :, N:NM], 0.0)
                dve.wait_ge(S["weights_in"], 16 * 11)
                dve.tensor_scalar(c1[:], lam[:], -2.0, 1.0, ALU.mult, ALU.add)
                dve.tensor_scalar(c2[:], lam[:], 3.0, None, ALU.mult)
                dve.tensor_scalar(wqkv0[:, 0:D], wqkv0[:, 0:D], SCALE, None, ALU.mult)
                dve.tensor_scalar(wqkv1[:, 0:D], wqkv1[:, 0:D], SCALE, None, ALU.mult)
                for s in range(SL):
                    last = dve.tensor_copy(T[s]["qs1"][D1:D1 + 1, :, :],
                                           lbias[D1:D1 + 1, :].unsqueeze(2).broadcast_to([1, H, N]))
                last.then_inc(S["ready"], 1)
                dve.wait_ge(S["ready"], 1)
        clear(nc, list(S.values()))
        with nc.Fori(0, B // SL) as it:
            hrow = [G.h[:, bass.ds(it * SL + s, 1), 0:D].rearrange("p a d -> p (a d)") for s in range(SL)]
            b0, b1 = [G.ps[2 * s] for s in range(SL)], [G.ps[2 * s + 1] for s in range(SL)]
            with nc.Block() as block:
                @block.vector
                def _(dve):
                    link = Chain(dve, S["dve_chain"])
                    for s in range(SL):
                        norm_stats(dve, link, hrow[s], T[s]["st"], T[s]["mv"], N, S["var"])
                    for s in range(SL):
                        dve.wait_ge(S["rstd"], s + 1)
                        norm_apply(dve, hrow[s], T[s]["xn"][:], T[s]["mv"], N).then_inc(S["xn"], 1)
                    for s in range(SL):
                        t = T[s]
                        dve.wait_ge(S["qk"], s + 1)
                        dve.tensor_tensor(t["qs0"][:], t["qk0"][:, 0, :].unsqueeze(1).broadcast_to([D0, H, N]),
                                          wl0[:].unsqueeze(2).broadcast_to([D0, H, N]), ALU.mult).then_inc(S["qs0"], 1)
                    for j in range(3):
                        for s in range(SL):
                            bk = (b0, b1, b0)[j][s]
                            dve.wait_ge(S["s_ps"], SL * j + s + 1)
                            dve.tensor_reduce(T[s]["nm"][:, 4 * j:4 * j + 4],
                                              bk[0:N, 0:4 * N].rearrange("p (g m) -> p g m", m=N), AX.X,
                                              ALU.max, negate=True).then_inc(S["negmax"], 1)
                    for s in range(SL):
                        t = T[s]
                        dve.wait_ge(S["exp"], 2 * SL + s + 1)
                        link(dve.reciprocal(t["rs"][:], t["rs"][:]))
                        dve.tensor_tensor(t["p"][:, :, 0:N], t["p"][:, :, 0:N],
                                          t["rs"][:].unsqueeze(2).broadcast_to([N, H, N]), ALU.mult).then_inc(S["p"], 1)
                    for j, (a, b) in enumerate(GROUPS):
                        for s in range(SL):
                            dve.wait_ge(S["m_ps"], SL * j + s + 1)
                            dve.tensor_copy(T[s]["m"][:].rearrange("p h (m c) -> p c (h m)", c=NC)[:, a:b, :],
                                            (b1, b0, b1)[j][s][0:N, 0:(b - a) * R]
                                            .rearrange("p (c r) -> p c r", r=R)).then_inc(S["m"], 1)
                    for s in range(SL):
                        dve.wait_ge(S["u_ps"], s + 1)
                        dve.tensor_copy(T[s]["u"][:], b1[s][0:N, 0:D]).then_inc(S["u"], 1)
                    for s in range(SL):
                        t = T[s]
                        dve.wait_ge(S["u"], s + 1)
                        link(dve.tensor_tensor(t["o"][:], t["u"][:], c1[:], ALU.mult))
                        dve.wait_ge(S["r_ps"], s + 1)
                        link(dve.tensor_tensor(t["u"][:], b0[s][0:N, 0:D], c2[:], ALU.mult))
                        dve.tensor_tensor(t["o"][:], t["o"][:], t["u"][:], ALU.add).then_inc(S["o"], 1)
                    for s in range(SL):
                        t = T[s]
                        dve.wait_ge(S["y_ps"], s + 1)
                        link(dve.tensor_tensor(hrow[s], hrow[s], b0[s][0:N, 0:D], ALU.add))
                        norm_stats(dve, link, hrow[s], t["st"], t["mv"], N, S["var"])
                    for s in range(SL):
                        t = T[s]
                        dve.wait_ge(S["rstd"], SL + s + 1)
                        norm_apply(dve, hrow[s], t["xn"][:], t["mv"], N).then_inc(S["yn"], 1)
                    for s in range(SL):
                        dve.wait_ge(S["lg_ps"], s + 1)
                        dve.tensor_copy(G.lg[:, :, bass.ds(it * SL + s, 1)], b0[s][0:N, 0:E].unsqueeze(2))

                @block.gpsimd
                def _(pool):
                    for s in range(SL):
                        pool.wait_ge(S["var"], s + 1)
                        norm_rstd(pool, G, T[s]["mv"], N, S["rstd"])
                    for s in range(SL):
                        t = T[s]
                        pool.wait_ge(S["qk"], s + 1)
                        pool.tensor_tensor(t["qs1"][0:D1, :, :],
                                           t["qk1"][0:D1, 0, :].unsqueeze(1).broadcast_to([D1, H, N]),
                                           wl1[:].unsqueeze(2).broadcast_to([D1, H, N]), ALU.mult).then_inc(S["qs1"], 1)
                    for s in range(SL):
                        pool.wait_ge(S["var"], SL + s + 1)
                        norm_rstd(pool, G, T[s]["mv"], N, S["rstd"])

                @block.scalar
                def _(act):
                    for s in range(SL):
                        act.wait_ge(S["xT_ps"], s + 1)
                        turned(act, b0[s], T[s]["xT0"], T[s]["xT1"]).then_inc(S["xT"], 1)
                    for s in range(SL):
                        t = T[s]
                        act.wait_ge(S["qkv_ps"], s + 1)
                        act.copy(t["qk0"][:].rearrange("p a n -> p (a n)"), b1[s][:, 0:2 * N])
                        act.copy(t["qk1"][0:D1, :, :].rearrange("p a n -> p (a n)"),
                                 b1[s][0:D1, 2 * N:4 * N]).then_inc(S["qk"], 1)
                        act.copy(t["v"][:], b0[s][0:N, 0:D]).then_inc(S["v"], 1)
                    for j in range(3):
                        for s in range(SL):
                            t, bk = T[s], (b0, b1, b0)[j][s]
                            act.wait_ge(S["negmax"], SL * j + s + 1)
                            for g in range(4 * j, 4 * j + 4):
                                last = act.activation(t["p"][:, g, 0:N], bk[0:N, (g % 4) * N:(g % 4 + 1) * N],
                                                      ACT.Exp, bias=t["nm"][:, g:g + 1], accum_out=t["rs"][:, g:g + 1])
                            last.then_inc(S["exp"], 1)
                    for j, (a, b) in enumerate(GROUPS):
                        for s in range(SL):
                            act.wait_ge(S["c_ps"], SL * j + s + 1)
                            act.copy(T[s]["c"][0:R, a:b, :].rearrange("p c n -> p (c n)"),
                                     (b1, b0, b1)[j][s][0:R, 0:(b - a) * N]).then_inc(S["c"], 1)
                    for j, (a, b) in enumerate(GROUPS):
                        for s in range(SL):
                            act.wait_ge(S["aT_ps"], SL * j + s + 1)
                            act.copy(T[s]["aT"][:, a:b, :].rearrange("p c n -> p (c n)"),
                                     (b0, b1, b0)[j][s][0:NM, 0:(b - a) * N]).then_inc(S["aT"], 1)
                    for name in ("oT", "yT"):
                        for s in range(SL):
                            act.wait_ge(S[name + "_ps"], s + 1)
                            turned(act, b1[s], T[s]["oT0"], T[s]["oT1"]).then_inc(S[name], 1)

                @block.tensor
                def _(pe):
                    for s in range(SL):
                        pe.wait_ge(S["xn"], s + 1)
                        turn(pe, G, T[s]["xn"], b0[s]).then_inc(S["xT_ps"], 1)
                    for s in range(SL):
                        pe.wait_ge(S["xT"], s + 1)
                        queries_keys_values(pe, wqkv0, wqkv1, T[s], b1[s], b0[s]).then_inc(S["qkv_ps"], 1)
                    for j in range(3):
                        for s in range(SL):
                            t, bk = T[s], (b0, b1, b0)[j][s]
                            if j == 0:
                                pe.wait_ge(S["qs0"], s + 1)
                                pe.wait_ge(S["qs1"], s + 1)
                                pe.wait_ge(S["v"], s + 1)
                            if j == 2:
                                pe.wait_ge(S["exp"], s + 1)
                            for g in range(4 * j, 4 * j + 4):
                                o = bk[0:N, (g % 4) * N:(g % 4 + 1) * N]
                                pe.matmul(o, t["qs0"][:, g, :], t["qk0"][:, 1, :], start=True, stop=False)
                                mm = pe.matmul(o, t["qs1"][:, g, :], t["qk1"][:, 1, :], start=False, stop=True)
                            mm.then_inc(S["s_ps"], 1)
                    for j, (a, b) in enumerate(GROUPS):
                        for s in range(SL):
                            pe.wait_ge(S["p"], s + 1)
                            if j == 2:
                                pe.wait_ge(S["c"], s + 1)
                            for c in range(a, b):
                                mm = pe.transpose((b1, b0, b1)[j][s][0:R, (c - a) * N:(c - a + 1) * N],
                                                  T[s]["p"][:].rearrange("p h (m c) -> p c (h m)", c=NC)[:, c, :],
                                                  G.ident[0:N, 0:N])
                            mm.then_inc(S["c_ps"], 1)
                    for j, (a, b) in enumerate(GROUPS):
                        for s in range(SL):
                            t = T[s]
                            pe.wait_ge(S["c"], 2 * SL + s + 1 if j == 0 else 3 * SL)
                            if j == 2:
                                pe.wait_ge(S["m"], s + 1)
                            for c in range(a, b):
                                mm = pe.matmul((b1, b0, b1)[j][s][0:N, (c - a) * R:(c - a + 1) * R], t["c"][:, c, :],
                                               mix[:], start=True, stop=True)
                            mm.then_inc(S["m_ps"], 1)
                    for j, (a, b) in enumerate(GROUPS):
                        for s in range(SL):
                            t = T[s]
                            pe.wait_ge(S["m"], 2 * SL + s + 1 if j == 0 else 3 * SL)
                            if j == 2:
                                pe.wait_ge(S["aT"], s + 1)
                            for g in range(a, b):
                                mm = pe.transpose((b0, b1, b0)[j][s][0:NM, (g - a) * N:(g - a + 1) * N],
                                                  t["m"][:, g, :], G.ident[0:N, 0:N])
                            mm.then_inc(S["aT_ps"], 1)

                    def applied(t, x, o):
                        for g in range(H):
                            last = pe.matmul(o[0:N, g * HD:(g + 1) * HD], t["aT"][0:N, g, :],
                                             x[:, g * HD:(g + 1) * HD], start=True, stop=True)
                        return last

                    for s in range(SL):
                        pe.wait_ge(S["aT"], 2 * SL + s + 1)
                        applied(T[s], T[s]["v"], b1[s]).then_inc(S["u_ps"], 1)
                    for s in range(SL):
                        pe.wait_ge(S["u"], s + 1)
                        applied(T[s], T[s]["u"], b0[s]).then_inc(S["r_ps"], 1)
                    for s in range(SL):
                        pe.wait_ge(S["o"], s + 1)
                        turn(pe, G, T[s]["o"], b1[s]).then_inc(S["oT_ps"], 1)
                    for s in range(SL):
                        t = T[s]
                        pe.wait_ge(S["oT"], s + 1)
                        pe.matmul(b0[s][0:N, 0:D], t["oT0"][:], wo0[:], start=True, stop=False)
                        pe.matmul(b0[s][0:N, 0:D], t["oT1"][:], wo1[:], start=False, stop=True).then_inc(S["y_ps"], 1)
                    for s in range(SL):
                        pe.wait_ge(S["yn"], s + 1)
                        turn(pe, G, T[s]["xn"], b1[s]).then_inc(S["yT_ps"], 1)
                    for s in range(SL):
                        t = T[s]
                        pe.wait_ge(S["yT"], s + 1)
                        pe.matmul(b0[s][0:N, 0:E], t["oT0"][:], sw0[:], start=True, stop=False)
                        pe.matmul(b0[s][0:N, 0:E], t["oT1"][:], sw1[:], start=False, stop=True).then_inc(S["lg_ps"], 1)
            clear(nc, list(S.values()))


class ExpertWeights:

    def __init__(self, nc, ctx, layer, W):
        sb, sem = allocator(nc, ctx)
        self.W = W
        self.w1a, self.w1b = sb(f"f{layer}_w1a", [D0, E * F]), sb(f"f{layer}_w1b", [D1 + 1, E * F])
        self.w2 = sb(f"f{layer}_w2s", [128, E * FT * D])
        self.b2 = sb(f"f{layer}_b2s", [1, E * D])
        self.weights_in = sem(f"f{layer}_weights_in")
        self.all_in = 16 * (3 * E + 1)

    def load(self, sp):
        W = self.W
        for e in range(E):
            sp.dma_start(self.w1a[:, e * F:(e + 1) * F], W["w1"][e, 0:D0, :]).then_inc(self.weights_in, 16)
            sp.dma_start(self.w1b[:, e * F:(e + 1) * F], W["w1"][e, D0:D + 1, :]).then_inc(self.weights_in, 16)
            sp.dma_start(self.w2[:, e * FT * D:(e + 1) * FT * D].rearrange("p (c d) -> p c d", d=D),
                         W["w2"][e].rearrange("(c p) d -> p c d", p=128)).then_inc(self.weights_in, 16)
        sp.dma_start(self.b2[:], W["b2"]).then_inc(self.weights_in, 16)


def route(nc, G, xs, layer, weights):
    Q = E * B
    with ExitStack() as ctx:
        sb, sem = allocator(nc, ctx)
        names = ("dve_chain", "dve_to_act", "act_to_dve", "dve_to_pe", "pe_to_dve", "iota", "dest")
        S = {n: sem(f"r{layer}_" + n) for n in names}
        z, ex, oh, key, t0, t1, rk, ekeep = (sb(f"r{layer}_{n}", [N, E, B]) for n in
                                             ("z", "ex", "oh", "key", "t0", "t1", "rk", "keep"))
        mx, t2, gate, dest = (sb(f"r{layer}_{n}", [N, B]) for n in ("mx", "t2", "gate", "dest"))
        dest_i = sb(f"r{layer}_desti", [N, B], I32)
        tok_i = sb(f"r{layer}_toki", [N, B], I32)
        pref_i = sb(f"r{layer}_prefi", [N, E], I32)
        pref = sb(f"r{layer}_pref", [N, E])
        lo, cand, cnt, few, step = (sb(f"r{layer}_{n}", [N, E]) for n in ("lo", "cand", "cnt", "few", "step"))
        blk, cum, base, start = (sb(f"r{layer}_{n}", [N, E]) for n in ("blk", "cum", "base", "start"))
        full_i, full = sb(f"r{layer}_fulli", [N, E, BLOCKS], I32), sb(f"r{layer}_full", [N, E, BLOCKS])
        bj_i = sb(f"r{layer}_bji", [1, BLOCKS, E], I32)
        bj, bje = sb(f"r{layer}_bj", [1, BLOCKS, E]), sb(f"r{layer}_bje", [1, BLOCKS])
        over_b = lambda a: a[:].unsqueeze(2).broadcast_to([N, E, B])
        over_e = lambda a: a[:].unsqueeze(1).broadcast_to([N, E, B])
        by_b = lambda a: a[:].rearrange("p e b -> p b e")
        flat = lambda a: a[:].rearrange("p e b -> p (e b)")
        counts = {"act": 0, "pe": 0}

        def ranked(dve, link, mask, out):
            counts["pe"] += 1
            dve.nop().then_inc(S["dve_to_pe"], 1)
            dve.wait_ge(S["pe_to_dve"], counts["pe"])
            link(dve.tensor_copy(flat(t1), G.ps[1][0:N, 0:Q]))
            link(dve.tensor_tensor_scan(flat(out), flat(z_ones), flat(t1), 0.0, ALU.mult, ALU.add))
            link(dve.tensor_tensor(out[:], out[:], t1[:], ALU.subtract))
            link(dve.tensor_copy(start[:], out[:, :, 0]))
            link(dve.tensor_tensor(cnt[:], out[:, :, B - 1], t1[:, :, B - 1], ALU.add))
            link(dve.tensor_tensor(cnt[:], cnt[:], start[:], ALU.subtract))
            link(dve.tensor_tensor(out[:], out[:], over_b(start), ALU.subtract))
            link(dve.tensor_tensor(flat(out), flat(out), G.ps[0][0:N, 0:Q], ALU.add))

        z_ones = ex if False else sb(f"r{layer}_ones", [N, E, B])
        with nc.Block() as block:
            @block.sync
            def _(sp):
                weights.load(sp)

            @block.gpsimd
            def _(pool):
                pool.iota(tok_i[:], [[N, B]], base=0, channel_multiplier=1)
                pool.iota(pref_i[:], [[-1, E]], base=E, channel_multiplier=0)
                pool.iota(full_i[:], [[0, E], [TW, BLOCKS]], base=0, channel_multiplier=0)
                pool.iota(bj_i[:], [[1, BLOCKS], [0, E]], base=0, channel_multiplier=0).then_inc(S["iota"], 1)

            @block.scalar
            def _(act):
                act.wait_ge(S["dve_to_act"], 1)
                act.activation(flat(ex), flat(z), ACT.Exp).then_inc(S["act_to_dve"], 1)

            @block.vector
            def _(dve):
                link = Chain(dve, S["dve_chain"])
                dve.memset(z_ones[:], 1.0)
                link(dve.tensor_reduce(mx[:], by_b(G.lg), AX.X, ALU.max))
                dve.tensor_tensor(z[:], G.lg[:], over_e(mx), ALU.subtract).then_inc(S["dve_to_act"], 1)
                dve.wait_ge(S["iota"], 1)
                link(dve.tensor_copy(G.h[:, :, TOK], tok_i[:]))
                link(dve.tensor_copy(pref[:], pref_i[:]))
                link(dve.tensor_copy(bj[:], bj_i[:]))
                link(dve.tensor_copy(full[:], full_i[:]))
                dve.wait_ge(S["act_to_dve"], 1)
                link(dve.tensor_reduce(t2[:], by_b(ex), AX.X, ALU.add))
                link(dve.reciprocal(gate[:], t2[:]))
                link(dve.tensor_copy(G.h[:, :, GATE], gate[:]))
                link(dve.tensor_scalar(t0[:], ex[:], 1.0, None, ALU.is_ge))
                link(dve.tensor_tensor(t0[:], t0[:], over_b(pref), ALU.mult))
                link(dve.tensor_reduce(t2[:], by_b(t0), AX.X, ALU.max))
                link(dve.tensor_tensor(oh[:], t0[:], over_e(t2), ALU.is_equal))
                link(dve.tensor_tensor(key[:], oh[:], over_e(gate), ALU.mult))
                link(dve.memset(lo[:], 0.0))
                link(dve.memset(step[:], 1.0))
                if layer:
                    link(dve.memset(G.h[:, :, KEEP:KEEP + 1], 1.0))
        clear(nc, list(S.values()))
        if layer == 0:
            BITS, UNROLL = 28, 7
            with nc.Fori(0, BITS // UNROLL) as it:
                with nc.Block() as block:
                    @block.tensor
                    def _(pe):
                        for j in range(UNROLL):
                            pe.wait_ge(S["dve_to_pe"], j + 1)
                            pe.matmul(G.ps[2][0:N, 0:E], G.ones[0:N, 0:N], few[:], start=True,
                                      stop=True).then_inc(S["pe_to_dve"], 1)

                    @block.vector
                    def _(dve):
                        link = Chain(dve, S["dve_chain"])
                        for j in range(UNROLL):
                            link(dve.tensor_tensor(cand[:], lo[:], step[:], ALU.add))
                            link(dve.tensor_tensor(t0[:], key[:], over_b(cand), ALU.is_ge))
                            dve.tensor_reduce(few[:], t0[:], AX.X, ALU.add).then_inc(S["dve_to_pe"], 1)
                            dve.wait_ge(S["pe_to_dve"], j + 1)
                            link(dve.scalar_tensor_tensor(cnt[:], G.ps[2][0:N, 0:E], float(CAP), step[:], ALU.is_ge,
                                                          ALU.mult))
                            dve.tensor_scalar(step[:], step[:], 0.5, None, ALU.mult)
                            link(dve.tensor_tensor(lo[:], lo[:], cnt[:], ALU.add))
                clear(nc, list(S.values()))
        masks = [oh] if layer else [ekeep, oh]
        with nc.Block() as block:
            @block.tensor
            def _(pe):
                n = 0
                if layer == 0:
                    n += 1
                    pe.wait_ge(S["dve_to_pe"], n)
                    pe.matmul(G.ps[2][0:N, 0:E], G.ones[0:N, 0:N], few[:], start=True, stop=True)\
                        .then_inc(S["pe_to_dve"], 1)
                for m in masks:
                    n += 1
                    pe.wait_ge(S["dve_to_pe"], n)
                    pe.matmul(G.ps[0][0:N, 0:Q], G.before[0:N, 0:N], flat(m), start=True, stop=True)
                    pe.matmul(G.ps[1][0:N, 0:Q], G.ones[0:N, 0:N], flat(m), start=True, stop=True)\
                        .then_inc(S["pe_to_dve"], 1)

            @block.vector
            def _(dve):
                link = Chain(dve, S["dve_chain"])
                if layer == 0:
                    link(dve.tensor_tensor(t0[:], key[:], over_b(lo), ALU.is_gt))
                    dve.tensor_reduce(few[:], t0[:], AX.X, ALU.add).then_inc(S["dve_to_pe"], 1)
                    counts["pe"] += 1
                    dve.wait_ge(S["pe_to_dve"], counts["pe"])
                    link(dve.tensor_scalar(few[:], G.ps[2][0:N, 0:E], -1.0, float(CAP), ALU.mult, ALU.add))
                    link(dve.tensor_tensor(ekeep[:], key[:], over_b(lo), ALU.is_equal))
                    link(dve.tensor_tensor(ekeep[:], ekeep[:], oh[:], ALU.mult))
                    ranked(dve, link, ekeep, rk)
                    link(dve.tensor_tensor(rk[:], rk[:], over_b(few), ALU.is_lt))
                    link(dve.tensor_tensor(ekeep[:], ekeep[:], rk[:], ALU.mult))
                    link(dve.tensor_tensor(ekeep[:], ekeep[:], t0[:], ALU.add))
                    link(dve.tensor_reduce(G.h[:, :, KEEP], by_b(ekeep), AX.X, ALU.add))
                ranked(dve, link, oh, rk)
                link(dve.tensor_tensor(full[:], cnt[:].unsqueeze(2).broadcast_to([N, E, BLOCKS]),
                                       full[:], ALU.is_gt))
                link(dve.tensor_reduce(blk[:], full[:], AX.X, ALU.add))
                link(dve.tensor_scalar(blk[:], blk[:], float(TW), None, ALU.mult))
                link(dve.tensor_tensor_scan(cum[:], z_ones[:, :, 0], blk[:], 0.0, ALU.mult, ALU.add))
                link(dve.tensor_tensor(base[:], cum[:], blk[:], ALU.subtract))
                link(dve.tensor_tensor(rk[:], rk[:], over_b(base), ALU.add))
                link(dve.tensor_tensor(rk[:], rk[:], oh[:], ALU.mult))
                link(dve.tensor_reduce(dest[:], by_b(rk), AX.X, ALU.add))
                dve.tensor_copy(dest_i[:], dest[:]).then_inc(S["dest"], 1)
                link(dve.tensor_scalar(cum[:], cum[:], 1.0 / TW, None, ALU.mult))
                link(dve.tensor_tensor(bj[:], bj[:], cum[0:1, :].unsqueeze(1).broadcast_to([1, BLOCKS, E]), ALU.is_ge))
                link(dve.tensor_reduce(bje[:], bj[:], AX.X, ALU.add))
                link(dve.tensor_scalar(bje[:], bje[:], float(E - 1), None, ALU.min))
                link(dve.tensor_copy(G.expert[0:1, :], bje[:]))

            @block.gpsimd
            def _(pool):
                pool.wait_ge(S["dest"], 1)
                for b in range(B):
                    pool.indirect_dma_start(xs, bass.IndirectOffsetOnAxis(dest_i[:, b:b + 1].bitcast(U32), 0),
                                            G.h[:, b, :], None).then_inc(G.rows_sent[layer], 16)
                pool.wait_ge(G.rows_sent[layer], 16 * B)
        clear(nc, list(S.values()))


def experts(nc, G, xs, dst, weights, layer):
    PER = 18
    n_it = BLOCKS // PER
    assert BLOCKS % PER == 0
    with ExitStack() as ctx:
        sb, sem = allocator(nc, ctx)
        names = ("ones_set", "xn", "xT_ps", "xT", "h_ps", "gelu", "hT_ps", "hT", "y_ps", "out", "var", "rstd",
                 "dve_chain")
        S = {n: sem(f"f{layer}_" + n) for n in names}
        THIRD = PER // 3
        xs_in = [sem(f"f{layer}_xs_in{j}") for j in range(3)]
        w1a, w1b, w2, b2 = weights.w1a, weights.w1b, weights.w2, weights.b2
        x = [sb(f"f{layer}_x{i}", [TW, HC]) for i in range(PER)]
        o = [sb(f"f{layer}_o{i}", [TW, D]) for i in range(PER)]
        tok = [sb(f"f{layer}_tok{i}", [TW, 1], I32) for i in range(PER)]
        xn = [sb(f"f{layer}_xn{i}", [TW, D]) for i in range(PER)]
        st = [sb(f"f{layer}_st{i}", [TW, 6]) for i in range(PER)]
        mv = [sb(f"f{layer}_mv{i}", [TW, 3]) for i in range(PER)]
        xT0 = [sb(f"f{layer}_xT0{i}", [D0, TW]) for i in range(2)]
        xT1 = [sb(f"f{layer}_xT1{i}", [D1 + 1, TW]) for i in range(2)]
        hs = [sb(f"f{layer}_hs{i}", [TW, F]) for i in range(2)]
        hT = [sb(f"f{layer}_hT{i}", [128, FT, TW]) for i in range(2)]
        with nc.Block() as block:
            @block.sync
            def _(sp):
                sp.wait_ge(weights.weights_in, weights.all_in)

            @block.vector
            def _(dve):
                for i in range(2):
                    dve.memset(xT1[i][D1:D1 + 1, :], 1.0).then_inc(S["ones_set"], 1)
                dve.wait_ge(S["ones_set"], 2)
        clear(nc, list(S.values()) + xs_in + [weights.weights_in])
        with nc.Fori(0, n_it) as it:
            with nc.Block() as block:
                @block.sync
                def _(sp):
                    for i in range(PER):
                        sp.dma_start(x[i][:], xs[bass.ds((it * PER + i) * TW, TW), :]).then_inc(xs_in[i // THIRD], 16)

                @block.vector
                def _(dve):
                    link = Chain(dve, S["dve_chain"])

                    def stats(i):
                        norm_stats(dve, link, x[i][:, 0:D], st[i], mv[i], TW, S["var"])
                        link(dve.tensor_copy(tok[i][:], x[i][:, TOK:TOK + 1]))

                    def norm(i):
                        dve.wait_ge(S["rstd"], i + 1)
                        norm_apply(dve, x[i][:, 0:D], xn[i][:], mv[i], TW).then_inc(S["xn"], 1)

                    def h_turned(i):
                        u = i % 2
                        dve.wait_ge(S["hT_ps"], i + 1)
                        dve.tensor_copy(hT[u][:, 0:4, :].rearrange("p c t -> p (c t)"), G.ps[6][:, :])
                        dve.tensor_copy(hT[u][:, 4:6, :].rearrange("p c t -> p (c t)"),
                                        G.ps[7][:, 0:2 * TW]).then_inc(S["hT"], 1)

                    def finish(i):
                        dve.wait_ge(S["y_ps"], i + 1)
                        y = G.ps[1][:, 0:D]
                        if layer:
                            dve.tensor_tensor(o[i][:], y, x[i][:, 0:D], ALU.add).then_inc(S["out"], 1)
                        else:
                            link(dve.tensor_tensor(o[i][:], y, xn[i][:], ALU.subtract))
                            link(dve.scalar_tensor_tensor(o[i][:], o[i][:], x[i][:, KEEP:KEEP + 1], xn[i][:],
                                                          ALU.mult, ALU.add))
                            dve.scalar_tensor_tensor(o[i][:], o[i][:], x[i][:, GATE:GATE + 1], x[i][:, 0:D],
                                                     ALU.mult, ALU.add).then_inc(S["out"], 1)

                    dve.wait_ge(xs_in[0], 16 * THIRD)
                    for i in range(THIRD):
                        stats(i)
                        if i >= 2:
                            norm(i - 2)
                    for i in range(PER):
                        h_turned(i)
                        if i:
                            finish(i - 1)
                        if i + THIRD < PER:
                            if (i + THIRD) % THIRD == 0:
                                dve.wait_ge(xs_in[(i + THIRD) // THIRD], 16 * THIRD)
                            stats(i + THIRD)
                        if i + THIRD - 2 < PER:
                            norm(i + THIRD - 2)
                    finish(PER - 1)

                @block.scalar
                def _(act):
                    def x_turned(i):
                        u = i % 2
                        act.wait_ge(S["xT_ps"], i + 1)
                        if i >= 2:
                            act.wait_ge(S["h_ps"], 2 * (i - 1))
                        act.copy(xT0[u][:], G.ps[0][:, 0:TW])
                        act.copy(xT1[u][0:D1, :], G.ps[0][0:D1, TW:2 * TW]).then_inc(S["xT"], 1)

                    x_turned(0)
                    for i in range(PER):
                        if i + 1 < PER:
                            x_turned(i + 1)
                        u = i % 2
                        if i >= 2:
                            act.wait_ge(S["hT_ps"], i - 1)
                        for c in range(2):
                            act.wait_ge(S["h_ps"], 2 * i + c + 1)
                            act.activation(hs[u][:, c * FH:(c + 1) * FH], G.ps[2 + 2 * u + c][:, 0:FH],
                                           ACT.Gelu).then_inc(S["gelu"], 1)

                @block.tensor
                def _(pe):
                    ex = [None] * PER

                    def turn(i):
                        ex[i] = pe.value_load(G.expert[0:1, bass.ds(it * PER + i, 1)], min_val=0, max_val=E - 1)
                        pe.wait_ge(S["xn"], i + 1)
                        if i:
                            pe.wait_ge(S["xT"], i)
                        pe.transpose(G.ps[0][:, 0:TW], xn[i][:, 0:D0], G.ident[:, :])
                        pe.transpose(G.ps[0][0:D1, TW:2 * TW], xn[i][:, D0:D], G.ident[:, :]).then_inc(S["xT_ps"], 1)

                    def first(i):
                        u = i % 2
                        pe.wait_ge(S["xT"], i + 1)
                        if i >= 2:
                            pe.wait_ge(S["gelu"], 2 * (i - 1))
                        for c in range(2):
                            at = bass.ds(ex[i] * F + c * FH, FH)
                            pe.matmul(G.ps[2 + 2 * u + c][:, 0:FH], xT0[u][:], w1a[:, at], start=True, stop=False)
                            pe.matmul(G.ps[2 + 2 * u + c][:, 0:FH], xT1[u][:], w1b[:, at], start=False,
                                      stop=True).then_inc(S["h_ps"], 1)

                    def turn_h(i):
                        u = i % 2
                        pe.wait_ge(S["gelu"], 2 * (i + 1))
                        if i:
                            pe.wait_ge(S["hT"], i)
                        if i >= 2:
                            pe.wait_ge(S["y_ps"], i - 1)
                        for c in range(FT):
                            mm = pe.transpose(G.ps[6 + c // 4][:, (c % 4) * TW:(c % 4 + 1) * TW],
                                              hs[u][:, c * 128:(c + 1) * 128], G.ident[:, :])
                        mm.then_inc(S["hT_ps"], 1)

                    def second(i):
                        u = i % 2
                        if i:
                            pe.wait_ge(S["out"], i)
                        pe.wait_ge(S["hT"], i + 1)
                        for c in range(FT):
                            pe.matmul(G.ps[1][:, 0:D], hT[u][:, c, :], w2[:, bass.ds(ex[i] * (FT * D) + c * D, D)],
                                      start=(c == 0), stop=False)
                        pe.matmul(G.ps[1][:, 0:D], G.ones[0:1, 0:TW], b2[:, bass.ds(ex[i] * D, D)], start=False,
                                  stop=True).then_inc(S["y_ps"], 1)

                    turn(0)
                    first(0)
                    for i in range(PER):
                        if i + 1 < PER:
                            turn(i + 1)
                            first(i + 1)
                        if i:
                            second(i - 1)
                        turn_h(i)
                    second(PER - 1)

                @block.gpsimd
                def _(pool):
                    def scale(i):
                        pool.wait_ge(S["var"], i + 1)
                        norm_rstd(pool, G, mv[i], TW, S["rstd"])

                    for i in range(THIRD):
                        scale(i)
                    for i in range(PER):
                        if i + THIRD < PER:
                            scale(i + THIRD)
                        pool.wait_ge(S["out"], i + 1)
                        pool.indirect_dma_start(dst, bass.IndirectOffsetOnAxis(tok[i][:].bitcast(U32), 0), o[i][:],
                                                None, bounds_check=NT - 1, oob_is_err=False).then_inc(G.rows_out[layer], 16)
                    pool.wait_ge(G.rows_out[layer], (it + 1) * (16 * PER))
            clear(nc, list(S.values()) + xs_in)


def reload_tokens(nc, G, src):
    with ExitStack() as ctx:
        sb, sem = allocator(nc, ctx)
        rows_in = sem("rows_back")
        with nc.Block() as block:
            @block.sync
            def _(sp):
                sp.dma_start(G.h[:, :, 0:D], src.rearrange("(b n) d -> n b d", n=N)).then_inc(rows_in, 16)
                sp.wait_ge(rows_in, 16)
        clear(nc, [rows_in])


def landmark_attention(nc, G, A, xd):
    PAIRS = H // 2
    SPAN = LM + LR
    STEPS = 6
    SC = 3.75
    ROOT = float(ZL) ** 0.5
    WV = PAIRS * LM
    with ExitStack() as ctx:
        sb, sem = allocator(nc, ctx)
        names = ("var", "rstd", "xn", "xT_ps", "xT", "xl", "qk_ps", "kl", "s2_ps", "nm", "exp", "x", "col_ps",
                 "x_out", "dve_chain", "act_chain", "pool_chain", "setup", "weights_in", "qk", "lm", "mq",
                 "v", "mk", "s1_ps", "s3_ps", "s1_shift", "s1_exp", "s3_nm", "s3_exp", "p1", "p1T_ps", "p3T_ps",
                 "p1T", "p3T", "r_ps", "xr", "w0_ps", "wv", "a_ps", "a", "g", "c0", "c", "n_ps", "va_ps", "vg", "vh",
                 "zr", "o_ps", "o", "oT_ps", "oT", "y_ps", "yn", "yT_ps", "yT", "lg_ps", "red")
        S = {n: sem("l1_" + n) for n in names}
        x_in = [sem(f"l1_x_in{s}") for s in range(SL)]
        sems = list(S.values()) + x_in
        wqkv0, wqkv1 = sb("l1_wqkv0", [D0, 3 * D]), sb("l1_wqkv1", [D1, 3 * D])
        wo0, wo1 = sb("l1_wo0", [D0, D]), sb("l1_wo1", [D1 + 1, D])
        sw0, sw1 = sb("l1_sw0", [D0, E]), sb("l1_sw1", [D1 + 1, E])
        head, rootw, colw = sb("l1_head_s", [128, 8]), sb("l1_rootw_s", [128, 1]), sb("l1_colw_s", [128, 2])
        rowmax, colmax = sb("l1_rowmax", [128, PAIRS]), sb("l1_colmax", [LM, PAIRS, 2])
        most, cinv = sb("l1_most", [128, 4]), sb("l1_cinv", [128, 1])
        T = []
        for s in range(SL):
            t = {}
            for n, shape in (("st", [N, 6]), ("mv", [N, 3]), ("xn", [N, D]), ("xT0", [D0, N]), ("xT1", [D1, N]),
                             ("xl0", [D0, LR]), ("xl1", [D1, LR]), ("mq0", [128, 8, LM]), ("mq1", [64, 4, LM]),
                             ("lm0", [D0, 2, LR]), ("lm1", [D1, 2, LR]), ("nm", [128, PAIRS]), ("rs", [128, PAIRS]),
                             ("rt", [128, PAIRS]), ("qk0", [D0, 2, N]), ("qk1", [D1, 2, N]),
                             ("v", [N, D]), ("mk0", [128, 8, LR]), ("mk1", [64, 4, LR]), ("p1", [N, H, LM]),
                             ("nm1", [N, H]), ("rz1", [N, H]), ("p3", [128, PAIRS, N]), ("nm3", [128, PAIRS]),
                             ("rs3", [128, PAIRS]), ("e3", [128, PAIRS]), ("p1T", [128, PAIRS, N]),
                             ("p3T", [N, PAIRS, 128]), ("xr", [128, PAIRS, LM]), ("wv", [128, PAIRS, LM]),
                             ("a", [128, PAIRS, LM]), ("g", [128, PAIRS, LM]), ("c", [128, PAIRS, LM]),
                             ("zr", [128, PAIRS, 2 * HD]), ("o", [N, D]), ("oT0", [D0, N]), ("oT1", [D1 + 1, N])):
                t[n] = sb(f"l1_{n}_{s}", shape)
            T.append(t)
        b0, b1 = [G.ps[2 * s] for s in range(SL)], [G.ps[2 * s + 1] for s in range(SL)]
        with nc.Block() as block:
            @block.sync
            def _(sp):
                lots = ((wqkv0[:], A["wqkv"][0:D0]), (wqkv1[:], A["wqkv"][D0:D]), (wo0[:], A["wo"][0:D0]),
                        (wo1[:], A["wo"][D0:D + 1]), (sw0[:], A["sw"][0:D0]), (sw1[:], A["sw"][D0:D + 1]),
                        (head[:], A["head"]), (rootw[:], A["rootw"]), (colw[:], A["colw"]))
                for dst, src in lots:
                    sp.dma_start(dst, src).then_inc(S["weights_in"], 16)

            @block.vector
            def _(dve):
                for s in range(SL):
                    t = T[s]
                    for n in ("xl0", "xl1", "lm0", "lm1", "mq0", "mq1", "p1", "xr", "zr"):
                        dve.memset(t[n][:], 0.0)
                    dve.memset(t["oT1"][D1:D1 + 1, :], 1.0)
                for bank in G.ps:
                    dve.memset(bank[:], 0.0)
                dve.memset(rowmax[:], 0.0)
                dve.memset(colmax[:], 0.0)
                dve.memset(most[:], 0.0)
                dve.wait_ge(S["weights_in"], 16 * 9)
                dve.tensor_scalar(wqkv0[:, 0:D], wqkv0[:, 0:D], SCALE, None, ALU.mult)
                dve.tensor_scalar(wqkv1[:, 0:D], wqkv1[:, 0:D], SCALE, None, ALU.mult)
                dve.tensor_scalar(head[:], head[:], 0.5, None, ALU.mult).then_inc(S["setup"], 1)
                dve.wait_ge(S["setup"], 1)
        clear(nc, sems)

        def hrow(it, s):
            return G.h[:, bass.ds(it * SL + s, 1), 0:D].rearrange("p a d -> p (a d)")

        def normed(dve, link, it):
            for s in range(SL):
                norm_stats(dve, link, hrow(it, s), T[s]["st"], T[s]["mv"], N, S["var"])
            for s in range(SL):
                dve.wait_ge(S["rstd"], s + 1)
                norm_apply(dve, hrow(it, s), T[s]["xn"][:], T[s]["mv"], N).then_inc(S["xn"], 1)

        def tiles(bk, n, width):
            return bk[:, 0:n * width].rearrange("p (a j) -> p a j", j=width)

        def masked(eng, src, out, rows, heads):
            return eng.tensor_tensor(out[:, :, 0:LR], src.unsqueeze(1).broadcast_to([rows, heads, LR]),
                                     head[0:rows, 0:heads].unsqueeze(2).broadcast_to([rows, heads, LR]), ALU.mult)

        def pair_query(t, p):
            m = t["mq0"][:, 2 * p:2 * p + 2, :] if p < 4 else t["mq1"][:, 2 * p - 8:2 * p - 6, :]
            return m.rearrange("p a j -> p (a j)")

        with nc.Fori(0, B // SL) as it:
            with nc.Block() as block:
                @block.sync
                def _(sp):
                    for s in range(SL):
                        sp.wait_ge(S["x"], s + 1)
                        sp.dma_start(xd[bass.ds(it * SL + s, 1), :, :].rearrange("a p q -> p (a q)"),
                                     T[s]["xr"][:].rearrange("p a j -> p (a j)")).then_inc(S["x_out"], 16)
                    sp.wait_ge(S["x_out"], 16 * SL)

                @block.gpsimd
                def _(pool):
                    for s in range(SL):
                        pool.wait_ge(S["var"], s + 1)
                        norm_rstd(pool, G, T[s]["mv"], N, S["rstd"])

                @block.vector
                def _(dve):
                    link = Chain(dve, S["dve_chain"])
                    normed(dve, link, it)
                    for s in range(SL):
                        t = T[s]
                        dve.wait_ge(S["xT_ps"], s + 1)
                        for x, o, n in ((b0[s][:, 0:N], t["xl0"], D0), (b0[s][0:D1, 128:128 + N], t["xl1"], D1)):
                            dve.tensor_copy(o[:, 0:1], x[:, 0:1])
                            last = dve.tensor_reduce(o[:, 1:LR - 1], x[:, 1:N].rearrange("p (j i) -> p j i", i=2),
                                                     AX.X, ALU.add)
                        last.then_inc(S["xl"], 1)
                    for s in range(SL):
                        t = T[s]
                        dve.wait_ge(S["qk_ps"], s + 1)
                        masked(dve, b1[s][:, 0:LR], t["mq0"], 128, 8)
                        masked(dve, b1[s][0:64, LR:2 * LR], t["mq1"], 64, 4)
                        dve.tensor_scalar(t["lm0"][:, 1, :], b1[s][:, 2 * LR:3 * LR], 0.5, None, ALU.mult)
                        dve.tensor_scalar(t["lm1"][:, 1, :], b1[s][0:64, 3 * LR:4 * LR], 0.5, None, ALU.mult)\
                           .then_inc(S["mq"], 1)
                    for s in range(SL):
                        dve.wait_ge(S["s2_ps"], s + 1)
                        dve.tensor_reduce(T[s]["nm"][:], tiles(b0[s], PAIRS, LR), AX.X, ALU.max,
                                          negate=True).then_inc(S["nm"], 1)
                    for s in range(SL):
                        t = T[s]
                        xe = t["xr"]
                        dve.wait_ge(S["exp"], s + 1)
                        link(dve.scalar_tensor_tensor(t["rs"][:], xe[:, :, LR - 1], float(ZL - 1), t["rs"][:],
                                                      ALU.mult, ALU.add))
                        link(dve.reciprocal(t["rt"][:], t["rs"][:]))
                        link(dve.tensor_tensor(t["rs"][:], t["rs"][:], t["rt"][:], ALU.mult))
                        link(dve.tensor_tensor(rowmax[:], rowmax[:], t["rs"][:], ALU.max))
                        link(dve.tensor_scalar(t["rt"][:], t["rt"][:], rootw[:], None, ALU.mult))
                        link(dve.tensor_scalar(xe[:, :, LR - 1], xe[:, :, LR - 1], ROOT, None, ALU.mult))
                        dve.tensor_tensor(xe[:, :, 0:LR], xe[:, :, 0:LR],
                                          t["rt"][:].unsqueeze(2).broadcast_to([128, PAIRS, LR]),
                                          ALU.mult).then_inc(S["x"], 1)
                    for s in range(SL):
                        dve.wait_ge(S["col_ps"], s + 1)
                        link(dve.tensor_tensor(colmax[:], colmax[:], tiles(b1[s], PAIRS, 2)[0:LM], ALU.max))

                @block.scalar
                def _(act):
                    for s in range(SL):
                        t = T[s]
                        act.wait_ge(S["nm"], s + 1)
                        for p in range(PAIRS):
                            last = act.activation(t["xr"][:, p, 0:LR], b0[s][:, p * LR:(p + 1) * LR], ACT.Exp,
                                                  bias=t["nm"][:, p:p + 1], accum_out=t["rs"][:, p:p + 1])
                        last.then_inc(S["exp"], 1)

                @block.tensor
                def _(pe):
                    for s in range(SL):
                        pe.wait_ge(S["xn"], s + 1)
                        turn(pe, G, T[s]["xn"], b0[s]).then_inc(S["xT_ps"], 1)
                    for s in range(SL):
                        t = T[s]
                        pe.wait_ge(S["xl"], s + 1)
                        for part in range(2):
                            for m, (a, n) in enumerate(((part * D, D0), (part * D + D0, D1))):
                                o = b1[s][0:n, (2 * part + m) * LR:(2 * part + m + 1) * LR]
                                pe.matmul(o, wqkv0[:, a:a + n], t["xl0"][:], start=True, stop=False)
                                mm = pe.matmul(o, wqkv1[:, a:a + n], t["xl1"][:], start=False, stop=True)
                        mm.then_inc(S["qk_ps"], 1)
                    for s in range(SL):
                        t = T[s]
                        pe.wait_ge(S["mq"], s + 1)
                        for p in range(PAIRS):
                            mm = pe.matmul(b0[s][:, p * LR:(p + 1) * LR], pair_query(t, p),
                                           (t["lm0"] if p < 4 else t["lm1"])[:, 1, :], start=True, stop=True)
                        mm.then_inc(S["s2_ps"], 1)
                    for s in range(SL):
                        pe.wait_ge(S["x"], s + 1)
                        for p in range(PAIRS):
                            mm = pe.matmul(b1[s][0:LM, 2 * p:2 * p + 2], T[s]["xr"][:, p, :], colw[:], start=True,
                                           stop=True)
                        mm.then_inc(S["col_ps"], 1)
            clear(nc, sems)
        with nc.Block() as block:
            @block.vector
            def _(dve):
                link = Chain(dve, S["dve_chain"])
                link(dve.tensor_reduce(most[0:LM, 1:2], colmax[:].rearrange("p a j -> p (a j)"), AX.X, ALU.max))
                link(dve.reciprocal(cinv[0:LM, :], rootw[0:LM, :]))
                link(dve.tensor_tensor(most[0:LM, 1:2], most[0:LM, 1:2], cinv[0:LM, :], ALU.mult))
                link(dve.tensor_reduce(most[:, 0:1], rowmax[:], AX.X, ALU.max))
                link(dve.tensor_reduce(cinv[:], colw[:], AX.X, ALU.add))
                link(dve.tensor_scalar(cinv[:], cinv[:], 0.0, None, ALU.is_gt))
                dve.tensor_tensor(most[:, 0:1], most[:, 0:1], cinv[:], ALU.mult).then_inc(S["setup"], 1)
                dve.wait_ge(S["red"], 1)
                link(dve.tensor_tensor(cinv[:], most[:, 2:3], most[:, 3:4], ALU.mult))
                link(dve.reciprocal(cinv[:], cinv[:]))

            @block.gpsimd
            def _(pool):
                pool.wait_ge(S["setup"], 1)
                pool.partition_all_reduce(most[:, 2:4], most[:, 0:2], 128, bass.bass_isa.ReduceOp.max)\
                    .then_inc(S["red"], 1)
        clear(nc, sems)

        halves = [(0, slice(0, LR), slice(0, LR)), (1, slice(LM, SPAN), slice(LM, SPAN))]

        def each_head(pe, lhs, rhs, out, a, b):
            for p in range(PAIRS):
                for _, k, m in halves:
                    last = pe.matmul(out[m, p * (b - a):(p + 1) * (b - a)], lhs[k, p, 0:LR], rhs[k, p, a:b], start=True,
                                     stop=True)
            return last

        with nc.Fori(0, B // SL) as it:
            with nc.Block() as block:
                @block.sync
                def _(sp):
                    for s in range(SL):
                        sp.dma_start(T[s]["xr"][:].rearrange("p a j -> p (a j)"),
                                     xd[bass.ds(it * SL + s, 1), :, :].rearrange("a p q -> p (a q)"))\
                          .then_inc(x_in[s], 16)

                @block.gpsimd
                def _(pool):
                    link = Chain(pool, S["pool_chain"])
                    for s in range(SL):
                        pool.wait_ge(S["var"], s + 1)
                        norm_rstd(pool, G, T[s]["mv"], N, S["rstd"])
                    for s in range(SL):
                        t = T[s]
                        pool.wait_ge(S["lm"], s + 1)
                        masked(pool, t["lm0"][:, 0, :], t["mq0"], 128, 8)
                        masked(pool, t["lm1"][:, 0, :], t["mq1"], 64, 4).then_inc(S["mq"], 1)
                    for k in range(STEPS - 1):
                        for s in range(SL):
                            t = T[s]
                            pool.wait_ge(S["a"], SL * k + s + 1)
                            pool.wait_ge(S["c0"], SL * k + s + 1)
                            pool.tensor_tensor(t["c"][:], t["c"][:], t["a"][:], ALU.subtract).then_inc(S["c"], 1)
                    for s in range(SL):
                        pool.wait_ge(S["var"], SL + s + 1)
                        norm_rstd(pool, G, T[s]["mv"], N, S["rstd"])

                @block.vector
                def _(dve):
                    link = Chain(dve, S["dve_chain"])
                    normed(dve, link, it)
                    for s in range(SL):
                        t = T[s]
                        dve.wait_ge(S["qk"], s + 1)
                        for x, o in ((t["qk0"], t["lm0"]), (t["qk1"], t["lm1"])):
                            rows = D0 if x is t["qk0"] else D1
                            dve.tensor_copy(o[:, :, 0:1], x[:, :, 0:1])
                            two = x[:, :, 1:N].rearrange("p a (j i) -> p a i j", i=2)
                            last = dve.tensor_tensor(o[:, :, 1:LR - 1], two[:, :, 0, :], two[:, :, 1, :], ALU.add)
                        last.then_inc(S["lm"], 1)
                        dve.wait_ge(S["lm"], s + 1)
                        masked(dve, t["lm0"][:, 1, :], t["mk0"], 128, 8)
                        masked(dve, t["lm1"][:, 1, :], t["mk1"], 64, 4).then_inc(S["mk"], 1)
                    for s in range(SL):
                        t = T[s]
                        dve.wait_ge(S["s1_ps"], s + 1)
                        h0, h1 = tiles(b0[s], 8, LR)[0:N], tiles(b1[s], 4, LR)[0:N]
                        dve.tensor_reduce(t["nm1"][:, 0:8], h0, AX.X, ALU.max, negate=True)
                        link(dve.tensor_reduce(t["nm1"][:, 8:H], h1, AX.X, ALU.max, negate=True))
                        over = lambda a, b: t["nm1"][:, a:b].unsqueeze(2).broadcast_to([N, b - a, LR])
                        dve.tensor_tensor(t["p1"][:, 0:8, 0:LR], h0, over(0, 8), ALU.add)
                        dve.tensor_tensor(t["p1"][:, 8:H, 0:LR], h1, over(8, H), ALU.add).then_inc(S["s1_shift"], 1)
                    for s in range(SL):
                        t = T[s]
                        dve.wait_ge(S["s3_ps"], s + 1)
                        for j, bk in enumerate((b0[s], b1[s])):
                            link(dve.tensor_reduce(t["nm3"][:, 3 * j:3 * j + 3], tiles(bk, 3, N), AX.X, ALU.max,
                                                   negate=True))
                        dve.tensor_scalar(t["nm3"][:], t["nm3"][:], 0.0, None, ALU.min).then_inc(S["s3_nm"], 1)
                    for s in range(SL):
                        t = T[s]
                        dve.wait_ge(S["s1_exp"], s + 1)
                        last = t["p1"][:, :, LR - 1]
                        link(dve.tensor_reduce(t["rz1"][:], t["p1"][:, :, 0:LR], AX.X, ALU.add))
                        link(dve.scalar_tensor_tensor(t["rz1"][:], last, float(ZL - 1), t["rz1"][:], ALU.mult, ALU.add))
                        link(dve.reciprocal(t["rz1"][:], t["rz1"][:]))
                        dve.tensor_scalar(last, last, ROOT, None, ALU.mult).then_inc(S["p1"], 1)
                    for s in range(SL):
                        t = T[s]
                        dve.wait_ge(S["s3_exp"], s + 1)
                        link(dve.scalar_tensor_tensor(t["rs3"][:], t["e3"][:], float(PADS), t["rs3"][:], ALU.mult,
                                                      ALU.add))
                        link(dve.reciprocal(t["rs3"][:], t["rs3"][:]))
                        link(dve.tensor_scalar(t["rs3"][:], t["rs3"][:], rootw[:], None, ALU.mult))
                    for s in range(SL):
                        t = T[s]
                        dve.wait_ge(x_in[s], 16)
                        dve.wait_ge(S["r_ps"], s + 1)
                        r = tiles(b0[s], PAIRS, 2 * HD)
                        for i in range(2):
                            h = slice(LM * i, LM * i + LM)
                            last = dve.tensor_tensor(t["xr"][h, :, LR:LM], r[h, :, HD * i:HD * i + HD],
                                                     t["rs3"][h, :].unsqueeze(2).broadcast_to([LM, PAIRS, HD]), ALU.mult)
                        last.then_inc(S["xr"], 1)
                    for s in range(SL):
                        dve.wait_ge(S["w0_ps"], s + 1)
                        dve.tensor_scalar(T[s]["wv"][:], tiles(b1[s], PAIRS, LM), cinv[:], SC,
                                          ALU.mult, ALU.mult).then_inc(S["wv"], 1)
                    for k in range(STEPS - 1):
                        for s in range(SL):
                            t = T[s]
                            dve.wait_ge(S["a"], SL * k + s + 1)
                            dve.wait_ge(S["wv"], SL * k + s + 1)
                            dve.scalar_tensor_tensor(t["g"][:], t["wv"][:], 7 * SC, t["a"][:], ALU.mult,
                                                     ALU.subtract).then_inc(S["g"], 1)
                        for s in range(SL):
                            t = T[s]
                            dve.wait_ge(S["n_ps"], SL * k + s + 1)
                            dve.wait_ge(S["c"], SL * k + s + 1)
                            dve.scalar_tensor_tensor(t["wv"][:], tiles(b1[s], PAIRS, LM), 0.25 / SC ** 3, t["c"][:], ALU.mult,
                                                     ALU.add).then_inc(S["wv"], 1)
                    for s in range(SL):
                        t = T[s]
                        a, v, c, g = b0[s], t["wv"][:, :, LR:LM], t["c"][:, :, 0:HD], t["g"][:, :, 0:HD]
                        dve.wait_ge(S["va_ps"], s + 1)
                        dve.wait_ge(S["c0"], SL * (STEPS - 1) + s + 1)
                        dve.scalar_tensor_tensor(g, v, 7 * SC, tiles(a, PAIRS, HD), ALU.mult, ALU.subtract)\
                           .then_inc(S["vg"], 1)
                        link(dve.scalar_tensor_tensor(c, tiles(a, PAIRS, HD), -3.75 / SC ** 2, c, ALU.mult, ALU.add))
                    for s in range(SL):
                        dve.wait_ge(S["va_ps"], SL + s + 1)
                        dve.tensor_copy(T[s]["g"][:, :, HD:2 * HD], tiles(b1[s], PAIRS, HD)).then_inc(S["vh"], 1)
                    for s in range(SL):
                        t = T[s]
                        dve.wait_ge(S["va_ps"], 2 * SL + s + 1)
                        for i, rows, _ in halves:
                            last = dve.scalar_tensor_tensor(t["zr"][rows, :, HD * i:HD * i + HD],
                                                            tiles(b0[s], PAIRS, HD)[rows], 0.25 / SC ** 4,
                                                            t["c"][rows, :, 0:HD], ALU.mult, ALU.add)
                        last.then_inc(S["zr"], 1)
                    for s in range(SL):
                        t = T[s]
                        dve.wait_ge(S["o_ps"], s + 1)
                        dve.tensor_tensor(t["o"][:].rearrange("p (h d) -> p h d", d=HD), tiles(b1[s], H, HD)[0:N],
                                          t["rz1"][:].unsqueeze(2).broadcast_to([N, H, HD]), ALU.mult)\
                           .then_inc(S["o"], 1)
                    for s in range(SL):
                        t = T[s]
                        dve.wait_ge(S["y_ps"], s + 1)
                        link(dve.tensor_tensor(hrow(it, s), hrow(it, s), b1[s][0:N, 0:D], ALU.add))
                        norm_stats(dve, link, hrow(it, s), t["st"], t["mv"], N, S["var"])
                    for s in range(SL):
                        t = T[s]
                        dve.wait_ge(S["rstd"], SL + s + 1)
                        norm_apply(dve, hrow(it, s), t["xn"][:], t["mv"], N).then_inc(S["yn"], 1)
                    for s in range(SL):
                        dve.wait_ge(S["lg_ps"], s + 1)
                        dve.tensor_copy(G.lg[:, :, bass.ds(it * SL + s, 1)], b1[s][0:N, 0:E].unsqueeze(2))

                @block.scalar
                def _(act):
                    for s in range(SL):
                        act.wait_ge(S["xT_ps"], s + 1)
                        turned(act, b0[s], T[s]["xT0"], T[s]["xT1"]).then_inc(S["xT"], 1)
                    for s in range(SL):
                        t = T[s]
                        act.wait_ge(S["qk_ps"], s + 1)
                        act.copy(t["qk0"][:].rearrange("p a n -> p (a n)"), b1[s][:, 0:2 * N])
                        act.copy(t["qk1"][:].rearrange("p a n -> p (a n)"), b1[s][0:D1, 2 * N:4 * N])\
                           .then_inc(S["qk"], 1)
                        act.copy(t["v"][:], b0[s][0:N, 0:D]).then_inc(S["v"], 1)
                    for s in range(SL):
                        t = T[s]
                        act.wait_ge(S["s1_shift"], s + 1)
                        act.activation(t["p1"][:, :, 0:LR], t["p1"][:, :, 0:LR], ACT.Exp).then_inc(S["s1_exp"], 1)
                    for s in range(SL):
                        t = T[s]
                        act.wait_ge(S["s3_nm"], s + 1)
                        for p in range(PAIRS):
                            bk = b0[s] if p < 3 else b1[s]
                            act.activation(t["p3"][:, p, :], bk[:, (p % 3) * N:(p % 3 + 1) * N],
                                           ACT.Exp, bias=t["nm3"][:, p:p + 1], accum_out=t["rs3"][:, p:p + 1])
                        act.activation(t["e3"][:], t["nm3"][:], ACT.Exp).then_inc(S["s3_exp"], 1)
                    for s in range(SL):
                        t = T[s]
                        act.wait_ge(S["p1T_ps"], s + 1)
                        act.copy(t["p1T"][:, 0:4, :], tiles(b0[s], 4, N))
                        act.copy(t["p1T"][:, 4:6, :], tiles(b1[s], 2, N)).then_inc(S["p1T"], 1)
                    for s in range(SL):
                        t = T[s]
                        act.wait_ge(S["p3T_ps"], s + 1)
                        act.copy(t["p3T"][:, 0:4, :], tiles(b0[s], 4, 128)[0:N])
                        act.copy(t["p3T"][:, 4:6, :], tiles(b1[s], 2, 128)[0:N]).then_inc(S["p3T"], 1)
                    for k in range(STEPS):
                        for s in range(SL):
                            t = T[s]
                            act.wait_ge(S["wv"], SL * k + s + 1)
                            if k < STEPS - 1:
                                act.mul(t["c"][:], t["wv"][:], 3.25).then_inc(S["c0"], 1)
                                act.wait_ge(S["a_ps"], SL * k + s + 1)
                                act.copy(t["a"][:], tiles(b0[s], PAIRS, LM)).then_inc(S["a"], 1)
                            else:
                                act.mul(t["c"][:, :, 0:HD], t["wv"][:, :, LR:LM], 3.25 / SC).then_inc(S["c0"], 1)
                    for name in ("oT", "yT"):
                        for s in range(SL):
                            act.wait_ge(S[name + "_ps"], s + 1)
                            turned(act, b0[s], T[s]["oT0"], T[s]["oT1"]).then_inc(S[name], 1)

                @block.tensor
                def _(pe):
                    flat = lambda a: a[:].rearrange("p a j -> p (a j)")
                    for s in range(SL):
                        pe.wait_ge(S["xn"], s + 1)
                        turn(pe, G, T[s]["xn"], b0[s]).then_inc(S["xT_ps"], 1)
                    for s in range(SL):
                        pe.wait_ge(S["xT"], s + 1)
                        queries_keys_values(pe, wqkv0, wqkv1, T[s], b1[s], b0[s]).then_inc(S["qk_ps"], 1)
                    for s in range(SL):
                        t = T[s]
                        pe.wait_ge(S["mk"], s + 1)
                        pe.wait_ge(S["v"], s + 1)
                        pe.matmul(b0[s][0:N, 0:8 * LR], t["qk0"][:, 0, :], flat(t["mk0"]), start=True, stop=True)
                        pe.matmul(b1[s][0:N, 0:4 * LR], t["qk1"][:, 0, :], flat(t["mk1"]), start=True,
                                  stop=True).then_inc(S["s1_ps"], 1)
                    for s in range(SL):
                        t = T[s]
                        pe.wait_ge(S["mq"], s + 1)
                        pe.wait_ge(S["s1_shift"], s + 1)
                        for p in range(PAIRS):
                            bk = b0[s] if p < 3 else b1[s]
                            mm = pe.matmul(bk[:, (p % 3) * N:(p % 3 + 1) * N], pair_query(t, p),
                                           (t["qk0"] if p < 4 else t["qk1"])[:, 1, :], start=True, stop=True)
                        mm.then_inc(S["s3_ps"], 1)
                    for s in range(SL):
                        t = T[s]
                        pe.wait_ge(S["p1"], s + 1)
                        pe.wait_ge(S["s3_exp"], s + 1)
                        for p in range(PAIRS):
                            mm = pe.transpose((b0 if p < 4 else b1)[s][:, (p % 4) * N:(p % 4 + 1) * N],
                                              t["p1"][:, 2 * p:2 * p + 2, :].rearrange("p a j -> p (a j)"),
                                              G.ident[0:N, 0:N])
                        mm.then_inc(S["p1T_ps"], 1)
                    for s in range(SL):
                        t = T[s]
                        pe.wait_ge(S["p1T"], s + 1)
                        for p in range(PAIRS):
                            mm = pe.transpose((b0 if p < 4 else b1)[s][0:N, (p % 4) * 128:(p % 4 + 1) * 128],
                                              t["p3"][:, p, :], G.ident[:, :])
                        mm.then_inc(S["p3T_ps"], 1)
                    for s in range(SL):
                        t = T[s]
                        pe.wait_ge(S["p3T"], s + 1)
                        for p in range(PAIRS):
                            mm = pe.matmul(b0[s][:, p * 2 * HD:(p + 1) * 2 * HD], t["p3T"][:, p, :],
                                           t["v"][:, p * 2 * HD:(p + 1) * 2 * HD], start=True, stop=True)
                        mm.then_inc(S["r_ps"], 1)
                    for s in range(SL):
                        pe.wait_ge(S["xr"], s + 1)
                        each_head(pe, T[s]["xr"], T[s]["xr"], b1[s], 0, LM).then_inc(S["w0_ps"], 1)
                    for k in range(STEPS - 1):
                        for s in range(SL):
                            t = T[s]
                            pe.wait_ge(S["wv"], SL * k + s + 1)
                            each_head(pe, t["wv"], t["wv"], b0[s], 0, LM).then_inc(S["a_ps"], 1)
                        for s in range(SL):
                            t = T[s]
                            pe.wait_ge(S["g"], SL * k + s + 1)
                            each_head(pe, t["a"], t["g"], b1[s], 0, LM).then_inc(S["n_ps"], 1)
                    for s in range(SL):
                        pe.wait_ge(S["wv"], SL * (STEPS - 1) + s + 1)
                        each_head(pe, T[s]["wv"], T[s]["wv"], b0[s], LR, LM).then_inc(S["va_ps"], 1)
                    for s in range(SL):
                        pe.wait_ge(S["vg"], s + 1)
                        each_head(pe, T[s]["wv"], T[s]["g"], b1[s], 0, HD).then_inc(S["va_ps"], 1)
                    for s in range(SL):
                        pe.wait_ge(S["vh"], s + 1)
                        each_head(pe, T[s]["wv"], T[s]["g"], b0[s], HD, 2 * HD).then_inc(S["va_ps"], 1)
                    for s in range(SL):
                        t = T[s]
                        pe.wait_ge(S["zr"], s + 1)
                        for p in range(PAIRS):
                            mm = pe.matmul(b1[s][0:N, p * 2 * HD:(p + 1) * 2 * HD], t["p1T"][:, p, :],
                                           t["zr"][:, p, :], start=True, stop=True)
                        mm.then_inc(S["o_ps"], 1)
                    for s in range(SL):
                        pe.wait_ge(S["o"], s + 1)
                        turn(pe, G, T[s]["o"], b0[s]).then_inc(S["oT_ps"], 1)
                    for s in range(SL):
                        t = T[s]
                        pe.wait_ge(S["oT"], s + 1)
                        pe.matmul(b1[s][0:N, 0:D], t["oT0"][:], wo0[:], start=True, stop=False)
                        pe.matmul(b1[s][0:N, 0:D], t["oT1"][:], wo1[:], start=False, stop=True).then_inc(S["y_ps"], 1)
                    for s in range(SL):
                        pe.wait_ge(S["yn"], s + 1)
                        turn(pe, G, T[s]["xn"], b0[s]).then_inc(S["yT_ps"], 1)
                    for s in range(SL):
                        t = T[s]
                        pe.wait_ge(S["yT"], s + 1)
                        pe.matmul(b1[s][0:N, 0:E], t["oT0"][:], sw0[:], start=True, stop=False)
                        pe.matmul(b1[s][0:N, 0:E], t["oT1"][:], sw1[:], start=False, stop=True).then_inc(S["lg_ps"], 1)
            clear(nc, sems)


class Shared:
    pass


def build(nc, img, pw, plg, plb, pb, txt, a0, f0, a1, f1, out):
    h0 = nc.dram_tensor("h0", [B * NP_TOK, D], F32).ap()
    xs = [nc.dram_tensor(f"xs{i}", [SLOTS, HC], F32).ap() for i in range(2)]
    xd = nc.dram_tensor("landmark_x", [B, 128, (H // 2) * LM], F32).ap()
    h2 = nc.dram_tensor("h2", [NT, D], F32).ap()
    with ExitStack() as ctx:
        sb, sem = allocator(nc, ctx)
        G = Shared()
        G.ps = [ctx.enter_context(nc.psum_tensor(f"bank{i}", [128, 512], F32)) for i in range(8)]
        G.ident, G.ones, G.before = sb("ident", [128, 128]), sb("ones", [128, 128]), sb("before", [128, 128])
        G.half = sb("minus_half", [128, 1])
        G.rows_sent = [sem(f"rows_sent{i}") for i in range(2)]
        G.rows_out = [sem(f"rows_out{i}") for i in range(2)]
        G.h = sb("h", [N, B, HC])
        G.lg = sb("logits", [N, E, B])
        G.expert = sb("expert", [1, BLOCKS], I32)
        set_a, set_b, set_c, zeroed = sem("set_a"), sem("set_b"), sem("set_c"), sem("zeroed")
        with ExitStack() as part1:
            empty = part1.enter_context(nc.sbuf_tensor("empty", [TW, BLOCKS, HC], F32))
            past_i = part1.enter_context(nc.sbuf_tensor("past", [TW, BLOCKS], I32))
            with nc.Block() as block:
                @block.vector
                def _(dve):
                    dve.memset(G.ones[:], 1.0).then_inc(set_a, 1)
                    dve.memset(G.half[:], -0.5)
                    dve.memset(G.h[:, :, D:HC], 0.0)
                    dve.memset(empty[:], 0.0).then_inc(set_a, 1)
                    dve.wait_ge(set_a, 2)
                    dve.wait_ge(set_b, 3)
                    dve.tensor_copy(empty[:, :, TOK], past_i[:]).then_inc(set_c, 1)

                @block.gpsimd
                def _(pool):
                    pool.iota(past_i[:], [[0, BLOCKS]], base=NT + 8, channel_multiplier=1).then_inc(set_b, 1)
                    pool.wait_ge(set_a, 1)
                    pool.affine_select(out=G.ident[:], in_=G.ones[:], compare_op=ALU.is_equal, fill=0.0, base=0,
                                       pattern=[[-1, 128]], channel_multiplier=1).then_inc(set_b, 1)
                    pool.affine_select(out=G.before[:], in_=G.ones[:], compare_op=ALU.is_gt, fill=0.0, base=0,
                                       pattern=[[1, 128]], channel_multiplier=-1).then_inc(set_b, 1)

                @block.sync
                def _(sp):
                    sp.wait_ge(set_c, 1)
                    for x in xs:
                        sp.dma_start(x.rearrange("(j p) c -> p j c", p=TW), empty[:]).then_inc(zeroed, 16)
                    sp.wait_ge(zeroed, 32)
            clear(nc, [set_a, set_b, set_c, zeroed])
        patch_embedding(nc, G, img, pw, plg, plb, pb, txt, h0)
        load_tokens(nc, G, h0, txt, None)
        talking_attention(nc, G, a0)
        with ExitStack() as layer:
            weights = ExpertWeights(nc, layer, 0, f0)
            route(nc, G, xs[0], 0, weights)
            experts(nc, G, xs[0], h2, weights, 0)
        reload_tokens(nc, G, h2)
        landmark_attention(nc, G, a1, xd)
        with ExitStack() as layer:
            weights = ExpertWeights(nc, layer, 1, f1)
            route(nc, G, xs[1], 1, weights)
            experts(nc, G, xs[1], out, weights, 1)


def kernel(**inputs):
    import numpy as np
    import concourse.bacc as _bacc
    from concourse.bass_utils import run_bass_kernel_spmd as _run

    I = {k: np.ascontiguousarray(v) for k, v in inputs.items()}
    xp = np.pad(I["x"], ((0, 0), (0, 0), (1, 1), (1, 1)))
    c = slice(1, -1)
    shifts = [xp[:, :, c, c], xp[:, :, c, :-2], xp[:, :, c, 2:], xp[:, :, :-2, c], xp[:, :, 2:, c]]
    xc = np.concatenate(shifts, axis=1).reshape(B, VAR_CH, GRID, PATCH, IMG)
    img = np.ascontiguousarray(xc.transpose(1, 3, 0, 2, 4)).reshape(VAR_CH * PATCH, B * GRID * IMG)
    feat = lambda a: np.ascontiguousarray(a.reshape(PATCH, PATCH, VAR_CH, -1).transpose(2, 0, 1, 3))
    rootw = np.tile(np.where(np.arange(LM) == LR - 1, ZL ** 0.5, 1.0), 2).astype(np.float32)
    real = np.tile(np.arange(LM) < LR, 2)
    mix = np.zeros((H * MC + 1, H, MC), np.float32)
    for m in range(MC):
        mix[m:H * MC:MC, :, m] = I["L0_attn_proj_w_w"].T
    mix[H * MC] = np.repeat(I["L0_attn_proj_w_b"], MC).reshape(H, MC)
    mix = mix.reshape(H * MC + 1, H * MC)
    a = {
        "img": img,
        "pw": feat(I["L0_tok_w"]).reshape(VAR_CH * PATCH, PATCH, D),
        "plg": feat(I["L0_tok_ln_gamma"]).reshape(VAR_CH * PATCH, PATCH),
        "plb": feat(I["L0_tok_ln_beta"]).reshape(VAR_CH * PATCH, PATCH),
        "pb": I["L0_tok_b"][None],
        "txt": I["txt"],
        "a0_wqkv": I["L0_attn_qkv_w"].T,
        "a0_wl": np.repeat(I["L0_attn_proj_l_w"].T, HD, axis=0),
        "a0_lb": I["L0_attn_proj_l_b"][None],
        "a0_mix": mix,
        "a0_lamb": np.repeat(I["L0_attn_lamb"], HD)[None],
        "a0_wo": np.concatenate([I["L0_attn_proj_out_w"].T, I["L0_attn_proj_out_b"][None]]),
        "a0_sw": np.concatenate([I["L0_ffn_switch_w"], I["L0_ffn_switch_b"][None]]),
        "f0_w1": np.concatenate([I["L0_ffn_w1"], I["L0_ffn_b1"][:, None]], axis=1),
        "f0_w2": I["L0_ffn_w2"],
        "f0_b2": I["L0_ffn_b2"].reshape(1, -1),
        "a1_wqkv": I["L1_attn_w_qkv"].T,
        "a1_wo": np.concatenate([I["L1_attn_w_proj"].T, I["L1_attn_b_proj"][None]]),
        "a1_head": np.kron(np.eye(8), np.ones((HD, 1))).astype(np.float32),
        "a1_rootw": rootw.reshape(-1, 1),
        "a1_colw": (np.kron(np.eye(2), np.ones((LM, 1))) * (rootw * real).reshape(-1, 1)).astype(np.float32),
        "a1_sw": np.concatenate([I["L1_ffn_gate_w"], I["L1_ffn_gate_b"][None]]),
        "f1_w1": np.concatenate([I["L1_ffn_w1"], I["L1_ffn_b1"][:, None]], axis=1),
        "f1_w2": I["L1_ffn_w2"],
        "f1_b2": I["L1_ffn_b2"].reshape(1, -1),
    }
    nc = _bacc.Bacc("TRN2", target_bir_lowering=False, num_devices=1)
    arrays, t = {}, {}
    for k, v in a.items():
        v = np.ascontiguousarray(v)
        arrays[k] = v
        t[k] = nc.dram_tensor(k, v.shape, mybir.dt.from_np(v.dtype), kind="ExternalInput").ap()
    out = nc.dram_tensor("out", (NT, D), F32, kind="ExternalOutput").ap()
    sub = lambda p: {k[3:]: v for k, v in t.items() if k.startswith(p + "_")}
    build(nc, t["img"], t["pw"], t["plg"], t["plb"], t["pb"], t["txt"], sub("a0"), sub("f0"), sub("a1"), sub("f1"),
          out)
    r = _run(nc, [arrays], core_ids=[0])
    return r.results[0]["out"].reshape(B, N, D)
```

```python
from contextlib import ExitStack

import concourse.bass as bass
from concourse import mybir

F32 = mybir.dt.float32
I32 = mybir.dt.int32
U32 = mybir.dt.uint32
ALU = mybir.AluOpType
ACT = mybir.ActivationFunctionType
AX = mybir.AxisListType

B, CH, IMG, PATCH = 64, 3, 64, 16
GRID = IMG // PATCH
NP_TOK = GRID * GRID
TXT = 77
N = NP_TOK + TXT
NT = B * N
D = 192
D0, D1 = 128, D - 128
H, HD = 12, 16
SCALE = HD ** -0.5
EPS = 1e-5
VAR_CH = 5 * CH
PD = PATCH * PATCH * VAR_CH
KA = 128
KB = VAR_CH * PATCH - KA
E, F = 8, 768
CAP = int(1.25 * NT / E)
LM = 64
PADS = (-N) % LM
NP = N + PADS
ZL = PADS // 2
LR = LM - ZL + 1
TW = 128
BLOCKS = (NT + E * (TW - 1)) // TW
HC = 196
GATE = 192
SL = 4
MC = 8
FH = F // 2
FT = F // 128


def clear(nc, sems):
    nums = sorted(s.num for s in sems)
    cuts = [0] + [i for i in range(1, len(nums)) if nums[i] != nums[i - 1] + 1] + [len(nums)]
    runs = [range(nums[a], nums[b - 1] + 1) for a, b in zip(cuts, cuts[1:])]
    for run in runs[1:]:
        nc.gpsimd.sem_clear(run)
    nc.all_engine_barrier(sems_to_clear=runs[0])


class Chain:

    def __init__(self, eng, sem):
        self.eng, self.sem, self.n = eng, sem, 0

    def __call__(self, ins):
        self.n += 1
        ins.then_inc(self.sem, 1)
        self.eng.wait_ge(self.sem, self.n)


def norm_stats(dve, link, x, st, mv, rows, done):
    link(dve.bn_stats(st[0:rows, :], x))
    link(dve.bn_aggr(mv[0:rows, 0:2], st[0:rows, :]))
    dve.tensor_scalar(mv[0:rows, 1:2], mv[0:rows, 1:2], EPS, None, ALU.add).then_inc(done, 1)


def norm_rstd(pool, G, mv, rows, done):
    pool.tensor_tensor(mv[0:rows, 2:3], mv[0:rows, 1:2], G.half[0:rows, :], ALU.pow).then_inc(done, 1)


def norm_apply(dve, x, out, mv, rows):
    return dve.tensor_scalar(out, x, mv[0:rows, 0:1], mv[0:rows, 2:3], ALU.subtract, ALU.mult)


def turn(pe, G, src, bk, at=0):
    pe.transpose(bk[:, at:at + N], src[:, 0:D0], G.ident[0:N, 0:N])
    return pe.transpose(bk[0:D1, at + N:at + 2 * N], src[:, D0:D], G.ident[0:N, 0:N])


def turned(act, bk, o0, o1, at=0):
    act.copy(o0[:], bk[:, at:at + N])
    return act.copy(o1[0:D1, :], bk[0:D1, at + N:at + 2 * N])


def padded_row(G, it, s, ahead):
    return G.h_all[:, bass.ds(it * SL + (s + SL + ahead * SL), 1), 0:D].rearrange("p a d -> p (a d)")


def queries_keys(pe, w0, w1, x0, x1, banks, done):
    for m, (a, n) in enumerate(((0, D0), (D0, D1))):
        for j in range(2):
            o = banks[2 * m + j][0:n, 0:SL * N]
            pe.matmul(o, w0[:, j * D + a:j * D + a + n], x0[:].rearrange("p s n -> p (s n)"), start=True, stop=False)
            pe.matmul(o, w1[:, j * D + a:j * D + a + n], x1[:].rearrange("p s n -> p (s n)"), start=False,
                      stop=True).then_inc(done, 1)


def queries_keys_out(act, q0, q1, banks, ready, done):
    for i in range(4):
        act.wait_ge(ready, i + 1)
        o = q0[:, i, :, :] if i < 2 else q1[0:D1, i - 2, :, :]
        act.copy(o.rearrange("p s n -> p (s n)"), banks[i][0:(D0, D1)[i // 2], 0:SL * N]).then_inc(done, 1)


def queries_keys_values(pe, w0, w1, t, qk, v):
    for m, (a, n) in enumerate(((0, D0), (D0, D1))):
        for j in range(2):
            o = qk[0:n, (2 * m + j) * N:(2 * m + j + 1) * N]
            pe.matmul(o, w0[:, j * D + a:j * D + a + n], t["xT0"][:], start=True, stop=False)
            pe.matmul(o, w1[:, j * D + a:j * D + a + n], t["xT1"][:], start=False, stop=True)
    pe.matmul(v[0:N, 0:D], t["xT0"][:], w0[:, 2 * D:3 * D], start=True, stop=False)
    return pe.matmul(v[0:N, 0:D], t["xT1"][:], w1[:, 2 * D:3 * D], start=False, stop=True)


def allocator(nc, ctx):
    def sb(name, shape, dt=F32):
        return ctx.enter_context(nc.sbuf_tensor(name, shape, dt))

    def sem(name):
        return ctx.enter_context(nc.semaphore(name))
    return sb, sem


def patch_embedding(nc, G, img, w_dram, lg_dram, lb_dram, b_dram, txt, h0):
    NG, GB = B // 8, 8
    PER = 4
    with ExitStack() as ctx:
        sb, sem = allocator(nc, ctx)
        wa, wb = sb("pe_wa", [KA, PATCH, D]), sb("pe_wb", [KB, PATCH, D])
        ga, gb = sb("pe_ga", [KA, PATCH]), sb("pe_gb", [KB, PATCH])
        ba, bb = sb("pe_ba", [KA, PATCH]), sb("pe_bb", [KB, PATCH])
        wga, wgb = sb("pe_wga", [KA, PATCH, D + 1]), sb("pe_wgb", [KB, PATCH, D + 1])
        suma, sumb = sb("pe_suma", [KA, 2, D + 1]), sb("pe_sumb", [KB, 2, D + 1])
        bias = sb("pe_bias", [1, D])
        gsum, csum = sb("pe_gsum", [128, D + 1]), sb("pe_csum", [128, D])
        xa = [sb(f"pe_xa{i}", [KA, GB * GRID * IMG]) for i in range(PER)]
        xb = [sb(f"pe_xb{i}", [KB, GB * GRID * IMG]) for i in range(PER)]
        sq = sb("pe_sq", [128, GB * GRID * IMG])
        sqa = [sb(f"pe_sqa{i}", [KA, 128]) for i in range(PER)]
        sqb = [sb(f"pe_sqb{i}", [KB, 128]) for i in range(PER)]
        mom = [sb(f"pe_mom{i}", [128, 8]) for i in range(PER)]
        ho = [sb(f"pe_ho{i}", [128, D]) for i in range(PER)]
        loaded, scaled, wsum, ones_ps, acted = (sem(f"pe_{n}") for n in ("loaded", "scaled", "wsum", "ones_ps", "csum"))
        pre = [loaded, scaled, wsum, ones_ps, acted]
        chain = sem("pe_chain")
        pre.append(chain)
        sq_done, sq_summed, acc_ps, var_done, rstd_done, h_done, stored = (
            sem(f"pe_{n}") for n in ("sq_done", "sq_summed", "acc_ps", "var_done", "rstd_done", "h_done", "stored"))
        img_in = [sem(f"pe_img_in{i}") for i in range(PER)]
        body = [sq_done, sq_summed, acc_ps, var_done, rstd_done, h_done, stored] + img_in
        with nc.Block() as block:
            @block.sync
            def _(sp):
                for dst, src in ((wa, w_dram[0:KA]), (wb, w_dram[KA:KA + KB]), (ga, lg_dram[0:KA]),
                                 (gb, lg_dram[KA:KA + KB]), (ba, lb_dram[0:KA]), (bb, lb_dram[KA:KA + KB])):
                    sp.dma_start(dst[:], src).then_inc(loaded, 16)
                sp.dma_start(bias[:], b_dram).then_inc(loaded, 16)

            @block.vector
            def _(dve):
                link = Chain(dve, chain)
                dve.wait_ge(loaded, 16 * 7)
                link(dve.memset(wga[:, :, D:D + 1], 1.0))
                link(dve.memset(wgb[:, :, D:D + 1], 1.0))
                for w, g, o, k, be, s in ((wa, ga, wga, KA, ba, suma), (wb, gb, wgb, KB, bb, sumb)):
                    link(dve.tensor_tensor(o[:, :, 0:D], w[:], g[:].unsqueeze(2).broadcast_to([k, PATCH, D]), ALU.mult))
                    link(dve.tensor_reduce(s[:, 0, :], o[:].rearrange("p f e -> p e f"), AX.X, ALU.add))
                    link(dve.tensor_tensor(w[:], w[:], be[:].unsqueeze(2).broadcast_to([k, PATCH, D]), ALU.mult))
                    link(dve.tensor_reduce(s[:, 1, 0:D], w[:].rearrange("p f e -> p e f"), AX.X, ALU.add))
                dve.tensor_copy(mom[0][:, 7:8], G.ones[:, 0:1]).then_inc(scaled, 1)
                dve.wait_ge(ones_ps, 1)
                dve.tensor_copy(gsum[:], G.ps[0][:, 0:D + 1])
                dve.tensor_copy(csum[:], G.ps[1][:, 0:D]).then_inc(acted, 1)
                dve.wait_ge(acted, 1)

            @block.tensor
            def _(pe):
                pe.wait_ge(scaled, 1)
                pe.matmul(G.ps[0][:, 0:D + 1], G.ones[0:KA, :], suma[:, 0, :], start=True, stop=False)
                pe.matmul(G.ps[0][:, 0:D + 1], G.ones[0:KB, :], sumb[:, 0, :], start=False, stop=True)
                pe.matmul(G.ps[1][:, 0:D], G.ones[0:KA, :], suma[:, 1, 0:D], start=True, stop=False)
                pe.matmul(G.ps[1][:, 0:D], G.ones[0:KB, :], sumb[:, 1, 0:D], start=False, stop=False)
                pe.matmul(G.ps[1][:, 0:D], G.ones[0:1, :], bias[:], start=False, stop=True).then_inc(ones_ps, 1)
        clear(nc, pre)
        with nc.Fori(0, NG // PER) as it:
            with nc.Block() as block:
                @block.sync
                def _(sp):
                    for s in range(PER):
                        at = bass.ds((it * PER + s) * (GB * GRID * IMG), GB * GRID * IMG)
                        sp.dma_start(xa[s][:], img[0:KA, at]).then_inc(img_in[s], 16)
                        sp.dma_start(xb[s][:], img[KA:KA + KB, at]).then_inc(img_in[s], 16)
                    for s in range(PER):
                        sp.wait_ge(h_done, s + 1)
                        sp.dma_start(h0[bass.ds((it * PER + s) * 128, 128), :], ho[s][:]).then_inc(stored, 16)
                    sp.wait_ge(stored, 16 * PER)

                @block.scalar
                def _(act):
                    for s in range(PER):
                        act.wait_ge(img_in[s], 32)
                        for t, (x, k) in enumerate(((xa[s], KA), (xb[s], KB))):
                            if s or t:
                                act.wait_ge(sq_summed, 2 * s + t)
                            act.activation(sq[0:k, :], x[:], ACT.Square).then_inc(sq_done, 1)

                @block.vector
                def _(dve):
                    link = Chain(dve, chain)
                    for s in range(PER):
                        for t, (o, k) in enumerate(((sqa[s], KA), (sqb[s], KB))):
                            dve.wait_ge(sq_done, 2 * s + t + 1)
                            dve.tensor_reduce(o[:], sq[0:k, :].rearrange("p (t f) -> p t f", f=PATCH), AX.X,
                                              ALU.add).then_inc(sq_summed, 1)
                        m, acc = mom[s], G.ps[s]
                        dve.wait_ge(acc_ps, s + 1)
                        link(dve.tensor_scalar(m[:, 0:1], acc[:, D:D + 1], 1.0 / PD, None, ALU.mult))
                        link(dve.tensor_tensor(m[:, 1:2], m[:, 0:1], m[:, 0:1], ALU.mult))
                        link(dve.tensor_scalar(m[:, 2:3], G.ps[4 + s][:, 0:1], 1.0 / PD, m[:, 1:2], ALU.mult, ALU.subtract))
                        link(dve.tensor_scalar(m[:, 2:3], m[:, 2:3], EPS, None, ALU.add))
                        dve.tensor_scalar(m[:, 4:5], m[:, 0:1], -1.0, None, ALU.mult).then_inc(var_done, 1)
                        dve.wait_ge(var_done, s + 1)
                        link(dve.scalar_tensor_tensor(ho[s][:], gsum[:, 0:D], m[:, 4:5], acc[:, 0:D], ALU.mult, ALU.add))
                        dve.wait_ge(rstd_done, s + 1)
                        dve.scalar_tensor_tensor(ho[s][:], ho[s][:], m[:, 3:4], csum[:], ALU.mult,
                                                 ALU.add).then_inc(h_done, 1)

                @block.gpsimd
                def _(pool):
                    for s in range(PER):
                        pool.wait_ge(var_done, s + 1)
                        pool.tensor_tensor(mom[s][:, 3:4], mom[s][:, 2:3], G.half[:], ALU.pow).then_inc(rstd_done, 1)

                @block.tensor
                def _(pe):
                    for s in range(PER):
                        pe.wait_ge(img_in[s], 32)
                        va = xa[s][:].rearrange("p (t f) -> p f t", f=PATCH)
                        vb = xb[s][:].rearrange("p (t f) -> p f t", f=PATCH)
                        for f in range(PATCH):
                            pe.matmul(G.ps[s][:, 0:D + 1], va[:, f, :], wga[:, f, :], start=(f == 0), stop=False)
                            pe.matmul(G.ps[s][:, 0:D + 1], vb[:, f, :], wgb[:, f, :], start=False,
                                      stop=(f == PATCH - 1))
                        pe.wait_ge(sq_summed, 2 * s + 2)
                        pe.matmul(G.ps[4 + s][:, 0:1], sqa[s][:], G.ones[0:KA, 0:1], start=True, stop=False)
                        pe.matmul(G.ps[4 + s][:, 0:1], sqb[s][:], G.ones[0:KB, 0:1], start=False,
                                  stop=True).then_inc(acc_ps, 1)
            clear(nc, [chain] + body)


def last_logits(nc, G, T, sw0, sw1, S):
    with nc.Block() as block:
        @block.vector
        def _(dve):
            link = Chain(dve, S["dve_chain"])
            for s in range(SL):
                norm_stats(dve, link, G.h[:, B - SL + s, 0:D], T[s]["st"], T[s]["mv"], N, S["var"])
            for s in range(SL):
                dve.wait_ge(S["rstd"], s + 1)
                norm_apply(dve, G.h[:, B - SL + s, 0:D], T[s]["xn"][:], T[s]["mv"], N).then_inc(S["yn"], 1)
            for s in range(SL):
                dve.wait_ge(S["lg_ps"], s + 1)
                dve.tensor_copy(G.lg[:, :, B - SL + s], G.ps[2 * s + 1][0:N, 0:E])

        @block.gpsimd
        def _(pool):
            for s in range(SL):
                pool.wait_ge(S["var"], s + 1)
                norm_rstd(pool, G, T[s]["mv"], N, S["rstd"])

        @block.scalar
        def _(act):
            for s in range(SL):
                act.wait_ge(S["yT_ps"], s + 1)
                turned(act, G.ps[2 * s], T[s]["oT0"], T[s]["oT1"]).then_inc(S["yT"], 1)

        @block.tensor
        def _(pe):
            for s in range(SL):
                pe.wait_ge(S["yn"], s + 1)
                turn(pe, G, T[s]["xn"], G.ps[2 * s]).then_inc(S["yT_ps"], 1)
            for s in range(SL):
                pe.wait_ge(S["yT"], s + 1)
                pe.matmul(G.ps[2 * s + 1][0:N, 0:E], T[s]["oT0"][:], sw0[:], start=True, stop=False)
                pe.matmul(G.ps[2 * s + 1][0:N, 0:E], T[s]["oT1"][:], sw1[:], start=False, stop=True)\
                  .then_inc(S["lg_ps"], 1)
    clear(nc, list(S.values()))


def talking_attention(nc, G, A, token_rows):
    NC = -(-N // MC)
    NM = NC * MC
    R = H * MC
    GROUPS = ((0, 5), (5, 10), (10, 12))
    assert NC == H
    with ExitStack() as ctx:
        sb, sem = allocator(nc, ctx)
        names = ("var", "rstd", "xn", "xT_ps", "xT", "qk_ps", "v_ps", "qk", "v", "qs0", "qs1", "s_ps", "negmax", "exp", "p",
                 "c_ps", "c", "m_ps", "m", "aT_ps", "aT", "uT_ps", "uT", "u_ps", "u", "r_ps", "o", "y_ps", "yn",
                 "yT_ps", "yT", "lg_ps", "dve_chain", "weights_in", "rows_in", "ready")
        S = {n: sem("l0_" + n) for n in names}
        wqkv0, wqkv1 = sb("l0_wqkv0", [D0, 3 * D]), sb("l0_wqkv1", [D1, 3 * D])
        wl0, wl1 = sb("l0_wl0", [D0, H]), sb("l0_wl1", [D1, H])
        lbias = sb("l0_lbias", [D1 + 1, H])
        mix = sb("l0_mixs", [R + 1, R])
        lam = sb("l0_lam", [128, H // 4])
        c1, c2 = sb("l0_c1", [128, H // 4]), sb("l0_c2", [128, H // 4])
        wo, wob = sb("l0_wo", [128, H // 4, D]), sb("l0_wob", [N, D])
        sw0, sw1 = sb("l0_sw0", [D0, E]), sb("l0_sw1", [D1 + 1, E])
        xT0, xT1 = sb("l0_xT0", [D0, SL, N]), sb("l0_xT1", [D1, SL, N])
        qk0, qk1 = sb("l0_qk0", [D0, 2, SL, N]), sb("l0_qk1", [D1 + 1, 2, SL, N])
        T = []
        for s in range(SL):
            t = {}
            for n, shape in (("st", [N, 6]), ("mv", [N, 3]), ("xn", [N, D]), ("v", [N, D]),
                             ("qs0", [D0, H, N]), ("qs1", [D1 + 1, H, N]), ("nm", [N, H]), ("rs", [N, H]),
                             ("p", [N, H, NM]), ("c", [R + 1, NC, N]), ("m", [N, H, NM]), ("aT", [NM, H, N]),
                             ("uT", [128, H // 4, N]), ("u", [N, H // 4, 128]), ("oT", [128, H // 4, N]), ("oT0", [D0, N]), ("oT1", [D1 + 1, N])):
                t[n] = sb(f"l0_{n}_{s}", shape)
            t["xT0"], t["xT1"], t["qk0"], t["qk1"] = xT0[:, s, :], xT1[:, s, :], qk0[:, :, s, :], qk1[:, :, s, :]
            T.append(t)
        b0, b1 = [G.ps[2 * s] for s in range(SL)], [G.ps[2 * s + 1] for s in range(SL)]
        with nc.Block() as block:
            @block.sync
            def _(sp):
                lots = ((wqkv0[:], A["wqkv"][0:D0]), (wqkv1[:], A["wqkv"][D0:D]), (wl0[:], A["wl"][0:D0]),
                        (wl1[:], A["wl"][D0:D]), (lbias[D1:D1 + 1, :], A["lb"]), (mix[:], A["mix"]),
                        (lam[:], A["lamb"]), (wo[:].rearrange("p c d -> p (c d)"), A["wo"]),
                        (wob[:], A["wob"].broadcast_to([N, D])),
                        (sw0[:], A["sw"][0:D0]), (sw1[:], A["sw"][D0:D + 1]))
                for dst, src in lots:
                    sp.dma_start(dst, src).then_inc(S["weights_in"], 16)
                for dst, src in token_rows:
                    sp.dma_start(dst, src).then_inc(S["rows_in"], 16)
                sp.wait_ge(S["rows_in"], 16 * len(token_rows))

            @block.vector
            def _(dve):
                dve.memset(qk1[D1:D1 + 1, :, :, :], 1.0)
                for bank in G.ps:
                    dve.memset(bank[:], 0.0)
                for s in range(SL):
                    t = T[s]
                    dve.memset(t["oT1"][D1:D1 + 1, :], 1.0)
                    dve.memset(t["c"][R:R + 1, :, :], 1.0)
                    dve.memset(t["p"][:, :, N:NM], 0.0)
                dve.wait_ge(S["weights_in"], 16 * 11)
                dve.tensor_scalar(c1[:], lam[:], -2.0, 1.0, ALU.mult, ALU.add)
                dve.tensor_scalar(c2[:], lam[:], 3.0, None, ALU.mult)
                dve.tensor_scalar(wqkv0[:, 0:D], wqkv0[:, 0:D], SCALE, None, ALU.mult)
                dve.tensor_scalar(wqkv1[:, 0:D], wqkv1[:, 0:D], SCALE, None, ALU.mult)
                for s in range(SL):
                    last = dve.tensor_copy(T[s]["qs1"][D1:D1 + 1, :, :],
                                           lbias[D1:D1 + 1, :].unsqueeze(2).broadcast_to([1, H, N]))
                last.then_inc(S["ready"], 1)
                dve.wait_ge(S["ready"], 1)
        clear(nc, list(S.values()))

        def norm_ahead(it, ahead):
            rows = [padded_row(G, it, s, ahead) for s in range(SL)]

            def stats(dve, link, s):
                norm_stats(dve, link, rows[s], T[s]["st"], T[s]["mv"], N, S["var"])

            def apply(dve, s, n):
                dve.wait_ge(S["rstd"], n + s + 1)
                norm_apply(dve, rows[s], T[s]["xn"][:], T[s]["mv"], N).then_inc(S["xn"], 1)
            return stats, apply

        with nc.Block() as block:
            @block.vector
            def _(dve):
                link = Chain(dve, S["dve_chain"])
                stats, apply = norm_ahead(0, 0)
                for s in range(SL):
                    stats(dve, link, s)
                for s in range(SL):
                    apply(dve, s, 0)

            @block.gpsimd
            def _(pool):
                for s in range(SL):
                    pool.wait_ge(S["var"], s + 1)
                    norm_rstd(pool, G, T[s]["mv"], N, S["rstd"])

            @block.tensor
            def _(pe):
                for s in range(SL):
                    pe.wait_ge(S["xn"], s + 1)
                    turn(pe, G, T[s]["xn"], b1[s]).then_inc(S["xT_ps"], 1)

            @block.scalar
            def _(act):
                for s in range(SL):
                    act.wait_ge(S["xT_ps"], s + 1)
                    turned(act, b1[s], T[s]["xT0"], T[s]["xT1"]).then_inc(S["xT"], 1)
        clear(nc, list(S.values()))
        BEHIND, LOGITS = D, 4 * N
        with nc.Fori(0, B // SL) as it:
            hrow = [padded_row(G, it, s, 0) for s in range(SL)]
            before = [padded_row(G, it, s, -1) for s in range(SL)]
            with nc.Block() as block:
                @block.vector
                def _(dve):
                    link = Chain(dve, S["dve_chain"])
                    stats, apply = norm_ahead(it, 1)

                    def negmax(j, s):
                        dve.wait_ge(S["s_ps"], SL * j + s + 1)
                        dve.tensor_reduce(T[s]["nm"][:, 4 * j:4 * j + 4],
                                          (b0, b1, b0)[j][s][0:N, 0:4 * N].rearrange("p (g m) -> p g m", m=N), AX.X,
                                          ALU.max, negate=True).then_inc(S["negmax"], 1)

                    def scaled(j, s):
                        h = slice(4 * j, 4 * j + 4)
                        dve.wait_ge(S["exp"], SL * j + s + 1)
                        link(dve.reciprocal(T[s]["rs"][:, h], T[s]["rs"][:, h]))
                        dve.tensor_tensor(T[s]["p"][:, h, 0:N], T[s]["p"][:, h, 0:N],
                                          T[s]["rs"][:, h].unsqueeze(2).broadcast_to([N, 4, N]), ALU.mult)\
                           .then_inc(S["p"], 1)

                    for s in range(SL):
                        norm_stats(dve, link, before[s], T[s]["st"], T[s]["mv"], N, S["var"])
                    for s in range(SL):
                        dve.wait_ge(S["rstd"], s + 1)
                        norm_apply(dve, before[s], T[s]["xn"][:], T[s]["mv"], N).then_inc(S["yn"], 1)
                    for s in range(SL):
                        t = T[s]
                        dve.wait_ge(S["qk"], 1 if s >= 2 else 3)
                        last = dve.tensor_tensor(t["qs0"][:], t["qk0"][:, 0, :].unsqueeze(1).broadcast_to([D0, H, N]),
                                                 wl0[:].unsqueeze(2).broadcast_to([D0, H, N]), ALU.mult)
                        if s < 2:
                            last = dve.tensor_tensor(t["qs1"][0:D1, :, :],
                                                     t["qk1"][0:D1, 0, :].unsqueeze(1).broadcast_to([D1, H, N]),
                                                     wl1[:].unsqueeze(2).broadcast_to([D1, H, N]), ALU.mult)
                        last.then_inc(S["qs0"], 1)
                    for s in range(SL):
                        dve.wait_ge(S["s_ps"], s + 1)
                        dve.tensor_copy(G.lg_all[:, :, bass.ds(it * SL + s, 1)],
                                        b0[s][0:N, LOGITS:LOGITS + E].unsqueeze(2))
                        negmax(0, s)
                    for j in (1, 2):
                        for s in range(SL):
                            negmax(j, s)
                            scaled(j - 1, s)
                    for s in range(SL):
                        scaled(2, s)
                    for j, (a, b) in enumerate(GROUPS):
                        for s in range(SL):
                            dve.wait_ge(S["m_ps"], SL * j + s + 1)
                            dve.tensor_copy(T[s]["m"][:].rearrange("p h (m c) -> p c (h m)", c=NC)[:, a:b, :],
                                            (b1, b0, b1)[j][s][0:N, 0:(b - a) * R]
                                            .rearrange("p (c r) -> p c r", r=R)).then_inc(S["m"], 1)
                    for s in range(SL):
                        stats(dve, link, s)
                        dve.tensor_tensor(hrow[s], hrow[s], wob[:], ALU.add)
                    for s in range(SL):
                        dve.wait_ge(S["u_ps"], s + 1)
                        dve.tensor_copy(T[s]["u"][:].rearrange("p c e -> p (c e)"), b1[s][0:N, 0:H // 4 * 128])\
                           .then_inc(S["u"], 1)
                    for s in range(SL):
                        apply(dve, s, SL)
                    for s in range(SL):
                        t = T[s]
                        over = lambda c: c[:].unsqueeze(2).broadcast_to([128, H // 4, N])
                        link(dve.tensor_tensor(t["oT"][:], t["uT"][:], over(c1), ALU.mult))
                        dve.wait_ge(S["r_ps"], s + 1)
                        link(dve.tensor_tensor(t["uT"][:], b0[s][:, 0:H // 4 * N].rearrange("p (c n) -> p c n", n=N),
                                               over(c2), ALU.mult))
                        dve.tensor_tensor(t["oT"][:], t["oT"][:], t["uT"][:], ALU.add).then_inc(S["o"], 1)
                    for s in range(SL):
                        dve.wait_ge(S["y_ps"], s + 1)
                        dve.tensor_tensor(hrow[s], hrow[s], b0[s][0:N, 0:D], ALU.add)

                @block.gpsimd
                def _(pool):
                    for s in range(SL):
                        pool.wait_ge(S["var"], s + 1)
                        norm_rstd(pool, G, T[s]["mv"], N, S["rstd"])
                    pool.wait_ge(S["qk"], 3)
                    for s in range(2, SL):
                        t = T[s]
                        pool.tensor_tensor(t["qs1"][0:D1, :, :],
                                           t["qk1"][0:D1, 0, :].unsqueeze(1).broadcast_to([D1, H, N]),
                                           wl1[:].unsqueeze(2).broadcast_to([D1, H, N]), ALU.mult).then_inc(S["qs1"], 1)
                    for s in range(SL):
                        pool.wait_ge(S["var"], SL + s + 1)
                        norm_rstd(pool, G, T[s]["mv"], N, S["rstd"])

                @block.scalar
                def _(act):
                    queries_keys_out(act, qk0, qk1, b1, S["qk_ps"], S["qk"])
                    for s in range(SL):
                        act.wait_ge(S["v_ps"], s + 1)
                        act.copy(T[s]["v"][:], b0[s][0:N, 0:D]).then_inc(S["v"], 1)
                    for s in range(SL):
                        act.wait_ge(S["yT_ps"], s + 1)
                        turned(act, b0[s], T[s]["oT0"], T[s]["oT1"], BEHIND).then_inc(S["yT"], 1)
                    for j in range(3):
                        for s in range(SL):
                            t, bk = T[s], (b0, b1, b0)[j][s]
                            act.wait_ge(S["negmax"], SL * j + s + 1)
                            for g in range(4 * j, 4 * j + 4):
                                last = act.activation(t["p"][:, g, 0:N], bk[0:N, (g % 4) * N:(g % 4 + 1) * N],
                                                      ACT.Exp, bias=t["nm"][:, g:g + 1], accum_out=t["rs"][:, g:g + 1])
                            last.then_inc(S["exp"], 1)
                    for j, (a, b) in enumerate(GROUPS):
                        for s in range(SL):
                            act.wait_ge(S["c_ps"], SL * j + s + 1)
                            act.copy(T[s]["c"][0:R, a:b, :].rearrange("p c n -> p (c n)"),
                                     (b1, b0, b1)[j][s][0:R, 0:(b - a) * N]).then_inc(S["c"], 1)
                    for j, (a, b) in enumerate(GROUPS):
                        for s in range(SL):
                            act.wait_ge(S["aT_ps"], SL * j + s + 1)
                            act.copy(T[s]["aT"][:, a:b, :].rearrange("p c n -> p (c n)"),
                                     (b0, b1, b0)[j][s][0:NM, 0:(b - a) * N]).then_inc(S["aT"], 1)
                    for s in range(SL):
                        act.wait_ge(S["uT_ps"], s + 1)
                        act.copy(T[s]["uT"][:].rearrange("p c n -> p (c n)"), b1[s][:, 0:H // 4 * N]).then_inc(S["uT"], 1)
                    for s in range(SL):
                        act.wait_ge(S["xT_ps"], s + 1)
                        turned(act, b1[s], T[s]["xT0"], T[s]["xT1"]).then_inc(S["xT"], 1)

                @block.tensor
                def _(pe):
                    queries_keys(pe, wqkv0, wqkv1, xT0, xT1, b1, S["qk_ps"])
                    for s in range(SL):
                        t = T[s]
                        pe.matmul(b0[s][0:N, 0:D], t["xT0"], wqkv0[:, 2 * D:3 * D], start=True, stop=False)
                        pe.matmul(b0[s][0:N, 0:D], t["xT1"], wqkv1[:, 2 * D:3 * D], start=False,
                                  stop=True).then_inc(S["v_ps"], 1)
                    for s in range(SL):
                        pe.wait_ge(S["yn"], s + 1)
                        pe.wait_ge(S["v"], s + 1)
                        turn(pe, G, T[s]["xn"], b0[s], BEHIND).then_inc(S["yT_ps"], 1)

                    def scores(j, s):
                        t, bk = T[s], (b0, b1, b0)[j][s]
                        for g in range(4 * j, 4 * j + 4):
                            o = bk[0:N, (g % 4) * N:(g % 4 + 1) * N]
                            pe.matmul(o, t["qs0"][:, g, :], t["qk0"][:, 1, :], start=True, stop=False)
                            mm = pe.matmul(o, t["qs1"][:, g, :], t["qk1"][:, 1, :], start=False, stop=True)
                        mm.then_inc(S["s_ps"], 1)

                    for s in range(SL):
                        t = T[s]
                        pe.wait_ge(S["yT"], s + 1)
                        if s == 0:
                            pe.wait_ge(S["qk"], 4)
                        pe.matmul(b0[s][0:N, LOGITS:LOGITS + E], t["oT0"][:], sw0[:], start=True, stop=False)
                        pe.matmul(b0[s][0:N, LOGITS:LOGITS + E], t["oT1"][:], sw1[:], start=False, stop=True)
                        pe.wait_ge(S["qs0"], s + 1)
                        if s >= 2:
                            pe.wait_ge(S["qs1"], s - 1)
                        scores(0, s)
                    for s in range(SL):
                        scores(1, s)
                    for s in range(SL):
                        pe.wait_ge(S["exp"], s + 1)
                        scores(2, s)
                    for j, (a, b) in enumerate(GROUPS):
                        for s in range(SL):
                            pe.wait_ge(S["p"], 2 * SL + s + 1 if j == 0 else 3 * SL)
                            if j == 2:
                                pe.wait_ge(S["c"], s + 1)
                            for c in range(a, b):
                                mm = pe.transpose((b1, b0, b1)[j][s][0:R, (c - a) * N:(c - a + 1) * N],
                                                  T[s]["p"][:].rearrange("p h (m c) -> p c (h m)", c=NC)[:, c, :],
                                                  G.ident[0:N, 0:N])
                            mm.then_inc(S["c_ps"], 1)
                    for j, (a, b) in enumerate(GROUPS):
                        for s in range(SL):
                            t = T[s]
                            pe.wait_ge(S["c"], 2 * SL + s + 1 if j == 0 else 3 * SL)
                            if j == 2:
                                pe.wait_ge(S["m"], s + 1)
                            for c in range(a, b):
                                mm = pe.matmul((b1, b0, b1)[j][s][0:N, (c - a) * R:(c - a + 1) * R], t["c"][:, c, :],
                                               mix[:], start=True, stop=True)
                            mm.then_inc(S["m_ps"], 1)
                    for j, (a, b) in enumerate(GROUPS):
                        for s in range(SL):
                            t = T[s]
                            pe.wait_ge(S["m"], 2 * SL + s + 1 if j == 0 else 3 * SL)
                            if j == 2:
                                pe.wait_ge(S["aT"], s + 1)
                            for g in range(a, b):
                                mm = pe.transpose((b0, b1, b0)[j][s][0:NM, (g - a) * N:(g - a + 1) * N],
                                                  t["m"][:, g, :], G.ident[0:N, 0:N])
                            mm.then_inc(S["aT_ps"], 1)

                    def applied(t, x, o):
                        for g in range(H):
                            c, j = g // 4, 32 * (g % 4)
                            last = pe.matmul(o[j:j + HD, c * N:(c + 1) * N], x(g), t["aT"][0:N, g, :], start=True,
                                             stop=True)
                        return last

                    for s in range(SL):
                        v = T[s]["v"]
                        pe.wait_ge(S["aT"], 2 * SL + s + 1)
                        applied(T[s], lambda g: v[:, g * HD:(g + 1) * HD], b1[s]).then_inc(S["uT_ps"], 1)
                    for s in range(SL):
                        pe.wait_ge(S["uT"], s + 1)
                        for c in range(H // 4):
                            mm = pe.transpose(b1[s][0:N, c * 128:(c + 1) * 128], T[s]["uT"][:, c, :], G.ident[:, :])
                        mm.then_inc(S["u_ps"], 1)
                    for s in range(SL):
                        u = T[s]["u"]
                        pe.wait_ge(S["u"], s + 1)
                        applied(T[s], lambda g: u[:, g // 4, 32 * (g % 4):32 * (g % 4) + HD], b0[s])\
                            .then_inc(S["r_ps"], 1)
                    for s in range(SL):
                        pe.wait_ge(S["xn"], s + 1)
                        turn(pe, G, T[s]["xn"], b1[s]).then_inc(S["xT_ps"], 1)
                    for s in range(SL):
                        t = T[s]
                        pe.wait_ge(S["o"], s + 1)
                        for c in range(H // 4):
                            mm = pe.matmul(b0[s][0:N, 0:D], t["oT"][:, c, :], wo[:, c, :], start=(c == 0),
                                           stop=(c == H // 4 - 1))
                        mm.then_inc(S["y_ps"], 1)
            clear(nc, list(S.values()))
        last_logits(nc, G, T, sw0, sw1, S)


class ExpertWeights:

    def __init__(self, nc, ctx, layer, W):
        sb, sem = allocator(nc, ctx)
        self.W = W
        self.w1a, self.w1b = sb(f"f{layer}_w1a", [D0, E * F]), sb(f"f{layer}_w1b", [D1 + 1, E * F])
        self.w2 = sb(f"f{layer}_w2s", [128, E * FT * D])
        self.b2 = sb(f"f{layer}_b2s", [1, E * D])
        self.weights_in = sem(f"f{layer}_weights_in")
        self.all_in = 16 * (3 * E + 1)

    def load(self, sp):
        W = self.W
        for e in range(E):
            sp.dma_start(self.w1a[:, e * F:(e + 1) * F], W["w1"][e, 0:D0, :]).then_inc(self.weights_in, 16)
            sp.dma_start(self.w1b[:, e * F:(e + 1) * F], W["w1"][e, D0:D + 1, :]).then_inc(self.weights_in, 16)
            sp.dma_start(self.w2[:, e * FT * D:(e + 1) * FT * D].rearrange("p (c d) -> p c d", d=D),
                         W["w2"][e].rearrange("(c p) d -> p c d", p=128)).then_inc(self.weights_in, 16)
        sp.dma_start(self.b2[:], W["b2"]).then_inc(self.weights_in, 16)


def route(nc, G, rows, layer, weights):
    Q = E * B
    with ExitStack() as ctx:
        sb, sem = allocator(nc, ctx)
        names = ("dve_chain", "dve_to_act", "act_to_dve", "dve_to_pe", "pe_to_dve", "iota", "place", "chunk_ps")
        S = {n: sem(f"r{layer}_" + n) for n in names}
        z, ex, oh, key, t0, t1, rk, ekeep = (sb(f"r{layer}_{n}", [N, E, B]) for n in
                                             ("z", "ex", "oh", "key", "t0", "t1", "rk", "keep"))
        mx, t2, gate, dest = (sb(f"r{layer}_{n}", [N, B]) for n in ("mx", "t2", "gate", "dest"))
        rows_out = sem(f"r{layer}_rows_out")
        CH = 8
        block_1 = sb(f"r{layer}_block_1", [N, BLOCKS])
        place = sb(f"r{layer}_place", [N, TW])
        at_block = sb(f"r{layer}_at_block", [N, B, BLOCKS])
        at_place = [sb(f"r{layer}_at_place{i}", [N, CH, TW]) for i in range(2)]
        tok1, nblk = sb(f"r{layer}_tok1", [N, B]), sb(f"r{layer}_nblk", [N, B])
        table, found, none = (sb(f"r{layer}_{n}", [TW, BLOCKS]) for n in ("table", "found", "none"))
        past, past_i = sb(f"r{layer}_past", [TW, 1]), sb(f"r{layer}_pasti", [TW, 1], I32)
        block_i, place_i = sb(f"r{layer}_blocki", [N, BLOCKS], I32), sb(f"r{layer}_placei", [N, TW], I32)
        tok_i = sb(f"r{layer}_toki", [N, B], I32)
        pref_i = sb(f"r{layer}_prefi", [N, E], I32)
        pref = sb(f"r{layer}_pref", [N, E])
        lo, cand, cnt, few, step = (sb(f"r{layer}_{n}", [N, E]) for n in ("lo", "cand", "cnt", "few", "step"))
        blk, cum, base, start = (sb(f"r{layer}_{n}", [N, E]) for n in ("blk", "cum", "base", "start"))
        full_i, full = sb(f"r{layer}_fulli", [N, E, BLOCKS], I32), sb(f"r{layer}_full", [N, E, BLOCKS])
        bj_i = sb(f"r{layer}_bji", [1, BLOCKS, E], I32)
        bj, bje = sb(f"r{layer}_bj", [1, BLOCKS, E]), sb(f"r{layer}_bje", [1, BLOCKS])
        over_b = lambda a: a[:].unsqueeze(2).broadcast_to([N, E, B])
        over_e = lambda a: a[:].unsqueeze(1).broadcast_to([N, E, B])
        by_b = lambda a: a[:].rearrange("p e b -> p b e")
        flat = lambda a: a[:].rearrange("p e b -> p (e b)")
        counts = {"act": 0, "pe": 0}

        def ranked(dve, link, mask, out):
            counts["pe"] += 1
            dve.nop().then_inc(S["dve_to_pe"], 1)
            dve.wait_ge(S["pe_to_dve"], counts["pe"])
            link(dve.tensor_copy(flat(t1), G.ps[1][0:N, 0:Q]))
            link(dve.tensor_tensor_scan(flat(out), flat(z_ones), flat(t1), 0.0, ALU.mult, ALU.add))
            link(dve.tensor_tensor(out[:], out[:], t1[:], ALU.subtract))
            link(dve.tensor_copy(start[:], out[:, :, 0]))
            link(dve.tensor_tensor(cnt[:], out[:, :, B - 1], t1[:, :, B - 1], ALU.add))
            link(dve.tensor_tensor(cnt[:], cnt[:], start[:], ALU.subtract))
            link(dve.tensor_tensor(out[:], out[:], over_b(start), ALU.subtract))
            link(dve.tensor_tensor(flat(out), flat(out), G.ps[0][0:N, 0:Q], ALU.add))

        z_ones = sb(f"r{layer}_ones", [N, E, B])
        with nc.Block() as block:
            @block.sync
            def _(sp):
                weights.load(sp)

            @block.gpsimd
            def _(pool):
                pool.iota(tok_i[:], [[N, B]], base=1, channel_multiplier=1)
                pool.iota(past_i[:], [[0, 1]], base=NT + 8, channel_multiplier=1)
                pool.iota(block_i[:], [[1, BLOCKS]], base=1, channel_multiplier=0)
                pool.iota(place_i[:], [[1, TW]], base=-TW, channel_multiplier=0)
                pool.iota(pref_i[:], [[-1, E]], base=E, channel_multiplier=0)
                pool.iota(full_i[:], [[0, E], [TW, BLOCKS]], base=0, channel_multiplier=0)
                pool.iota(bj_i[:], [[1, BLOCKS], [0, E]], base=0, channel_multiplier=0).then_inc(S["iota"], 1)

            @block.scalar
            def _(act):
                act.wait_ge(S["dve_to_act"], 1)
                act.activation(flat(ex), flat(z), ACT.Exp).then_inc(S["act_to_dve"], 1)

            @block.vector
            def _(dve):
                link = Chain(dve, S["dve_chain"])
                dve.memset(z_ones[:], 1.0)
                link(dve.tensor_reduce(mx[:], by_b(G.lg), AX.X, ALU.max))
                dve.tensor_tensor(z[:], G.lg[:], over_e(mx), ALU.subtract).then_inc(S["dve_to_act"], 1)
                dve.wait_ge(S["iota"], 1)
                link(dve.tensor_copy(tok1[:], tok_i[:]))
                link(dve.tensor_copy(past[:], past_i[:]))
                link(dve.tensor_copy(block_1[:], block_i[:]))
                link(dve.tensor_copy(place[:], place_i[:]))
                link(dve.tensor_copy(pref[:], pref_i[:]))
                link(dve.tensor_copy(bj[:], bj_i[:]))
                link(dve.tensor_copy(full[:], full_i[:]))
                dve.wait_ge(S["act_to_dve"], 1)
                link(dve.tensor_reduce(t2[:], by_b(ex), AX.X, ALU.add))
                link(dve.reciprocal(gate[:], t2[:]))
                link(dve.tensor_copy(G.h[:, :, GATE], gate[:]))
                link(dve.tensor_scalar(t0[:], ex[:], 1.0, None, ALU.is_ge))
                link(dve.tensor_tensor(t0[:], t0[:], over_b(pref), ALU.mult))
                link(dve.tensor_reduce(t2[:], by_b(t0), AX.X, ALU.max))
                link(dve.tensor_tensor(oh[:], t0[:], over_e(t2), ALU.is_equal))
                link(dve.tensor_tensor(key[:], oh[:], over_e(gate), ALU.mult))
                link(dve.memset(lo[:], 0.0))
                link(dve.memset(step[:], 1.0))
        clear(nc, list(S.values()))
        with nc.Block() as block:
            @block.sync
            def _(sp):
                sp.dma_start(rows.rearrange("(b n) d -> n b d", n=N), G.h).then_inc(rows_out, 16)
        if layer == 0:
            BITS, UNROLL = 28, 7
            with nc.Fori(0, BITS // UNROLL) as it:
                with nc.Block() as block:
                    @block.tensor
                    def _(pe):
                        for j in range(UNROLL):
                            pe.wait_ge(S["dve_to_pe"], j + 1)
                            pe.matmul(G.ps[2][0:N, 0:E], G.ones[0:N, 0:N], few[:], start=True,
                                      stop=True).then_inc(S["pe_to_dve"], 1)

                    @block.vector
                    def _(dve):
                        link = Chain(dve, S["dve_chain"])
                        for j in range(UNROLL):
                            link(dve.tensor_tensor(cand[:], lo[:], step[:], ALU.add))
                            link(dve.tensor_tensor(t0[:], key[:], over_b(cand), ALU.is_ge))
                            dve.tensor_reduce(few[:], t0[:], AX.X, ALU.add).then_inc(S["dve_to_pe"], 1)
                            dve.wait_ge(S["pe_to_dve"], j + 1)
                            link(dve.scalar_tensor_tensor(cnt[:], G.ps[2][0:N, 0:E], float(CAP), step[:], ALU.is_ge,
                                                          ALU.mult))
                            dve.tensor_scalar(step[:], step[:], 0.5, None, ALU.mult)
                            link(dve.tensor_tensor(lo[:], lo[:], cnt[:], ALU.add))
                clear(nc, list(S.values()))
        masks = [oh] if layer else [ekeep, oh]
        with nc.Block() as block:
            @block.tensor
            def _(pe):
                n = 0
                if layer == 0:
                    n += 1
                    pe.wait_ge(S["dve_to_pe"], n)
                    pe.matmul(G.ps[2][0:N, 0:E], G.ones[0:N, 0:N], few[:], start=True, stop=True)\
                        .then_inc(S["pe_to_dve"], 1)
                for m in masks:
                    n += 1
                    pe.wait_ge(S["dve_to_pe"], n)
                    pe.matmul(G.ps[0][0:N, 0:Q], G.before[0:N, 0:N], flat(m), start=True, stop=True)
                    pe.matmul(G.ps[1][0:N, 0:Q], G.ones[0:N, 0:N], flat(m), start=True, stop=True)\
                        .then_inc(S["pe_to_dve"], 1)
                for c in range(B // CH):
                    pe.wait_ge(S["place"], c + 1)
                    for b in range(CH):
                        mm = pe.matmul(G.ps[3][:, 0:BLOCKS], at_place[c % 2][:, b, :], at_block[:, c * CH + b, :],
                                       start=(c == 0 and b == 0), stop=(c == B // CH - 1 and b == CH - 1))
                    mm.then_inc(S["chunk_ps"], 1)

            @block.vector
            def _(dve):
                link = Chain(dve, S["dve_chain"])
                if layer == 0:
                    link(dve.tensor_tensor(t0[:], key[:], over_b(lo), ALU.is_gt))
                    dve.tensor_reduce(few[:], t0[:], AX.X, ALU.add).then_inc(S["dve_to_pe"], 1)
                    counts["pe"] += 1
                    dve.wait_ge(S["pe_to_dve"], counts["pe"])
                    link(dve.tensor_scalar(few[:], G.ps[2][0:N, 0:E], -1.0, float(CAP), ALU.mult, ALU.add))
                    link(dve.tensor_tensor(ekeep[:], key[:], over_b(lo), ALU.is_equal))
                    link(dve.tensor_tensor(ekeep[:], ekeep[:], oh[:], ALU.mult))
                    ranked(dve, link, ekeep, rk)
                    link(dve.tensor_tensor(rk[:], rk[:], over_b(few), ALU.is_lt))
                    link(dve.tensor_tensor(ekeep[:], ekeep[:], rk[:], ALU.mult))
                    link(dve.tensor_tensor(ekeep[:], ekeep[:], t0[:], ALU.add))
                    link(dve.tensor_reduce(gate[:], by_b(ekeep), AX.X, ALU.add))
                    link(dve.tensor_scalar(gate[:], gate[:], 2.0, -1.0, ALU.mult, ALU.add))
                    link(dve.tensor_tensor(tok1[:], tok1[:], gate[:], ALU.mult))
                ranked(dve, link, oh, rk)
                link(dve.tensor_tensor(full[:], cnt[:].unsqueeze(2).broadcast_to([N, E, BLOCKS]),
                                       full[:], ALU.is_gt))
                link(dve.tensor_reduce(blk[:], full[:], AX.X, ALU.add))
                link(dve.tensor_scalar(blk[:], blk[:], float(TW), None, ALU.mult))
                link(dve.tensor_tensor_scan(cum[:], z_ones[:, :, 0], blk[:], 0.0, ALU.mult, ALU.add))
                link(dve.tensor_tensor(base[:], cum[:], blk[:], ALU.subtract))
                link(dve.tensor_tensor(rk[:], rk[:], over_b(base), ALU.add))
                link(dve.tensor_tensor(rk[:], rk[:], oh[:], ALU.mult))
                link(dve.tensor_reduce(dest[:], by_b(rk), AX.X, ALU.add))
                blocks = lambda a: a[:].unsqueeze(1).broadcast_to([N, B, BLOCKS])
                tokens = lambda a: a[:].unsqueeze(2).broadcast_to([N, B, BLOCKS])
                link(dve.tensor_scalar(block_1[:], block_1[:], -1.0, float(TW), ALU.add, ALU.mult))
                link(dve.tensor_tensor(at_block[:], tokens(dest), blocks(block_1), ALU.is_ge))
                link(dve.tensor_scalar(block_1[:], block_1[:], 1.0 / TW, 1.0, ALU.mult, ALU.add))
                link(dve.tensor_reduce(nblk[:], at_block[:], AX.X, ALU.add))
                link(dve.scalar_tensor_tensor(dest[:], nblk[:], -float(TW), dest[:], ALU.mult, ALU.add))
                link(dve.tensor_tensor(at_block[:], tokens(nblk), blocks(block_1), ALU.is_equal))
                link(dve.tensor_tensor(at_block[:], at_block[:], tokens(tok1), ALU.mult))
                for c in range(B // CH):
                    if c >= 2:
                        dve.wait_ge(S["chunk_ps"], c - 1)
                    dve.tensor_tensor(at_place[c % 2][:],
                                      dest[:, c * CH:(c + 1) * CH].unsqueeze(2).broadcast_to([N, CH, TW]),
                                      place[:].unsqueeze(1).broadcast_to([N, CH, TW]), ALU.is_equal)\
                       .then_inc(S["place"], 1)
                link(dve.tensor_scalar(cum[:], cum[:], 1.0 / TW, None, ALU.mult))
                link(dve.tensor_tensor(bj[:], bj[:], cum[0:1, :].unsqueeze(1).broadcast_to([1, BLOCKS, E]), ALU.is_ge))
                link(dve.tensor_reduce(bje[:], bj[:], AX.X, ALU.add))
                link(dve.tensor_scalar(bje[:], bje[:], float(E - 1), None, ALU.min))
                link(dve.tensor_copy(G.expert[0:1, :], bje[:]))
                dve.wait_ge(S["chunk_ps"], B // CH)
                link(dve.tensor_copy(table[:], G.ps[3][:, 0:BLOCKS]))
                link(dve.tensor_scalar(G.kept[:], table[:], 0.0, None, ALU.is_ge))
                link(dve.scalar_tensor_tensor(found[:], table[:], -1.0, table[:], ALU.mult, ALU.max))
                link(dve.tensor_scalar(none[:], found[:], 0.5, past[:], ALU.is_lt, ALU.mult))
                link(dve.tensor_scalar(found[:], found[:], -1.0, None, ALU.add))
                link(dve.tensor_tensor(none[:], none[:], found[:], ALU.add))
                link(dve.tensor_copy(G.result_row[:], none[:]))
                link(dve.tensor_scalar(found[:], found[:], 0.0, None, ALU.max))
                link(dve.tensor_copy(G.fetch_row[:], found[:]))

            @block.sync
            def _(sp):
                sp.wait_ge(rows_out, 16)
        clear(nc, list(S.values()) + [rows_out])


def experts(nc, G, rows, dst, weights, layer):
    PER = 27
    n_it = BLOCKS // PER
    assert BLOCKS % PER == 0
    with ExitStack() as ctx:
        sb, sem = allocator(nc, ctx)
        names = ("ones_set", "xn", "xT_ps", "xT", "h_ps", "gelu", "hT_ps", "hT", "y_ps", "out", "var", "rstd",
                 "tables", "dve_chain")
        S = {n: sem(f"f{layer}_" + n) for n in names}
        AHEAD = 4
        FETCH = len(G.rows_got[layer])
        assert PER % FETCH == 0 and FETCH > AHEAD
        w1a, w1b, w2, b2 = weights.w1a, weights.w1b, weights.w2, weights.b2
        x = [sb(f"f{layer}_x{i}", [TW, HC]) for i in range(PER)]
        part = [sb(f"f{layer}_part{i}", [TW, D]) for i in range(2)]
        fetch, result = sb(f"f{layer}_fetch", [TW, PER], I32), sb(f"f{layer}_result", [TW, PER], I32)
        kept = sb(f"f{layer}_kept", [TW, PER])
        RING = 8
        xn = [sb(f"f{layer}_xn{i}", [TW, D]) for i in range(RING)]
        st = [sb(f"f{layer}_st{i}", [TW, 6]) for i in range(PER)]
        mv = [sb(f"f{layer}_mv{i}", [TW, 3]) for i in range(PER)]
        xT0 = [sb(f"f{layer}_xT0{i}", [D0, TW]) for i in range(2)]
        xT1 = [sb(f"f{layer}_xT1{i}", [D1 + 1, TW]) for i in range(2)]
        hs = [sb(f"f{layer}_hs{i}", [TW, F]) for i in range(2)]
        hT = [sb(f"f{layer}_hT{i}", [128, FT, TW]) for i in range(2)]
        with nc.Block() as block:
            @block.sync
            def _(sp):
                sp.wait_ge(weights.weights_in, weights.all_in)

            @block.vector
            def _(dve):
                for i in range(2):
                    dve.memset(xT1[i][D1:D1 + 1, :], 1.0).then_inc(S["ones_set"], 1)
                dve.wait_ge(S["ones_set"], 2)
        clear(nc, list(S.values()) + [weights.weights_in])
        with nc.Fori(0, n_it) as it:
            with nc.Block() as block:
                @block.vector
                def _(dve):
                    link = Chain(dve, S["dve_chain"])

                    def stats(i):
                        dve.wait_ge(G.rows_got[layer][i % FETCH], (it * (PER // FETCH) + (i // FETCH + 1)) * 16)
                        norm_stats(dve, link, x[i][:, 0:D], st[i], mv[i], TW, S["var"])

                    def norm(i):
                        dve.wait_ge(S["rstd"], i + 1)
                        norm_apply(dve, x[i][:, 0:D], xn[i % RING][:], mv[i], TW).then_inc(S["xn"], 1)

                    def h_turned(i):
                        u = i % 2
                        dve.wait_ge(S["hT_ps"], i + 1)
                        dve.tensor_copy(hT[u][:, 0:4, :].rearrange("p c t -> p (c t)"), G.ps[6][:, :])
                        dve.tensor_copy(hT[u][:, 4:6, :].rearrange("p c t -> p (c t)"),
                                        G.ps[7][:, 0:2 * TW]).then_inc(S["hT"], 1)

                    def finish(i):
                        dve.wait_ge(S["y_ps"], i + 1)
                        y, u = G.ps[1][:, 0:D], part[i % 2]
                        if layer:
                            dve.tensor_tensor(x[i][:, 0:D], y, x[i][:, 0:D], ALU.add).then_inc(S["out"], 1)
                        else:
                            link(dve.tensor_tensor(u[:], y, xn[i % RING][:], ALU.subtract))
                            link(dve.scalar_tensor_tensor(u[:], u[:], kept[:, i:i + 1], xn[i % RING][:],
                                                          ALU.mult, ALU.add))
                            dve.scalar_tensor_tensor(x[i][:, 0:D], u[:], x[i][:, GATE:GATE + 1], x[i][:, 0:D],
                                                     ALU.mult, ALU.add).then_inc(S["out"], 1)

                    now = bass.ds(it * PER, PER)
                    dve.tensor_copy(fetch[:], G.fetch_row[:, now])
                    dve.tensor_copy(result[:], G.result_row[:, now])
                    link(dve.tensor_copy(kept[:], G.kept[:, now]))
                    dve.nop().then_inc(S["tables"], 1)
                    for i in range(AHEAD):
                        stats(i)
                        if i >= 2:
                            norm(i - 2)
                    norm(AHEAD - 2)
                    for i in range(PER):
                        if i + AHEAD - 1 < PER:
                            norm(i + AHEAD - 1)
                        h_turned(i)
                        if i:
                            finish(i - 1)
                        if i + AHEAD < PER:
                            stats(i + AHEAD)
                    finish(PER - 1)

                @block.scalar
                def _(act):
                    def x_turned(i):
                        u = i % 2
                        act.wait_ge(S["xT_ps"], i + 1)
                        if i >= 2:
                            act.wait_ge(S["h_ps"], 2 * (i - 1))
                        act.copy(xT0[u][:], G.ps[0][:, 0:TW])
                        act.copy(xT1[u][0:D1, :], G.ps[0][0:D1, TW:2 * TW]).then_inc(S["xT"], 1)

                    x_turned(0)
                    x_turned(1)
                    for i in range(PER):
                        u = i % 2
                        if i >= 2:
                            act.wait_ge(S["hT_ps"], i - 1)
                        for c in range(2):
                            act.wait_ge(S["h_ps"], 2 * i + c + 1)
                            act.activation(hs[u][:, c * FH:(c + 1) * FH], G.ps[2 + 2 * u + c][:, 0:FH],
                                           ACT.Gelu).then_inc(S["gelu"], 1)
                        if 1 <= i < PER - 1:
                            x_turned(i + 1)

                @block.tensor
                def _(pe):
                    ex = [None] * PER

                    def turn(i):
                        ex[i] = pe.value_load(G.expert[0:1, bass.ds(it * PER + i, 1)], min_val=0, max_val=E - 1)
                        pe.wait_ge(S["xn"], i + 1)
                        if i:
                            pe.wait_ge(S["xT"], i)
                        pe.transpose(G.ps[0][:, 0:TW], xn[i % RING][:, 0:D0], G.ident[:, :])
                        pe.transpose(G.ps[0][0:D1, TW:2 * TW], xn[i % RING][:, D0:D], G.ident[:, :]).then_inc(S["xT_ps"], 1)

                    def first(i):
                        u = i % 2
                        pe.wait_ge(S["xT"], i + 1)
                        if i >= 2:
                            pe.wait_ge(S["gelu"], 2 * (i - 1))
                        for c in range(2):
                            at = bass.ds(ex[i] * F + c * FH, FH)
                            pe.matmul(G.ps[2 + 2 * u + c][:, 0:FH], xT0[u][:], w1a[:, at], start=True, stop=False)
                            pe.matmul(G.ps[2 + 2 * u + c][:, 0:FH], xT1[u][:], w1b[:, at], start=False,
                                      stop=True).then_inc(S["h_ps"], 1)

                    def turn_h(i):
                        u = i % 2
                        pe.wait_ge(S["gelu"], 2 * (i + 1))
                        if i:
                            pe.wait_ge(S["hT"], i)
                        if i >= 2:
                            pe.wait_ge(S["y_ps"], i - 1)
                        for c in range(FT):
                            mm = pe.transpose(G.ps[6 + c // 4][:, (c % 4) * TW:(c % 4 + 1) * TW],
                                              hs[u][:, c * 128:(c + 1) * 128], G.ident[:, :])
                        mm.then_inc(S["hT_ps"], 1)

                    def second(i):
                        u = i % 2
                        if i:
                            pe.wait_ge(S["out"], i)
                        pe.wait_ge(S["hT"], i + 1)
                        for c in range(FT):
                            pe.matmul(G.ps[1][:, 0:D], hT[u][:, c, :], w2[:, bass.ds(ex[i] * (FT * D) + c * D, D)],
                                      start=(c == 0), stop=False)
                        pe.matmul(G.ps[1][:, 0:D], G.ones[0:1, 0:TW], b2[:, bass.ds(ex[i] * D, D)], start=False,
                                  stop=True).then_inc(S["y_ps"], 1)

                    turn(0)
                    turn(1)
                    first(0)
                    for i in range(PER):
                        if i + 1 < PER:
                            first(i + 1)
                        if i + 2 < PER:
                            turn(i + 2)
                        if i:
                            second(i - 1)
                        turn_h(i)
                    second(PER - 1)

                @block.gpsimd
                def _(pool):
                    def scale(i):
                        pool.wait_ge(S["var"], i + 1)
                        norm_rstd(pool, G, mv[i], TW, S["rstd"])

                    def fetched(i):
                        pool.indirect_dma_start(x[i][:], None, rows,
                                                bass.IndirectOffsetOnAxis(fetch[:, i:i + 1].bitcast(U32), 0))\
                            .then_inc(G.rows_got[layer][i % FETCH], 16)

                    pool.wait_ge(S["tables"], 1)
                    for i in range(FETCH):
                        fetched(i)
                    for i in range(AHEAD):
                        scale(i)
                    for i in range(PER):
                        if i + FETCH < PER:
                            fetched(i + FETCH)
                        if i + AHEAD < PER:
                            scale(i + AHEAD)
                        pool.wait_ge(S["out"], i + 1)
                        pool.indirect_dma_start(dst, bass.IndirectOffsetOnAxis(result[:, i:i + 1].bitcast(U32), 0), x[i][:, 0:D],
                                                None, bounds_check=NT - 1, oob_is_err=False).then_inc(G.rows_out[layer], 16)
                    pool.wait_ge(G.rows_out[layer], (it + 1) * (16 * PER))
            clear(nc, list(S.values()))


def landmark_attention(nc, G, A, xd, token_rows):
    PAIRS = H // 2
    SPAN = LM + LR
    STEPS = 6
    SC = 3.75
    ROOT = float(ZL) ** 0.5
    WV = PAIRS * LM
    with ExitStack() as ctx:
        sb, sem = allocator(nc, ctx)
        names = ("var", "rstd", "xn", "xT_ps", "xT", "xl", "qk_ps", "kl", "v_ps", "s2_ps", "nm", "exp", "x", "col_ps",
                 "x_out", "dve_chain", "act_chain", "pool_chain", "setup", "weights_in", "rows_in", "qk", "lm", "mq",
                 "v", "mk", "s1_ps", "s3_ps", "s1_shift", "s1_exp", "s3_nm", "s3_exp", "p1", "p1T_ps", "p3T_ps",
                 "p1T", "p3T", "rT_ps", "rT", "r_ps", "xr", "w0_ps", "wv", "a_ps", "a", "g", "c0", "c", "n_ps",
                 "zr", "o_ps", "o", "oT_ps", "oT", "y_ps", "yn", "yT_ps", "yT", "lg_ps", "red")
        S = {n: sem("l1_" + n) for n in names}
        x_in = [sem(f"l1_x_in{s}") for s in range(SL)]
        sems = list(S.values()) + x_in
        wqkv0, wqkv1 = sb("l1_wqkv0", [D0, 3 * D]), sb("l1_wqkv1", [D1, 3 * D])
        wo0, wo1 = sb("l1_wo0", [D0, D]), sb("l1_wo1", [D1 + 1, D])
        sw0, sw1 = sb("l1_sw0", [D0, E]), sb("l1_sw1", [D1 + 1, E])
        head, rootw, colw = sb("l1_head_s", [128, 8]), sb("l1_rootw_s", [128, 1]), sb("l1_colw_s", [128, 2])
        rowmax, colmax = sb("l1_rowmax", [128, PAIRS]), sb("l1_colmax", [LM, PAIRS, 2])
        most, cinv = sb("l1_most", [128, 4]), sb("l1_cinv", [128, 1])
        xT0, xT1 = sb("l1_xT0", [D0, SL, N]), sb("l1_xT1", [D1, SL, N])
        qk0, qk1 = sb("l1_qk0", [D0, 2, SL, N]), sb("l1_qk1", [D1, 2, SL, N])
        xl0, xl1 = sb("l1_xl0", [D0, SL, LR]), sb("l1_xl1", [D1, SL, LR])
        lm0, lm1 = sb("l1_lm0", [D0, 2, SL, LR]), sb("l1_lm1", [D1, 2, SL, LR])
        T = []
        for s in range(SL):
            t = {}
            for n, shape in (("st", [N, 6]), ("mv", [N, 3]), ("xn", [N, D]), ("mq0", [128, 8, LM]), ("mq1", [64, 4, LM]),
                             ("nm", [128, PAIRS]), ("rs", [128, PAIRS]),
                             ("rt", [128, PAIRS]), 
                             ("v", [N, D]), ("mk0", [128, 8, LR]), ("mk1", [64, 4, LR]), ("p1", [N, H, LM]),
                             ("nm1", [N, H]), ("rz1", [N, H]), ("p3", [128, PAIRS, N]), ("nm3", [128, PAIRS]),
                             ("rs3", [128, PAIRS]), ("e3", [128, PAIRS]), ("p1T", [128, PAIRS, N]),
                             ("p3T", [N, PAIRS, 128]), ("rT", [128, 2, 128]), ("xr", [128, PAIRS, LM]), ("wv", [128, PAIRS, LM]),
                             ("a", [128, PAIRS, LM]), ("g", [128, PAIRS, LM]), ("c", [128, PAIRS, LM]),
                             ("zr", [128, PAIRS, 2 * HD]), ("oT0", [D0, N]), ("oT1", [D1 + 1, N])):
                t[n] = sb(f"l1_{n}_{s}", shape)
            t["xT0"], t["xT1"], t["qk0"], t["qk1"] = xT0[:, s, :], xT1[:, s, :], qk0[:, :, s, :], qk1[:, :, s, :]
            t["xl0"], t["xl1"], t["lm0"], t["lm1"] = xl0[:, s, :], xl1[:, s, :], lm0[:, :, s, :], lm1[:, :, s, :]
            T.append(t)
        b0, b1 = [G.ps[2 * s] for s in range(SL)], [G.ps[2 * s + 1] for s in range(SL)]
        with nc.Block() as block:
            @block.sync
            def _(sp):
                lots = ((wqkv0[:], A["wqkv"][0:D0]), (wqkv1[:], A["wqkv"][D0:D]), (wo0[:], A["wo"][0:D0]),
                        (wo1[:], A["wo"][D0:D + 1]), (sw0[:], A["sw"][0:D0]), (sw1[:], A["sw"][D0:D + 1]),
                        (head[:], A["head"]), (rootw[:], A["rootw"]), (colw[:], A["colw"]))
                for dst, src in lots:
                    sp.dma_start(dst, src).then_inc(S["weights_in"], 16)
                for dst, src in token_rows:
                    sp.dma_start(dst, src).then_inc(S["rows_in"], 16)
                sp.wait_ge(S["rows_in"], 16 * len(token_rows))

            @block.vector
            def _(dve):
                for s in range(SL):
                    t = T[s]
                    for n in ("mq0", "mq1", "p1", "xr", "zr"):
                        dve.memset(t[n][:], 0.0)
                    dve.memset(t["oT1"][D1:D1 + 1, :], 1.0)
                for bank in G.ps:
                    dve.memset(bank[:], 0.0)
                for x in (xl0, xl1, lm0, lm1):
                    dve.memset(x[:], 0.0)
                dve.memset(rowmax[:], 0.0)
                dve.memset(colmax[:], 0.0)
                dve.memset(most[:], 0.0)
                dve.wait_ge(S["weights_in"], 16 * 9)
                dve.tensor_scalar(wqkv0[:, 0:D], wqkv0[:, 0:D], SCALE, None, ALU.mult)
                dve.tensor_scalar(wqkv1[:, 0:D], wqkv1[:, 0:D], SCALE, None, ALU.mult)
                dve.tensor_scalar(head[:], head[:], 0.5, None, ALU.mult).then_inc(S["setup"], 1)
                dve.wait_ge(S["setup"], 1)
        clear(nc, sems)

        def stats(dve, link, it, s, ahead):
            norm_stats(dve, link, padded_row(G, it, s, ahead), T[s]["st"], T[s]["mv"], N, S["var"])

        def apply(dve, it, s, ahead, n, done):
            dve.wait_ge(S["rstd"], n + s + 1)
            norm_apply(dve, padded_row(G, it, s, ahead), T[s]["xn"][:], T[s]["mv"], N).then_inc(S[done], 1)

        def norm_scales(pool, n):
            for s in range(SL):
                pool.wait_ge(S["var"], n + s + 1)
                norm_rstd(pool, G, T[s]["mv"], N, S["rstd"])

        def first_group(bank, at, left):
            with nc.Block() as block:
                @block.vector
                def _(dve):
                    link = Chain(dve, S["dve_chain"])
                    for s in range(SL):
                        stats(dve, link, 0, s, 0)
                    for s in range(SL):
                        apply(dve, 0, s, 0, 0, "xn")
                    for s in range(SL):
                        left(dve, s)

                @block.gpsimd
                def _(pool):
                    norm_scales(pool, 0)

                @block.tensor
                def _(pe):
                    for s in range(SL):
                        pe.wait_ge(S["xn"], s + 1)
                        turn(pe, G, T[s]["xn"], bank[s], at[s]).then_inc(S["xT_ps"], 1)
            clear(nc, sems)

        def tiles(bk, n, width):
            return bk[:, 0:n * width].rearrange("p (a j) -> p a j", j=width)

        def masked(eng, src, out, rows, heads):
            return eng.tensor_tensor(out[:, :, 0:LR], src.unsqueeze(1).broadcast_to([rows, heads, LR]),
                                     head[0:rows, 0:heads].unsqueeze(2).broadcast_to([rows, heads, LR]), ALU.mult)

        def pair_query(t, p):
            m = t["mq0"][:, 2 * p:2 * p + 2, :] if p < 4 else t["mq1"][:, 2 * p - 8:2 * p - 6, :]
            return m.rearrange("p a j -> p (a j)")

        first_bank, second_bank, x_bank, x_at = b1[0], b1[1], (b1[2], b1[2], b1[3], b1[3]), (0, 2 * N, 0, 2 * N)

        def token_sums(dve, s):
            dve.wait_ge(S["xT_ps"], 2 * (s // 2) + 2)
            a = x_at[s]
            for x, o in ((x_bank[s][:, a:a + N], xl0[:, s, :]), (x_bank[s][0:D1, a + N:a + 2 * N], xl1[:, s, :])):
                dve.tensor_copy(o[:, 0:1], x[:, 0:1])
                dve.tensor_reduce(o[:, 1:LR - 1], x[:, 1:N].rearrange("p (j i) -> p j i", i=2), AX.X, ALU.add)

        first_group(x_bank, x_at, token_sums)
        with nc.Fori(0, B // SL) as it:
            with nc.Block() as block:
                @block.sync
                def _(sp):
                    for s in range(SL):
                        sp.wait_ge(S["x"], s + 1)
                        sp.dma_start(xd[bass.ds(it * SL + s, 1), :, :].rearrange("a p q -> p (a q)"),
                                     T[s]["xr"][:].rearrange("p a j -> p (a j)")).then_inc(S["x_out"], 16)
                    sp.wait_ge(S["x_out"], 16 * SL)

                @block.gpsimd
                def _(pool):
                    norm_scales(pool, 0)

                @block.vector
                def _(dve):
                    link = Chain(dve, S["dve_chain"])
                    for s in range(SL):
                        stats(dve, link, it, s, 1)
                    dve.wait_ge(S["qk_ps"], 2)
                    for s in range(SL):
                        q, k = s * LR, (SL + s) * LR
                        masked(dve, first_bank[:, k:k + LR], T[s]["mk0"], 128, 8)
                        dve.tensor_scalar(T[s]["lm0"][:, 0, :], first_bank[:, q:q + LR], 0.5, None, ALU.mult)

                    def negmax(s):
                        dve.wait_ge(S["s2_ps"], s + 1)
                        dve.tensor_reduce(T[s]["nm"][:], tiles(b0[s], PAIRS, LR), AX.X, ALU.max,
                                          negate=True).then_inc(S["nm"], 1)

                    dve.wait_ge(S["qk_ps"], 4)
                    for s in range(SL):
                        q, k = s * LR, (SL + s) * LR
                        masked(dve, second_bank[0:64, k:k + LR], T[s]["mk1"], 64, 4)
                        dve.tensor_scalar(T[s]["lm1"][:, 0, :], second_bank[0:64, q:q + LR], 0.5, None, ALU.mult)\
                           .then_inc(S["mq"], 1)
                        if s >= 2:
                            negmax(s - 2)
                    negmax(SL - 2)
                    negmax(SL - 1)
                    for s in range(SL):
                        apply(dve, it, s, 1, 0, "xn")
                    for s in range(SL):
                        t = T[s]
                        xe = t["xr"]
                        dve.wait_ge(S["exp"], s + 1)
                        link(dve.scalar_tensor_tensor(t["rs"][:], xe[:, :, LR - 1], float(ZL - 1), t["rs"][:],
                                                      ALU.mult, ALU.add))
                        dve.tensor_scalar(xe[:, :, LR - 1], xe[:, :, LR - 1], ROOT, None, ALU.mult)
                        link(dve.reciprocal(t["rt"][:], t["rs"][:]))
                        link(dve.tensor_tensor(t["rs"][:], t["rs"][:], t["rt"][:], ALU.mult))
                        dve.tensor_scalar(t["rt"][:], t["rt"][:], rootw[:], None, ALU.mult)
                        link(dve.tensor_tensor(rowmax[:], rowmax[:], t["rs"][:], ALU.max))
                        dve.tensor_tensor(xe[:, :, 0:LR], xe[:, :, 0:LR],
                                          t["rt"][:].unsqueeze(2).broadcast_to([128, PAIRS, LR]),
                                          ALU.mult).then_inc(S["x"], 1)
                    for s in range(SL):
                        token_sums(dve, s)
                    for s in range(SL):
                        dve.wait_ge(S["col_ps"], s + 1)
                        link(dve.tensor_tensor(colmax[:], colmax[:], tiles(b0[s], PAIRS, 2)[0:LM], ALU.max))

                @block.scalar
                def _(act):
                    for s in range(SL):
                        t = T[s]
                        act.wait_ge(S["nm"], s + 1)
                        for p in range(PAIRS):
                            last = act.activation(t["xr"][:, p, 0:LR], b0[s][:, p * LR:(p + 1) * LR], ACT.Exp,
                                                  bias=t["nm"][:, p:p + 1], accum_out=t["rs"][:, p:p + 1])
                        last.then_inc(S["exp"], 1)

                @block.tensor
                def _(pe):
                    for m, (a, n, bank) in enumerate(((0, D0, first_bank), (D0, D1, second_bank))):
                        for part in range(2):
                            o = bank[0:n, part * SL * LR:(part + 1) * SL * LR]
                            w = slice(part * D + a, part * D + a + n)
                            pe.matmul(o, wqkv0[:, w], xl0[:].rearrange("p s j -> p (s j)"), start=True, stop=False)
                            pe.matmul(o, wqkv1[:, w], xl1[:].rearrange("p s j -> p (s j)"), start=False,
                                      stop=True).then_inc(S["qk_ps"], 1)
                    for s in range(SL):
                        t = T[s]
                        pe.wait_ge(S["mq"], s + 1)
                        for i in range(2):
                            for q, k, a in ((t["lm0"], t["mk0"], 0), (t["lm1"], t["mk1"], 4)):
                                h = k[:].rearrange("p (a i) j -> p i a j", i=2)[:, i, :, :]
                                o = b0[s][LM * i:LM * i + LR, a * LR:(a + h.shape[1]) * LR]
                                mm = pe.matmul(o.rearrange("p (a j) -> p a j", j=LR), q[:, 0, :], h, start=True,
                                               stop=True)
                        mm.then_inc(S["s2_ps"], 1)
                    for s in range(SL):
                        pe.wait_ge(S["xn"], s + 1)
                        turn(pe, G, T[s]["xn"], x_bank[s], x_at[s]).then_inc(S["xT_ps"], 1)
                    for s in range(SL):
                        pe.wait_ge(S["x"], s + 1)
                        for p in range(PAIRS):
                            mm = pe.matmul(b0[s][0:LM, 2 * p:2 * p + 2], T[s]["xr"][:, p, :], colw[:], start=True,
                                           stop=True)
                        mm.then_inc(S["col_ps"], 1)
            clear(nc, sems)
        with nc.Block() as block:
            @block.vector
            def _(dve):
                link = Chain(dve, S["dve_chain"])
                link(dve.tensor_reduce(most[0:LM, 1:2], colmax[:].rearrange("p a j -> p (a j)"), AX.X, ALU.max))
                link(dve.reciprocal(cinv[0:LM, :], rootw[0:LM, :]))
                link(dve.tensor_tensor(most[0:LM, 1:2], most[0:LM, 1:2], cinv[0:LM, :], ALU.mult))
                link(dve.tensor_reduce(most[:, 0:1], rowmax[:], AX.X, ALU.max))
                link(dve.tensor_reduce(cinv[:], colw[:], AX.X, ALU.add))
                link(dve.tensor_scalar(cinv[:], cinv[:], 0.0, None, ALU.is_gt))
                dve.tensor_tensor(most[:, 0:1], most[:, 0:1], cinv[:], ALU.mult).then_inc(S["setup"], 1)
                dve.wait_ge(S["red"], 1)
                link(dve.tensor_tensor(cinv[:], most[:, 2:3], most[:, 3:4], ALU.mult))
                link(dve.reciprocal(cinv[:], cinv[:]))

            @block.gpsimd
            def _(pool):
                pool.wait_ge(S["setup"], 1)
                pool.partition_all_reduce(most[:, 2:4], most[:, 0:2], 128, bass.bass_isa.ReduceOp.max)\
                    .then_inc(S["red"], 1)
        clear(nc, sems)

        halves = [(0, slice(0, LR), slice(0, LR)), (1, slice(LM, SPAN), slice(LM, SPAN))]

        def each_head(pe, lhs, rhs, out, a, b):
            for p in range(PAIRS):
                for _, k, m in halves:
                    last = pe.matmul(out[m, p * (b - a):(p + 1) * (b - a)], lhs[k, p, 0:LR], rhs[k, p, a:b], start=True,
                                     stop=True)
            return last

        AHEAD = 2 * N
        BEHIND, LOGITS = D, 8 * LR
        turned_first = lambda dve, s: (dve.wait_ge(S["xT_ps"], s + 1),
                                       dve.tensor_copy(xT0[:, s, :], b0[s][:, AHEAD:AHEAD + N]),
                                       dve.tensor_copy(xT1[:, s, :], b0[s][0:D1, AHEAD + N:AHEAD + 2 * N]))
        first_group(b0, (AHEAD,) * SL, turned_first)
        with nc.Fori(0, B // SL) as it:
            with nc.Block() as block:
                @block.sync
                def _(sp):
                    for s in range(SL):
                        sp.dma_start(T[s]["xr"][:].rearrange("p a j -> p (a j)"),
                                     xd[bass.ds(it * SL + s, 1), :, :].rearrange("a p q -> p (a q)"))\
                          .then_inc(x_in[s], 16)

                @block.gpsimd
                def _(pool):
                    norm_scales(pool, 0)
                    pool.wait_ge(S["lm"], 1)
                    for s in range(SL):
                        t = T[s]
                        masked(pool, t["lm0"][:, 0, :], t["mq0"], 128, 8)
                        masked(pool, t["lm1"][:, 0, :], t["mq1"], 64, 4).then_inc(S["mq"], 1)
                    for k in range(STEPS - 1):
                        for s in range(SL):
                            t = T[s]
                            pool.wait_ge(S["a"], SL * k + s + 1)
                            pool.wait_ge(S["c0"], SL * k + s + 1)
                            pool.tensor_tensor(t["c"][:], t["c"][:], t["a"][:], ALU.subtract).then_inc(S["c"], 1)
                        if k == 0:
                            norm_scales(pool, SL)

                @block.vector
                def _(dve):
                    link = Chain(dve, S["dve_chain"])
                    for s in range(SL):
                        stats(dve, link, it, s, -1)
                    for s in range(SL):
                        apply(dve, it, s, -1, 0, "yn")
                    for i, (x, o) in enumerate(((qk0, lm0), (qk1, lm1))):
                        dve.wait_ge(S["qk"], 2 * i + 2)
                        x, o = x[:].rearrange("p a s n -> p (a s) n"), o[:].rearrange("p a s n -> p (a s) n")
                        dve.tensor_copy(o[:, :, 0:1], x[:, :, 0:1])
                        two = x[:, :, 1:N].rearrange("p a (j i) -> p a i j", i=2)
                        last = dve.tensor_tensor(o[:, :, 1:LR - 1], two[:, :, 0, :], two[:, :, 1, :], ALU.add)
                    last.then_inc(S["lm"], 1)
                    dve.wait_ge(S["lm"], 1)
                    for s in range(SL):
                        t = T[s]
                        masked(dve, t["lm0"][:, 1, :], t["mk0"], 128, 8)
                        masked(dve, t["lm1"][:, 1, :], t["mk1"], 64, 4).then_inc(S["mk"], 1)
                    def shifted(s):
                        t = T[s]
                        dve.wait_ge(S["s1_ps"], s + 1)
                        dve.tensor_copy(G.lg_all[:, :, bass.ds(it * SL + s, 1)],
                                        b0[s][0:N, LOGITS:LOGITS + E].unsqueeze(2))
                        h0, h1 = tiles(b0[s], 8, LR)[0:N], tiles(b1[s], 4, LR)[0:N]
                        dve.tensor_reduce(t["nm1"][:, 0:8], h0, AX.X, ALU.max, negate=True)
                        link(dve.tensor_reduce(t["nm1"][:, 8:H], h1, AX.X, ALU.max, negate=True))
                        over = lambda a, b: t["nm1"][:, a:b].unsqueeze(2).broadcast_to([N, b - a, LR])
                        dve.tensor_tensor(t["p1"][:, 0:8, 0:LR], h0, over(0, 8), ALU.add)
                        dve.tensor_tensor(t["p1"][:, 8:H, 0:LR], h1, over(8, H), ALU.add).then_inc(S["s1_shift"], 1)

                    def largest(s):
                        t = T[s]
                        dve.wait_ge(S["s3_ps"], s + 1)
                        for j, bk in enumerate((b0[s], b1[s])):
                            link(dve.tensor_reduce(t["nm3"][:, 3 * j:3 * j + 3], tiles(bk, 3, N), AX.X, ALU.max,
                                                   negate=True))
                        dve.tensor_scalar(t["nm3"][:], t["nm3"][:], 0.0, None, ALU.min).then_inc(S["s3_nm"], 1)

                    shifted(0)
                    for s in range(1, SL):
                        shifted(s)
                        largest(s - 1)
                    largest(SL - 1)
                    for s in range(SL):
                        t = T[s]
                        dve.wait_ge(S["s3_exp"], s + 1)
                        link(dve.scalar_tensor_tensor(t["rs3"][:], t["e3"][:], float(PADS), t["rs3"][:], ALU.mult,
                                                      ALU.add))
                        link(dve.reciprocal(t["rs3"][:], t["rs3"][:]))
                        link(dve.tensor_scalar(t["rs3"][:], t["rs3"][:], rootw[:], None, ALU.mult))
                        dve.wait_ge(S["p3T_ps"], s + 1)
                        dve.tensor_copy(t["p3T"][:, 0:4, :], tiles(b0[s], 4, 128)[0:N])
                        dve.tensor_copy(t["p3T"][:, 4:6, :], tiles(b1[s], 2, 128)[0:N]).then_inc(S["p3T"], 1)
                    for s in range(SL):
                        t = T[s]
                        dve.wait_ge(x_in[s], 16)
                        dve.wait_ge(S["r_ps"], s + 1)
                        r = tiles(b0[s], PAIRS, 2 * HD)
                        for i in range(2):
                            h = slice(LM * i, LM * i + LM)
                            last = dve.tensor_tensor(t["xr"][h, :, LR:LM], r[h, :, HD * i:HD * i + HD],
                                                     t["rs3"][h, :].unsqueeze(2).broadcast_to([LM, PAIRS, HD]), ALU.mult)
                        last.then_inc(S["xr"], 1)
                    for s in range(SL):
                        dve.wait_ge(S["w0_ps"], s + 1)
                        dve.tensor_scalar(T[s]["wv"][:], tiles(b1[s], PAIRS, LM), cinv[:], SC,
                                          ALU.mult, ALU.mult).then_inc(S["wv"], 1)
                    for s in range(SL):
                        t = T[s]
                        dve.wait_ge(S["s1_exp"], s + 1)
                        last = t["p1"][:, :, LR - 1]
                        link(dve.tensor_reduce(t["rz1"][:], t["p1"][:, :, 0:LR], AX.X, ALU.add))
                        link(dve.scalar_tensor_tensor(t["rz1"][:], last, float(ZL - 1), t["rz1"][:], ALU.mult, ALU.add))
                        dve.tensor_scalar(last, last, ROOT, None, ALU.mult)
                        link(dve.reciprocal(t["rz1"][:], t["rz1"][:]))
                        dve.tensor_tensor(t["p1"][:, :, 0:LR], t["p1"][:, :, 0:LR],
                                          t["rz1"][:].unsqueeze(2).broadcast_to([N, H, LR]), ALU.mult)\
                           .then_inc(S["p1"], 1)
                    for k in range(STEPS - 1):
                        for s in range(SL):
                            t = T[s]
                            dve.wait_ge(S["a"], SL * k + s + 1)
                            dve.wait_ge(S["wv"], SL * k + s + 1)
                            dve.scalar_tensor_tensor(t["g"][:], t["wv"][:], 7 * SC, t["a"][:], ALU.mult,
                                                     ALU.subtract).then_inc(S["g"], 1)
                        if k == 0:
                            for s in range(SL):
                                stats(dve, link, it, s, 1)
                        for s in range(SL):
                            t = T[s]
                            dve.wait_ge(S["n_ps"], SL * k + s + 1)
                            dve.wait_ge(S["c"], SL * k + s + 1)
                            dve.scalar_tensor_tensor(t["wv"][:], tiles(b1[s], PAIRS, LM), 0.25 / SC ** 3, t["c"][:], ALU.mult,
                                                     ALU.add).then_inc(S["wv"], 1)
                        if k == 0:
                            for s in range(SL):
                                apply(dve, it, s, 1, SL, "xn")
                    for s in range(SL):
                        t = T[s]
                        a, v, c, g = (t[n][:, :, cols] for n, cols in
                                      (("a", slice(LR, LM)), ("wv", slice(LR, LM)), ("c", slice(0, HD)),
                                       ("g", slice(0, HD))))
                        dve.wait_ge(S["a"], SL * (STEPS - 1) + s + 1)
                        dve.scalar_tensor_tensor(g, v, 7 * SC, a, ALU.mult, ALU.subtract).then_inc(S["g"], 1)
                        link(dve.scalar_tensor_tensor(c, a, -3.75 / SC ** 2, c, ALU.mult, ALU.add))
                    for s in range(SL):
                        t = T[s]
                        dve.wait_ge(S["n_ps"], SL * (STEPS - 1) + s + 1)
                        for i, rows, _ in halves:
                            last = dve.scalar_tensor_tensor(t["zr"][rows, :, HD * i:HD * i + HD],
                                                            tiles(b1[s], PAIRS, HD)[rows], 0.25 / SC ** 4,
                                                            t["c"][rows, :, 0:HD], ALU.mult, ALU.add)
                        last.then_inc(S["zr"], 1)
                    for s in range(SL):
                        t = T[s]
                        row = padded_row(G, it, s, 0)
                        dve.wait_ge(S["y_ps"], s + 1)
                        dve.tensor_tensor(row, row, b1[s][0:N, 0:D], ALU.add)

                @block.scalar
                def _(act):
                    queries_keys_out(act, qk0, qk1, b1, S["qk_ps"], S["qk"])
                    for s in range(SL):
                        act.wait_ge(S["v_ps"], s + 1)
                        act.copy(T[s]["v"][:], b0[s][0:N, 0:D]).then_inc(S["v"], 1)
                    for s in range(SL):
                        act.wait_ge(S["yT_ps"], s + 1)
                        turned(act, b0[s], T[s]["oT0"], T[s]["oT1"], BEHIND).then_inc(S["yT"], 1)
                    for s in range(SL):
                        t = T[s]
                        act.wait_ge(S["s3_nm"], s + 1)
                        for p in range(PAIRS):
                            bk = b0[s] if p < 3 else b1[s]
                            act.activation(t["p3"][:, p, :], bk[:, (p % 3) * N:(p % 3 + 1) * N],
                                           ACT.Exp, bias=t["nm3"][:, p:p + 1], accum_out=t["rs3"][:, p:p + 1])
                        act.activation(t["e3"][:], t["nm3"][:], ACT.Exp).then_inc(S["s3_exp"], 1)
                    for s in range(SL):
                        act.wait_ge(S["rT_ps"], s + 1)
                        act.copy(T[s]["rT"][:, 0, :], b0[s][:, 0:128])
                        act.copy(T[s]["rT"][0:D1, 1, :], b0[s][0:D1, 128:256]).then_inc(S["rT"], 1)
                    for s in range(SL):
                        t = T[s]
                        act.wait_ge(S["s1_shift"], s + 1)
                        act.activation(t["p1"][:, :, 0:LR], t["p1"][:, :, 0:LR], ACT.Exp).then_inc(S["s1_exp"], 1)
                    for k in range(STEPS):
                        for s in range(SL):
                            t = T[s]
                            act.wait_ge(S["wv"], SL * k + s + 1)
                            if k < STEPS - 1:
                                act.mul(t["c"][:], t["wv"][:], 3.25).then_inc(S["c0"], 1)
                            else:
                                act.mul(t["c"][:, :, 0:HD], t["wv"][:, :, LR:LM], 3.25 / SC).then_inc(S["c0"], 1)
                            act.wait_ge(S["a_ps"], SL * k + s + 1)
                            act.copy(t["a"][:], tiles(b0[s], PAIRS, LM)).then_inc(S["a"], 1)
                        if k < 2:
                            for s in range(SL):
                                act.wait_ge(S["p1T_ps"], SL * k + s + 1)
                                act.copy(T[s]["p1T"][:, 3 * k:3 * k + 3, :], tiles(b1[s], 3, N)).then_inc(S["p1T"], 1)
                    for s in range(SL):
                        act.wait_ge(S["o_ps"], s + 1)
                        turned(act, b1[s], T[s]["oT0"], T[s]["oT1"]).then_inc(S["oT"], 1)
                    for s in range(SL):
                        act.wait_ge(S["xT_ps"], s + 1)
                        turned(act, b0[s], T[s]["xT0"], T[s]["xT1"], AHEAD).then_inc(S["xT"], 1)

                @block.tensor
                def _(pe):
                    flat = lambda a: a[:].rearrange("p a j -> p (a j)")
                    queries_keys(pe, wqkv0, wqkv1, xT0, xT1, b1, S["qk_ps"])
                    for s in range(SL):
                        t = T[s]
                        pe.matmul(b0[s][0:N, 0:D], t["xT0"], wqkv0[:, 2 * D:3 * D], start=True, stop=False)
                        pe.matmul(b0[s][0:N, 0:D], t["xT1"], wqkv1[:, 2 * D:3 * D], start=False,
                                  stop=True).then_inc(S["v_ps"], 1)
                    for s in range(SL):
                        pe.wait_ge(S["yn"], s + 1)
                        pe.wait_ge(S["v"], s + 1)
                        turn(pe, G, T[s]["xn"], b0[s], BEHIND).then_inc(S["yT_ps"], 1)
                    def first_scores(s):
                        t = T[s]
                        pe.wait_ge(S["yT"], s + 1)
                        pe.matmul(b0[s][0:N, LOGITS:LOGITS + E], t["oT0"][:], sw0[:], start=True, stop=False)
                        pe.matmul(b0[s][0:N, LOGITS:LOGITS + E], t["oT1"][:], sw1[:], start=False, stop=True)
                        pe.wait_ge(S["mk"], s + 1)
                        pe.matmul(b0[s][0:N, 0:8 * LR], t["qk0"][:, 0, :], flat(t["mk0"]), start=True, stop=True)
                        pe.matmul(b1[s][0:N, 0:4 * LR], t["qk1"][:, 0, :], flat(t["mk1"]), start=True,
                                  stop=True).then_inc(S["s1_ps"], 1)

                    def third_scores(s):
                        t = T[s]
                        pe.wait_ge(S["mq"], s + 1)
                        pe.wait_ge(S["s1_shift"], s + 1)
                        for p in range(PAIRS):
                            bk = b0[s] if p < 3 else b1[s]
                            mm = pe.matmul(bk[:, (p % 3) * N:(p % 3 + 1) * N], pair_query(t, p),
                                           (t["qk0"] if p < 4 else t["qk1"])[:, 1, :], start=True, stop=True)
                        mm.then_inc(S["s3_ps"], 1)

                    def turned_probs(s):
                        t = T[s]
                        pe.wait_ge(S["s3_exp"], s + 1)
                        for p in range(PAIRS):
                            mm = pe.transpose((b0 if p < 4 else b1)[s][0:N, (p % 4) * 128:(p % 4 + 1) * 128],
                                              t["p3"][:, p, :], G.ident[:, :])
                        mm.then_inc(S["p3T_ps"], 1)

                    def landmark_values_T(s):
                        t = T[s]
                        pe.wait_ge(S["p3T"], s + 1)
                        for p in range(PAIRS):
                            j, c = 2 * HD * (p % 4), p // 4 * 128
                            mm = pe.matmul(b0[s][j:j + 2 * HD, c:c + 128], t["v"][:, p * 2 * HD:(p + 1) * 2 * HD],
                                           t["p3T"][:, p, :], start=True, stop=True)
                        mm.then_inc(S["rT_ps"], 1)

                    first_scores(0)
                    for s in range(1, SL):
                        first_scores(s)
                        third_scores(s - 1)
                    third_scores(SL - 1)
                    turned_probs(0)
                    for s in range(1, SL):
                        turned_probs(s)
                        landmark_values_T(s - 1)
                    landmark_values_T(SL - 1)
                    for s in range(SL):
                        t = T[s]
                        pe.wait_ge(S["rT"], s + 1)
                        pe.transpose(b0[s][:, 0:128], t["rT"][:, 0, :], G.ident[:, :])
                        pe.transpose(b0[s][:, 128:128 + D1], t["rT"][0:D1, 1, :], G.ident[0:D1, 0:D1])\
                          .then_inc(S["r_ps"], 1)
                    for s in range(SL):
                        pe.wait_ge(S["xr"], s + 1)
                        each_head(pe, T[s]["xr"], T[s]["xr"], b1[s], 0, LM).then_inc(S["w0_ps"], 1)
                    for k in range(STEPS):
                        for s in range(SL):
                            t = T[s]
                            pe.wait_ge(S["wv"], SL * k + s + 1)
                            each_head(pe, t["wv"], t["wv"], b0[s], 0, LM).then_inc(S["a_ps"], 1)
                        if k < 2:
                            for s in range(SL):
                                if k == 0:
                                    pe.wait_ge(S["p1"], s + 1)
                                for p in range(3 * k, 3 * k + 3):
                                    mm = pe.transpose(b1[s][:, (p % 3) * N:(p % 3 + 1) * N],
                                                      T[s]["p1"][:, 2 * p:2 * p + 2, :].rearrange("p a j -> p (a j)"),
                                                      G.ident[0:N, 0:N])
                                mm.then_inc(S["p1T_ps"], 1)
                        for s in range(SL):
                            t = T[s]
                            if k < 2:
                                pe.wait_ge(S["p1T"], SL * k + s + 1)
                            pe.wait_ge(S["g"], SL * k + s + 1)
                            each_head(pe, t["a"], t["g"], b1[s], 0, LM if k < STEPS - 1 else HD).then_inc(S["n_ps"], 1)
                    for s in range(SL):
                        t = T[s]
                        pe.wait_ge(S["zr"], s + 1)
                        for p in range(PAIRS):
                            j, c = 2 * HD * (p % 4), p // 4 * N
                            mm = pe.matmul(b1[s][j:j + 2 * HD, c:c + N], t["zr"][:, p, :], t["p1T"][:, p, :],
                                           start=True, stop=True)
                        mm.then_inc(S["o_ps"], 1)
                    for s in range(SL):
                        pe.wait_ge(S["xn"], s + 1)
                        turn(pe, G, T[s]["xn"], b0[s], AHEAD).then_inc(S["xT_ps"], 1)
                    for s in range(SL):
                        t = T[s]
                        pe.wait_ge(S["oT"], s + 1)
                        pe.matmul(b1[s][0:N, 0:D], t["oT0"][:], wo0[:], start=True, stop=False)
                        pe.matmul(b1[s][0:N, 0:D], t["oT1"][:], wo1[:], start=False, stop=True).then_inc(S["y_ps"], 1)
            clear(nc, sems)
        last_logits(nc, G, T, sw0, sw1, S)


class Shared:
    pass


def build(nc, img, pw, plg, plb, pb, txt, a0, f0, a1, f1, out):
    h0 = nc.dram_tensor("h0", [B * NP_TOK, D], F32).ap()
    rows = [nc.dram_tensor(f"rows{i}", [NT, HC], F32).ap() for i in range(2)]
    xd = nc.dram_tensor("landmark_x", [B, 128, (H // 2) * LM], F32).ap()
    h2 = nc.dram_tensor("h2", [NT, D], F32).ap()
    with ExitStack() as ctx:
        sb, sem = allocator(nc, ctx)
        G = Shared()
        G.ps = [ctx.enter_context(nc.psum_tensor(f"bank{i}", [128, 512], F32)) for i in range(8)]
        G.ident, G.ones, G.before = sb("ident", [128, 128]), sb("ones", [128, 128]), sb("before", [128, 128])
        G.half = sb("minus_half", [128, 1])
        G.rows_got = [[sem(f"rows_got{i}_{j}") for j in range(9)] for i in range(2)]
        G.rows_out = [sem(f"rows_out{i}") for i in range(2)]
        G.h_all = sb("h", [N, B + 2 * SL, HC])
        G.h = G.h_all[:, SL:SL + B, :]
        G.lg_all = sb("logits", [N, E, B + SL])
        G.lg = G.lg_all[:, :, SL:SL + B]
        G.expert = sb("expert", [1, BLOCKS], I32)
        G.fetch_row, G.result_row = sb("fetch_row", [TW, BLOCKS], I32), sb("result_row", [TW, BLOCKS], I32)
        G.kept = sb("kept", [TW, BLOCKS])
        set_a, set_b = sem("set_a"), sem("set_b")
        with nc.Block() as block:
            @block.vector
            def _(dve):
                dve.memset(G.ones[:], 1.0).then_inc(set_a, 1)
                dve.memset(G.half[:], -0.5)
                dve.memset(G.h[:, :, D:HC], 0.0)
                dve.memset(G.h_all[:, 0:SL, :], 0.0)
                dve.memset(G.h_all[:, SL + B:SL + B + SL, :], 0.0)

            @block.gpsimd
            def _(pool):
                pool.wait_ge(set_a, 1)
                pool.affine_select(out=G.ident[:], in_=G.ones[:], compare_op=ALU.is_equal, fill=0.0, base=0,
                                   pattern=[[-1, 128]], channel_multiplier=1).then_inc(set_b, 1)
                pool.affine_select(out=G.before[:], in_=G.ones[:], compare_op=ALU.is_gt, fill=0.0, base=0,
                                   pattern=[[1, 128]], channel_multiplier=-1).then_inc(set_b, 1)
        clear(nc, [set_a, set_b])
        patch_embedding(nc, G, img, pw, plg, plb, pb, txt, h0)
        talking_attention(nc, G, a0, [(G.h[0:NP_TOK, :, 0:D], h0.rearrange("(b n) d -> n b d", n=NP_TOK)),
                                      (G.h[NP_TOK:N, :, 0:D], txt.rearrange("b n d -> n b d"))])
        with ExitStack() as layer:
            weights = ExpertWeights(nc, layer, 0, f0)
            route(nc, G, rows[0], 0, weights)
            experts(nc, G, rows[0], h2, weights, 0)
        landmark_attention(nc, G, a1, xd, [(G.h[:, :, 0:D], h2.rearrange("(b n) d -> n b d", n=N))])
        with ExitStack() as layer:
            weights = ExpertWeights(nc, layer, 1, f1)
            route(nc, G, rows[1], 1, weights)
            experts(nc, G, rows[1], out, weights, 1)


def kernel(**inputs):
    import numpy as np
    import concourse.bacc as _bacc
    from concourse.bass_utils import run_bass_kernel_spmd as _run

    I = {k: np.ascontiguousarray(v) for k, v in inputs.items()}
    xp = np.pad(I["x"], ((0, 0), (0, 0), (1, 1), (1, 1)))
    c = slice(1, -1)
    shifts = [xp[:, :, c, c], xp[:, :, c, :-2], xp[:, :, c, 2:], xp[:, :, :-2, c], xp[:, :, 2:, c]]
    xc = np.concatenate(shifts, axis=1).reshape(B, VAR_CH, GRID, PATCH, IMG)
    img = np.ascontiguousarray(xc.transpose(1, 3, 0, 2, 4)).reshape(VAR_CH * PATCH, B * GRID * IMG)
    feat = lambda a: np.ascontiguousarray(a.reshape(PATCH, PATCH, VAR_CH, -1).transpose(2, 0, 1, 3))
    rootw = np.tile(np.where(np.arange(LM) == LR - 1, ZL ** 0.5, 1.0), 2).astype(np.float32)
    real = np.tile(np.arange(LM) < LR, 2)
    def spread(rows):
        out = np.zeros((4, 2 * HD, H // 4, rows.shape[1]), np.float32)
        out[:, 0:HD] = rows.reshape(H // 4, 4, HD, -1).transpose(1, 2, 0, 3)
        return out.reshape(128, -1)

    mix = np.zeros((H * MC + 1, H, MC), np.float32)
    for m in range(MC):
        mix[m:H * MC:MC, :, m] = I["L0_attn_proj_w_w"].T
    mix[H * MC] = np.repeat(I["L0_attn_proj_w_b"], MC).reshape(H, MC)
    mix = mix.reshape(H * MC + 1, H * MC)
    a = {
        "img": img,
        "pw": feat(I["L0_tok_w"]).reshape(VAR_CH * PATCH, PATCH, D),
        "plg": feat(I["L0_tok_ln_gamma"]).reshape(VAR_CH * PATCH, PATCH),
        "plb": feat(I["L0_tok_ln_beta"]).reshape(VAR_CH * PATCH, PATCH),
        "pb": I["L0_tok_b"][None],
        "txt": I["txt"],
        "a0_wqkv": I["L0_attn_qkv_w"].T,
        "a0_wl": np.repeat(I["L0_attn_proj_l_w"].T, HD, axis=0),
        "a0_lb": I["L0_attn_proj_l_b"][None],
        "a0_mix": mix,
        "a0_lamb": spread(np.repeat(I["L0_attn_lamb"], HD)[:, None]),
        "a0_wo": spread(I["L0_attn_proj_out_w"].T),
        "a0_wob": I["L0_attn_proj_out_b"][None],
        "a0_sw": np.concatenate([I["L0_ffn_switch_w"], I["L0_ffn_switch_b"][None]]),
        "f0_w1": np.concatenate([I["L0_ffn_w1"], I["L0_ffn_b1"][:, None]], axis=1),
        "f0_w2": I["L0_ffn_w2"],
        "f0_b2": I["L0_ffn_b2"].reshape(1, -1),
        "a1_wqkv": I["L1_attn_w_qkv"].T,
        "a1_wo": np.concatenate([I["L1_attn_w_proj"].T, I["L1_attn_b_proj"][None]]),
        "a1_head": np.kron(np.eye(8), np.ones((HD, 1))).astype(np.float32),
        "a1_rootw": rootw.reshape(-1, 1),
        "a1_colw": (np.kron(np.eye(2), np.ones((LM, 1))) * (rootw * real).reshape(-1, 1)).astype(np.float32),
        "a1_sw": np.concatenate([I["L1_ffn_gate_w"], I["L1_ffn_gate_b"][None]]),
        "f1_w1": np.concatenate([I["L1_ffn_w1"], I["L1_ffn_b1"][:, None]], axis=1),
        "f1_w2": I["L1_ffn_w2"],
        "f1_b2": I["L1_ffn_b2"].reshape(1, -1),
    }
    nc = _bacc.Bacc("TRN2", target_bir_lowering=False, num_devices=1)
    arrays, t = {}, {}
    for k, v in a.items():
        v = np.ascontiguousarray(v)
        arrays[k] = v
        t[k] = nc.dram_tensor(k, v.shape, mybir.dt.from_np(v.dtype), kind="ExternalInput").ap()
    out = nc.dram_tensor("out", (NT, D), F32, kind="ExternalOutput").ap()
    sub = lambda p: {k[3:]: v for k, v in t.items() if k.startswith(p + "_")}
    build(nc, t["img"], t["pw"], t["plg"], t["plb"], t["pb"], t["txt"], sub("a0"), sub("f0"), sub("a1"), sub("f1"),
          out)
    r = _run(nc, [arrays], core_ids=[0])
    return r.results[0]["out"].reshape(B, N, D)
```
